# Optimizing a Trainium2 kernel written in Bass

```python
import numpy as np
import jax
import jax.numpy as jnp

def _softmax(x, axis=-1):
    return jax.nn.softmax(x, axis=axis)

def _gelu(x):
    return jax.nn.gelu(x, approximate=True)

def _silu(x):
    return jax.nn.silu(x)

def _sigmoid(x):
    return jax.nn.sigmoid(x)

def _layernorm(x, axis=-1, eps=1e-05):
    m = jnp.mean(x, axis=axis, keepdims=True)
    v = jnp.var(x, axis=axis, keepdims=True)
    return (x - m) / jnp.sqrt(v + eps)

def _scatter_add(tgt, idx, src, axis=0):
    return tgt.at[idx].add(src)

def _segment_sum(src, seg, n):
    return jax.ops.segment_sum(src, seg, n)
kernel_name = 'mk_gnn_ffn_d1_gnn_r8_6712c6'

def setup_inputs(seed: int=0):
    np.random.seed(seed)
    _w = jnp.asarray

    def _rec_inputs():
        import jax
        import jax.numpy as jnp
        _gk = jax.random.key(seed)
        x = -0.0002117 + 1 * jax.random.normal(jax.random.fold_in(_gk, 1), (12500, 256), jnp.float32)
        src = jax.random.randint(jax.random.fold_in(_gk, 2), (200000,), 0, 12500, jnp.int32)
        dst = jnp.minimum((12500 * jax.random.uniform(jax.random.fold_in(_gk, 3), (200000,)) ** 2.0).astype(jnp.int32), 99999)
        _o = jnp.argsort(dst, stable=True)
        src = src[_o]
        dst = dst[_o]
        edge_weight = jax.random.uniform(jax.random.fold_in(_gk, 12), (200000,), jnp.float32, 0.0, 1)
        return (x, src, dst, edge_weight)
    x, src, dst, edge_weight = _rec_inputs()

    def _L0_gnn_setup():
        import jax, jax.numpy as jnp
        import numpy as np
        N_NODES = 12500
        N_EDGES = 400000
        IN_FEATS = 256
        OUT_FEATS = 256
        key = jax.random.key(seed)
        k1, k2, k3, k4, k5, k6 = jax.random.split(key, 6)
        features = jax.random.normal(k1, (N_NODES, IN_FEATS), dtype=jnp.float32)
        edge_src = jax.random.randint(k2, (N_EDGES,), 0, N_NODES, dtype=jnp.int64)
        edge_dst = jnp.sort(jax.random.randint(k3, (N_EDGES,), 0, N_NODES, dtype=jnp.int64))
        edge_weight = jax.random.uniform(k4, (N_EDGES,), dtype=jnp.float32)
        bound = 1.0 / np.sqrt(IN_FEATS)
        W = jax.random.uniform(k5, (OUT_FEATS, IN_FEATS), dtype=jnp.float32, minval=-bound, maxval=bound)
        b = jax.random.uniform(k6, (OUT_FEATS,), dtype=jnp.float32, minval=-bound, maxval=bound)
        return {'features': features, 'edge_src': edge_src, 'edge_dst': edge_dst, 'edge_weight': edge_weight, 'W': W, 'b': b}
    _L0_gnn_all = _L0_gnn_setup()
    _L0_gnn_in = {k: v for k, v in _L0_gnn_all.items() if k in ('W', 'b')}
    del _L0_gnn_all

    def _L0_ffn_setup():
        import jax, jax.numpy as jnp
        import numpy as np
        B, N, D = (16, 512, 256)
        NUM_EXPERTS, TOP_K, HEADS = (4, 2, 4)
        N_EDGES = 131072
        LN_EPS = 1e-05

        def _layernorm(x, g, b):
            mu = x.mean(-1, keepdims=True)
            var = ((x - mu) ** 2).mean(-1, keepdims=True)
            return (x - mu) * jax.lax.rsqrt(var + LN_EPS) * g + b

        def _forward(x, edge_index, W_gat, att_src, att_dst, b_gat, ln_gamma, ln_beta, W1, b1, W2, b2):
            Bc, Nc, Dc = x.shape
            M = Bc * Nc
            x_flat = x.reshape(M, Dc)
            h = (x_flat @ W_gat).reshape(M, HEADS, NUM_EXPERTS)
            loops = jnp.arange(M, dtype=edge_index.dtype)
            src = jnp.concatenate([edge_index[0], loops])
            dst = jnp.concatenate([edge_index[1], loops])
            a_src = (h * att_src).sum(-1)
            a_dst = (h * att_dst).sum(-1)
            e = jax.nn.leaky_relu(a_src[src] + a_dst[dst], negative_slope=0.2)
            e_max = jax.ops.segment_max(e, dst, num_segments=M)
            ee = jnp.exp(e - e_max[dst])
            denom = jax.ops.segment_sum(ee, dst, num_segments=M)
            alpha = ee / (denom[dst] + 1e-16)
            msg = h[src] * alpha[:, :, None]
            agg = jax.ops.segment_sum(msg, dst, num_segments=M).reshape(M, HEADS * NUM_EXPERTS) + b_gat
            scores = _layernorm(agg, ln_gamma, ln_beta).reshape(M, HEADS, NUM_EXPERTS).mean(1)
            scores = scores.reshape(Bc, Nc, NUM_EXPERTS)
            topk_s, topk_i = jax.lax.top_k(scores, TOP_K)
            w = jax.nn.softmax(topk_s, axis=-1)
            out = jnp.zeros_like(x)
            for ei in range(NUM_EXPERTS):
                g = jnp.where(topk_i == ei, w, 0.0).sum(-1)
                hh = jax.nn.gelu(x @ W1[ei] + b1[ei], approximate=False)
                out = out + g[..., None] * (hh @ W2[ei] + b2[ei])
            return out
        key = jax.random.key(seed)
        ks = jax.random.split(key, 8)
        s = 0.05
        return {'x': jax.random.normal(ks[0], (B, N, D), jnp.float32), 'W_gat': jax.random.normal(ks[1], (D, HEADS * NUM_EXPERTS), jnp.float32) * s, 'att_src': jax.random.normal(ks[2], (HEADS, NUM_EXPERTS), jnp.float32) * s, 'att_dst': jax.random.normal(ks[3], (HEADS, NUM_EXPERTS), jnp.float32) * s, 'b_gat': jnp.zeros((HEADS * NUM_EXPERTS,), jnp.float32), 'ln_gamma': jnp.ones((HEADS * NUM_EXPERTS,), jnp.float32), 'ln_beta': jnp.zeros((HEADS * NUM_EXPERTS,), jnp.float32), 'W1': jax.random.normal(ks[4], (NUM_EXPERTS, D, 2 * D), jnp.float32) * s, 'b1': jnp.zeros((NUM_EXPERTS, 2 * D), jnp.float32), 'W2': jax.random.normal(ks[5], (NUM_EXPERTS, 2 * D, D), jnp.float32) * s, 'b2': jnp.zeros((NUM_EXPERTS, D), jnp.float32), 'edge_index': jax.random.randint(ks[6], (2, N_EDGES), 0, B * N, jnp.int32)}
    _L0_ffn_all = _L0_ffn_setup()
    _L0_ffn_in = {k: v for k, v in _L0_ffn_all.items() if k in ('W_gat', 'att_src', 'att_dst', 'b_gat', 'ln_gamma', 'ln_beta', 'W1', 'b1', 'W2', 'b2', 'edge_index')}
    del _L0_ffn_all
    return {'x': x, 'src': src, 'dst': dst, 'edge_weight': edge_weight, 'L0_gnn_W': _L0_gnn_in['W'], 'L0_gnn_b': _L0_gnn_in['b'], 'L0_ffn_W_gat': _L0_ffn_in['W_gat'], 'L0_ffn_att_src': _L0_ffn_in['att_src'], 'L0_ffn_att_dst': _L0_ffn_in['att_dst'], 'L0_ffn_b_gat': _L0_ffn_in['b_gat'], 'L0_ffn_ln_gamma': _L0_ffn_in['ln_gamma'], 'L0_ffn_ln_beta': _L0_ffn_in['ln_beta'], 'L0_ffn_W1': _L0_ffn_in['W1'], 'L0_ffn_b1': _L0_ffn_in['b1'], 'L0_ffn_W2': _L0_ffn_in['W2'], 'L0_ffn_b2': _L0_ffn_in['b2'], 'L0_ffn_edge_index': _L0_ffn_in['edge_index']}

def reference(x, src, dst, edge_weight, L0_gnn_W, L0_gnn_b, L0_ffn_W_gat, L0_ffn_att_src, L0_ffn_att_dst, L0_ffn_b_gat, L0_ffn_ln_gamma, L0_ffn_ln_beta, L0_ffn_W1, L0_ffn_b1, L0_ffn_W2, L0_ffn_b2, L0_ffn_edge_index):
    import jax
    import jax.numpy as jnp

    def _L0_gnn_ref(features, edge_src, edge_dst, edge_weight, W, b):
        import jax, jax.numpy as jnp
        import numpy as np
        N_NODES = 12500
        N_EDGES = 400000
        IN_FEATS = 256
        OUT_FEATS = 256
        msgs = features[edge_src] * edge_weight[:, None]
        agg = jax.ops.segment_sum(msgs, edge_dst, num_segments=N_NODES, indices_are_sorted=True)
        return jnp.einsum('ni,oi->no', agg, W) + b

    def _L0_ffn_ref(x, W_gat, att_src, att_dst, b_gat, ln_gamma, ln_beta, W1, b1, W2, b2, edge_index):
        import jax, jax.numpy as jnp
        import numpy as np
        B, N, D = (16, 512, 256)
        NUM_EXPERTS, TOP_K, HEADS = (4, 2, 4)
        N_EDGES = 131072
        LN_EPS = 1e-05

        def _layernorm(x, g, b):
            mu = x.mean(-1, keepdims=True)
            var = ((x - mu) ** 2).mean(-1, keepdims=True)
            return (x - mu) * jax.lax.rsqrt(var + LN_EPS) * g + b

        def _forward(x, edge_index, W_gat, att_src, att_dst, b_gat, ln_gamma, ln_beta, W1, b1, W2, b2):
            Bc, Nc, Dc = x.shape
            M = Bc * Nc
            x_flat = x.reshape(M, Dc)
            h = (x_flat @ W_gat).reshape(M, HEADS, NUM_EXPERTS)
            loops = jnp.arange(M, dtype=edge_index.dtype)
            src = jnp.concatenate([edge_index[0], loops])
            dst = jnp.concatenate([edge_index[1], loops])
            a_src = (h * att_src).sum(-1)
            a_dst = (h * att_dst).sum(-1)
            e = jax.nn.leaky_relu(a_src[src] + a_dst[dst], negative_slope=0.2)
            e_max = jax.ops.segment_max(e, dst, num_segments=M)
            ee = jnp.exp(e - e_max[dst])
            denom = jax.ops.segment_sum(ee, dst, num_segments=M)
            alpha = ee / (denom[dst] + 1e-16)
            msg = h[src] * alpha[:, :, None]
            agg = jax.ops.segment_sum(msg, dst, num_segments=M).reshape(M, HEADS * NUM_EXPERTS) + b_gat
            scores = _layernorm(agg, ln_gamma, ln_beta).reshape(M, HEADS, NUM_EXPERTS).mean(1)
            scores = scores.reshape(Bc, Nc, NUM_EXPERTS)
            topk_s, topk_i = jax.lax.top_k(scores, TOP_K)
            w = jax.nn.softmax(topk_s, axis=-1)
            out = jnp.zeros_like(x)
            for ei in range(NUM_EXPERTS):
                g = jnp.where(topk_i == ei, w, 0.0).sum(-1)
                hh = jax.nn.gelu(x @ W1[ei] + b1[ei], approximate=False)
                out = out + g[..., None] * (hh @ W2[ei] + b2[ei])
            return out
        return _forward(x, edge_index, W_gat, att_src, att_dst, b_gat, ln_gamma, ln_beta, W1, b1, W2, b2)
    x = x + _L0_gnn_ref(_layernorm(x, axis=-1), src, dst, edge_weight, L0_gnn_W, L0_gnn_b)
    x = x + _L0_ffn_ref(_layernorm(x, axis=-1)[None], L0_ffn_W_gat, L0_ffn_att_src, L0_ffn_att_dst, L0_ffn_b_gat, L0_ffn_ln_gamma, L0_ffn_ln_beta, L0_ffn_W1, L0_ffn_b1, L0_ffn_W2, L0_ffn_b2, L0_ffn_edge_index)[0]
    return x

_drawn_inputs = setup_inputs


def setup_inputs(seed=0):
    import zlib

    import numpy as np

    out = dict(_drawn_inputs(seed))
    spreads = {'L0_ffn_b_gat': (0.0, 0.1),
     'L0_ffn_ln_gamma': (1.0, 0.2),
     'L0_ffn_ln_beta': (0.0, 0.1),
     'L0_ffn_b1': (0.0, 0.1),
     'L0_ffn_b2': (0.0, 0.1)}
    factors = {}
    for name, (base, spread) in spreads.items():
        noise = np.random.default_rng([zlib.crc32(name.encode()), seed]).standard_normal(out[name].shape)
        drawn = base * np.exp(spread * noise) if base else spread * noise
        out[name] = jnp.asarray(drawn.astype(out[name].dtype))
    for name, factor in factors.items():
        out[name] = (out[name] * factor).astype(out[name].dtype)
    return out
```

```python
from contextlib import ExitStack

import concourse.bass as bass
from concourse import mybir

F32 = mybir.dt.float32
BF16 = mybir.dt.bfloat16
I32 = mybir.dt.int32
ALU = mybir.AluOpType
ACT = mybir.ActivationFunctionType
AX_X = mybir.AxisListType.X
ds = bass.ds

P = 128
NODES = 12500
FEAT = 256
TILES = -(-NODES // P)
NPAD = TILES * P
FULL_TILES = NODES // P
LAST_ROWS = NODES - FULL_TILES * P
CH = 7
CHUNKS = TILES // CH
LN_EPS = 1e-5

EDGES = 200000
ETILES = -(-EDGES // P)
GT = 4
GROUPS = -(-ETILES // GT)
EBLOCKS = -(-ETILES // P)
ECOLS = EBLOCKS * P
STEPS = GROUPS + TILES - 1
RING = 8
HALVES = FEAT // P

GEDGES = 131072
GCOLS = GEDGES // P
KEY_SHIFT = 14
KEY_TOP = 1 << 28
HCOLS = 32
HPIECES = GCOLS // HCOLS

HEADS, EXPERTS = 4, 4
HID = 2 * FEAT
HE = HEADS * EXPERTS
ROWF = HE + HEADS
STATE = HE + 2 * HEADS
BIG = 1.5e38
SLOPE = 0.2


class Shared:
    pass


class Count:

    def __init__(self, eng, sem, start=0):
        self.eng, self.sem, self.n = eng, sem, start

    def inc(self, ins):
        self.n += 1
        return ins.then_inc(self.sem, 1)

    def done(self, ins):
        self.inc(ins)
        self.eng.wait_ge(self.sem, self.n)


def build(nc, x, src, dst, edge_weight, W, b, W_gat, att_src, att_dst, b_gat, gamma, beta,
          W1, b1, W2, b2, edge_index, out):
    m = Shared()

    def dram(name, shape):
        return nc.dram_tensor(name, shape, F32).ap()

    feats = dram("feats", (NPAD, FEAT))
    m.x1_dram = dram("x1_dram", (NPAD, FEAT))
    m.yt_dram = dram("yt_dram", (P, HALVES, NPAD))
    m.y_dram = dram("y_dram", (NPAD, EXPERTS, FEAT))
    m.row_dram = dram("row_dram", (NPAD, ROWF))
    m.adst_dram = dram("adst_dram", (NPAD, HEADS))
    m.adst_first = dram("adst_first", (GEDGES, HEADS))
    m.state_dram = dram("state_dram", (GEDGES, STATE))

    with ExitStack() as top:
        def sem(name):
            return top.enter_context(nc.semaphore(name))

        def keep(name, shape, dt=F32):
            return top.enter_context(nc.sbuf_tensor(name, shape, dt))

        m.ident = keep("ident", [P, P])
        m.ones = keep("ones", [P, P])
        m.iota = keep("iota", [P, P])
        m.eps = keep("eps", [P, 1])
        m.src_sorted = keep("src_sorted", [P, GCOLS], I32)
        m.seg_keep = keep("seg_keep", [P, GCOLS])
        m.dst_first = keep("dst_first", [P, 1], I32)
        m.link = keep("link", [P, 2])
        m.first_pos = keep("first_pos", [P, TILES], I32)
        m.last_pos = keep("last_pos", [P, TILES], I32)
        m.has_edges = keep("has_edges", [P, TILES])
        m.node_row = keep("node_row", [P, TILES, ROWF])
        m.node_dst = keep("node_dst", [P, TILES, HEADS])

        with ExitStack() as part1:
            def sb(name, shape, dt=F32):
                return part1.enter_context(nc.sbuf_tensor(name, shape, dt))

            m.acc = sb("acc", [P, TILES, FEAT])
            m.dst_t = sb("dst_t", [P, ECOLS])
            m.src_t = sb("src_t", [P, ECOLS], I32)
            m.ew_t = sb("ew_t", [P, ECOLS])
            m.step_group = sb("step_group", [P, STEPS], I32)
            m.step_slot = sb("step_slot", [P, STEPS], I32)
            m.step_tile = sb("step_tile", [P, STEPS], I32)
            m.step_base = sb("step_base", [P, STEPS])
            m.group_end = sb("group_end", [P, GROUPS], I32)
            layernorm_and_plan(nc, sem, x, src, dst, edge_weight, feats, m)
            weighted_sums(nc, sem, feats, edge_index, m)
            node_update(nc, sem, x, W, b, W_gat, att_src, att_dst, m)
        with nc.sbuf_tensor("states", [P, GCOLS, STATE], F32) as states:
            m.states = states
            gather_and_experts(nc, sem, W1, b1, W2, b2, edge_index, m)
            segment_softmax(nc, sem, m)
        combine(nc, sem, b_gat, gamma, beta, out, m)


def layernorm_and_plan(nc, sem, x, src, dst, ew, feats, m):
    with ExitStack() as ctx:
        def sb(name, shape, dt):
            return ctx.enter_context(nc.sbuf_tensor(name, shape, dt))

        xin = sb("xin", [P, 2, CH, FEAT], F32)
        xout = sb("xout", [P, 2, CH, FEAT], F32)
        stats = sb("stats", [P, 2, CH, 6], F32)
        mv = sb("mv", [P, 2, CH, 2], F32)
        rstd = sb("rstd", [P, 2, CH], F32)
        lent = m.acc[:].rearrange("p t f -> p (t f)")
        raw_i = lent[:, 0:2 * ECOLS].bitcast(I32).rearrange("p (a b e) -> p a b e", a=2, e=P)
        raw_f = lent[:, 2 * ECOLS:5 * ECOLS].rearrange("p (a b e) -> p a b e", a=3, e=P)
        LENT = -(-5 * ECOLS // (CH * FEAT)) * CH
        last_sel = sb("last_sel", [P, P], F32)
        gi = sb("gi", [P, GROUPS], I32)
        gf = sb("gf", [P, GROUPS], F32)
        ge = sb("ge", [P, GROUPS], F32)
        giota = sb("giota", [P, STEPS], F32)
        gend = sb("gend", [P, 4], F32)
        spent = lent[:, 2 * ECOLS:5 * ECOLS]
        passed = spent[:, 0:4 * STEPS].rearrange("p (q s) -> p q s", q=4)
        gdiag = spent[:, 4 * STEPS:4 * STEPS + 4 * P].rearrange("p (q n) -> p q n", q=4)
        stepf = spent[:, 4 * STEPS + 4 * P:6 * STEPS + 4 * P].rearrange("p (q s) -> p q s", q=2)
        turn = ctx.enter_context(nc.psum_tensor("turn", [P, 2, 2048], F32))

        s_const, s_raw0, s_raw = sem("a_const"), sem("a_raw_cleared"), sem("a_raw_loaded")
        s_xin = [sem("a_x0"), sem("a_x1")]
        s_out = [sem("a_out0"), sem("a_out1")]
        s_clear = sem("a_x_cleared")
        s_past = sem("a_past")
        s_var, s_std, s_norm = sem("a_var"), sem("a_std"), sem("a_norm")
        s_v, s_t, s_ev = sem("a_vector"), sem("a_turned"), sem("a_turn_read")
        s_pl = sem("a_pool")
        s_edge = sem("a_edge_vector")

        x_tiles = x[0:FULL_TILES * P, :].rearrange("(t p) f -> p t f", p=P)
        f_tiles = feats.rearrange("(t p) f -> p t f", p=P)
        main = (EBLOCKS - 1) * P * P
        rest = (EDGES - main) // P
        tail = EDGES - main - rest * P

        block = ctx.enter_context(nc.Block())

        @block.sync
        def _(sp):
            sp.wait_ge(s_raw0, 3)
            for a, t in ((dst, raw_i[:, 0]), (src, raw_i[:, 1]), (ew, raw_f[:, 2])):
                sp.dma_start(t[:, 0:EBLOCKS - 1, :],
                             a[0:main].rearrange("(b q e) -> q b e", q=P, e=P)).then_inc(s_raw, 16)
                sp.dma_start(t[0:rest, EBLOCKS - 1, :],
                             a[main:main + rest * P].rearrange("(q e) -> q e", e=P)).then_inc(s_raw, 16)
                sp.dma_start(t[rest:rest + 1, EBLOCKS - 1, 0:tail],
                             a[main + rest * P:EDGES].rearrange("(q e) -> q e", q=1)).then_inc(s_raw, 16)

            def load(c, k):
                sp.dma_start(xin[:, k, :, :], x_tiles[:, ds(c * CH, CH), :]).then_inc(s_xin[k], 16)

            def store(c, k, n):
                sp.wait_ge(s_norm, n)
                sp.dma_start(f_tiles[:, ds(c * CH, CH), :], xout[:, k, :, :]).then_inc(s_out[k], 16)

            load(0, 0)
            load(1, 1)
            with sp.Fori(1, CHUNKS // 2 - 1) as i:
                for k in range(2):
                    store(i * 2 + k - 2, k, i * 2 + k - 1)
                    load(i * 2 + k, k)
            for k in range(2):
                c = CHUNKS - 2 + k
                store(c - 2, k, c - 1)
                if k == 0:
                    load(c, k)
                else:
                    sp.dma_start(xin[:, k, 0:CH - 1, :], x_tiles[:, c * CH:FULL_TILES, :]).then_inc(s_xin[k], 16)
                    sp.wait_ge(s_clear, 1)
                    sp.dma_start(xin[0:LAST_ROWS, k, CH - 1, :], x[FULL_TILES * P:NODES, :]).then_inc(s_xin[k], 16)
            for k in range(2):
                store(CHUNKS - 2 + k, k, CHUNKS - 1 + k)
            for k in range(2):
                sp.wait_ge(s_out[k], 16 * (CHUNKS // 2))

        @block.gpsimd
        def _(pool):
            pool.memset(raw_i[:, 0, :, :], -1).then_inc(s_raw0, 1)
            pool.memset(raw_i[:, 1, :, :], 0).then_inc(s_raw0, 1)
            pool.memset(raw_f[:, 2, :, :], 0.0).then_inc(s_raw0, 1)
            c = Count(pool, s_pl)
            c.inc(pool.memset(m.ident[:], 0.0))
            c.inc(pool.memset(m.ones[:], 1.0))
            c.inc(pool.memset(last_sel[:], 0.0))
            pool.memset(m.eps[:], LN_EPS).then_inc(s_const, 1)
            pool.iota(m.iota[:], pattern=[[1, P]], base=0, channel_multiplier=0,
                      allow_small_or_imprecise_dtypes=True).then_inc(s_const, 1)
            pool.iota(giota[:], pattern=[[1, STEPS]], base=0, channel_multiplier=0,
                      allow_small_or_imprecise_dtypes=True).then_inc(s_const, 1)
            pool.wait_ge(s_pl, c.n)
            pool.affine_select(out=m.ident[:], in_=m.ident[:], compare_op=ALU.not_equal, fill=1.0, base=0,
                               pattern=[[-1, P]], channel_multiplier=1).then_inc(s_const, 1)
            pool.affine_select(out=last_sel[:], in_=last_sel[:], compare_op=ALU.not_equal, fill=1.0,
                               base=1 - P, pattern=[[0, P]], channel_multiplier=1).then_inc(s_const, 1)
            for t in range(LENT, TILES, CH):
                pool.memset(m.acc[:, t:t + CH, :], 0.0).then_inc(s_const, 1)
            pool.wait_ge(s_ev, 5)
            for t in range(0, LENT, CH):
                pool.memset(m.acc[:, t:t + CH, :], 0.0).then_inc(s_const, 1)

        @block.scalar
        def _(act):
            act.wait_ge(s_const, 1)
            with act.Fori(0, CHUNKS // 2) as i:
                for k in range(2):
                    act.wait_ge(s_var, i * 2 + (k + 1))
                    act.activation(rstd[:, k, :], mv[:, k, :, 1], ACT.Sqrt, bias=m.eps[:, 0:1]).then_inc(s_std, 1)

        @block.vector
        def _(v):
            c = Count(v, s_edge)

            v.wait_ge(s_raw, 9 * 16)
            for a in range(2):
                c.inc(v.tensor_copy(raw_f[:, a, :, :], raw_i[:, a, :, :]))
            for n, t in enumerate((m.dst_t, m.src_t, m.ew_t)):
                v.wait_ge(s_t, n + 1)
                c.inc(v.tensor_copy(t[:], turn[:, n % 2, 0:ECOLS]))
                v.wait_ge(s_edge, c.n)
                v.sem_inc(s_ev, 1)
            v.wait_ge(s_t, 4)
            c.done(v.tensor_copy(gi[:], turn[:, 1, 0:GROUPS]))
            c.done(v.tensor_scalar(gi[:], gi[:], 7, None, ALU.arith_shift_right))
            c.done(v.tensor_copy(gf[:], gi[:]))
            c.done(v.memset(gf[:, GROUPS - 1:GROUPS], float(TILES - 1)))
            v.wait_ge(s_const, 5)
            c.done(v.tensor_tensor(ge[:], gf[:], giota[:, 0:GROUPS], ALU.add))
            c.inc(v.tensor_scalar(m.group_end[:], ge[:], 1.0, None, ALU.add))
            for q in range(4):
                w = min(P, GROUPS - q * P)
                c.inc(v.tensor_tensor(gdiag[:, q, 0:w], ge[:, q * P:q * P + w], m.ident[:, 0:w], ALU.mult))
            v.wait_ge(s_edge, c.n)
            for q in range(4):
                w = min(P, GROUPS - q * P)
                c.inc(v.tensor_reduce(gend[:, q:q + 1], gdiag[:, q, 0:w], AX_X, ALU.add))
            v.wait_ge(s_edge, c.n)
            for q in range(4):
                c.inc(v.tensor_scalar(passed[:, q, :], giota[:], gend[:, q:q + 1], None, ALU.is_gt))
            v.wait_ge(s_edge, c.n)
            v.sem_inc(s_ev, 1)
            v.wait_ge(s_t, 5)
            c.done(v.tensor_copy(stepf[:, 0, :], turn[:, 0, 0:STEPS]))
            c.inc(v.tensor_copy(m.step_group[:], stepf[:, 0, :]))
            c.done(v.tensor_tensor(stepf[:, 1, :], giota[:], stepf[:, 0, :], ALU.subtract))
            c.inc(v.tensor_copy(m.step_tile[:], stepf[:, 1, :]))
            c.inc(v.tensor_scalar(m.step_base[:], stepf[:, 1, :], float(P), None, ALU.mult))
            c.done(v.tensor_scalar(m.step_slot[:], m.step_group[:], RING - 1, None, ALU.bitwise_and))
            v.sem_inc(s_ev, 1)

            def normalise(i, k, last=False):
                n = i * 2 + k
                v.wait_ge(s_xin[k], i * 16 + (32 if last else 16))
                for t in range(CH):
                    q = v.bn_stats(stats[:, k, t, :], xin[:, k, t, :])
                q.then_inc(s_v, 1)
                v.wait_ge(s_v, n * 3 + 1)
                v.sem_inc(s_past, 1)
                for t in range(CH):
                    q = v.bn_aggr(mv[:, k, t, :], stats[:, k, t, :])
                q.then_inc(s_var, 1)
                v.wait_ge(s_std, n + 1)
                v.reciprocal(rstd[:, k, :], rstd[:, k, :]).then_inc(s_v, 1)
                v.wait_ge(s_v, n * 3 + 2)
                if not (isinstance(i, int) and i == 0):
                    v.wait_ge(s_out[k], i * 16)
                for t in range(CH):
                    q = v.tensor_scalar(xout[:, k, t, :], xin[:, k, t, :], mv[:, k, t, 0:1],
                                        rstd[:, k, t:t + 1], ALU.subtract, ALU.mult)
                    if t == CH - 2:
                        q.then_inc(s_v, 1)
                q.then_inc(s_norm, 1)

            normalise(0, 0)
            normalise(0, 1)
            with v.Fori(1, CHUNKS // 2 - 1) as i:
                for k in range(2):
                    normalise(i, k)
            normalise(CHUNKS // 2 - 1, 0)
            v.wait_ge(s_norm, CHUNKS - 2)
            v.memset(xin[:, 1, CH - 1, :], 0.0).then_inc(s_clear, 1)
            normalise(CHUNKS // 2 - 1, 1, last=True)
            v.wait_ge(s_norm, CHUNKS)

        @block.tensor
        def _(pe):
            pe.wait_ge(s_edge, 2)
            pe.wait_ge(s_const, 5)
            for n in range(3):
                if n == 2:
                    pe.wait_ge(s_ev, 1)
                for q in range(EBLOCKS):
                    t = pe.transpose(turn[:, n % 2, q * P:(q + 1) * P], raw_f[:, n, q, :], m.ident[:])
                t.then_inc(s_t, 1)
            pe.wait_ge(s_ev, 2)
            pe.matmul(turn[:, 1, 0:GROUPS], last_sel[:], m.dst_t[:, GT - 1:GROUPS * GT:GT],
                      start=True, stop=True).then_inc(s_t, 1)
            pe.wait_ge(s_ev, 4)
            for q in range(4):
                w = min(P, GROUPS - q * P)
                t = pe.matmul(turn[:, 0, 0:STEPS], m.ones[0:w, :], passed[0:w, q, :], start=(q == 0), stop=(q == 3))
            t.then_inc(s_t, 1)


def weighted_sums(nc, sem, feats, edge_index, m):
    with ExitStack() as ctx:
        def sb(name, shape, dt):
            return ctx.enter_context(nc.sbuf_tensor(name, shape, dt))

        rows = sb("rows", [P, RING, GT, FEAT], F32)
        idx = sb("idx", [P, RING, GT], I32)
        rel = sb("rel", [P, 2, GT], F32)
        hot = sb("hot", [P, 2, GT, P], F32)
        key = sb("key", [P, 3, GCOLS], F32)
        key_i = [key[:, n, :].bitcast(I32) for n in range(3)]
        sign = sb("sign", [P, 2], F32)
        shift_dn = sb("shift_dn", [P, P], F32)
        lastd = sb("lastd", [P, 2], F32)
        psA = [ctx.enter_context(nc.psum_tensor(f"sums{n}", [P, 512], F32)) for n in range(2)]
        psD = ctx.enter_context(nc.psum_tensor("prefix", [P, 512], F32))
        psT = ctx.enter_context(nc.psum_tensor("turned", [P, GCOLS], F32))

        s_ei = sem("b_edge_index")
        s_idx, s_ready = sem("b_idx_ready"), sem("b_rows_ready")
        s_got = [sem(f"b_gathered{k}") for k in range(RING)]
        s_past = sem("b_past")
        s_rel, s_hot, s_mm, s_acc = sem("b_rel"), sem("b_hot_ready"), sem("b_step_multiplied"), sem("b_step_added")
        s_s = sem("b_sort")
        s_turn, s_turned = sem("b_turn_ask"), sem("b_turned")
        s_pc = sem("b_pool_const")

        block = ctx.enter_context(nc.Block())
        full_rounds = GROUPS // RING
        left = GROUPS - full_rounds * RING

        PAIRS = STEPS // 2
        PHASES = GEDGES.bit_length() - 1
        CUT = [(PAIRS - 1) * n // PHASES for n in range(PHASES + 1)]
        assert STEPS % 2 == 0

        @block.sync
        def _(sp):
            sp.dma_start(key_i[0], edge_index[1, :].rearrange("(p j) -> p j", p=P)).then_inc(s_ei, 16)
            sp.dma_start(key_i[1], edge_index[0, :].rearrange("(p j) -> p j", p=P)).then_inc(s_ei, 16)
            sp.wait_ge(s_ei, 32)

        @block.scalar
        def _(act):
            def indices(g, k):
                act.copy(idx[:, k, :], m.src_t[:, ds(g * GT, GT)]).then_inc(s_idx, 1)

            for k in range(RING):
                indices(k, k)
            with act.Fori(0, full_rounds) as i:
                for k in range(RING):
                    act.wait_ge(s_got[k], i * (16 * GT) + 16 * GT)
                    act.sem_inc(s_ready, 1)
                    indices(i * RING + (RING + k), k)
            for k in range(left):
                act.wait_ge(s_got[k], (full_rounds + 1) * 16 * GT)
                act.sem_inc(s_ready, 1)

        @block.gpsimd
        def _(pool):
            c = Count(pool, s_pc)
            c.inc(pool.memset(shift_dn[:], 0.0))
            c.inc(pool.iota(sign[:, 1:2], pattern=[[0, 1]], base=0, channel_multiplier=1,
                            allow_small_or_imprecise_dtypes=True))
            pool.wait_ge(s_pc, c.n)
            c.inc(pool.affine_select(out=shift_dn[:], in_=shift_dn[:], compare_op=ALU.not_equal, fill=1.0,
                                     base=1, pattern=[[-1, P]], channel_multiplier=1))

            def gather(k):
                for j in range(GT):
                    pool.indirect_dma_start(rows[:, k, j, :], None, feats,
                                            bass.IndirectOffsetOnAxis(ap=idx[:, k, j:j + 1], axis=0)
                                            ).then_inc(s_got[k], 16)

            for k in range(RING):
                pool.wait_ge(s_idx, k + 1)
                gather(k)

            def refill(i, k):
                end = pool.value_load(m.group_end[0:1, ds(i * RING + (k - RING), 1)], min_val=1, max_val=STEPS)
                pool.wait_ge(s_mm, end)
                pool.wait_ge(s_idx, i * RING + (k + 1))
                pool.sem_inc(s_past, 1)
                gather(k)

            with pool.Fori(1, full_rounds) as i:
                for k in range(RING):
                    refill(i, k)
            for k in range(left):
                refill(full_rounds, k)

        def key_at(k, back):
            return plan[(k, back)]

        plan, cur = {}, 2
        for k in range(1, 18):
            if k >= 11:
                plan[(k, 0)] = cur
                cur = 1 if cur != 1 else 0
                for _ in range(k - 10):
                    cur = 1 - cur
                plan[(k, 1)] = cur
                cur = 1 - cur
                for _ in range(10):
                    cur = 1 - cur
            else:
                for _ in range(k):
                    cur = 1 if cur == 2 else 1 - cur

        @block.tensor
        def _(pe):
            def step(s, par, first=False):
                g = pe.value_load(m.step_group[0:1, ds(s, 1)], min_val=0, max_val=GROUPS - 1)
                slot = pe.value_load(m.step_slot[0:1, ds(s, 1)], min_val=0, max_val=RING - 1)
                pe.wait_ge(s_hot, s + 1)
                pe.wait_ge(s_ready, g + 1)
                if not first:
                    pe.wait_ge(s_acc, s - 1)
                for j in range(GT):
                    t = pe.matmul(psA[par][:, 0:FEAT], hot[:, par, j, :], rows[:, ds(slot, 1), j, :],
                                  start=(j == 0), stop=(j == GT - 1))
                t.then_inc(s_mm, 1)

            pe.wait_ge(s_pc, 3)
            for par in range(2):
                step(par, par, first=True)
            hp, turns = 0, 0
            for n, a in enumerate(range(1, PHASES + 1)):
                with pe.Fori(1 + CUT[n], 1 + CUT[n + 1]) as u:
                    for par in range(2):
                        step(u * 2 + par, par)
                if a >= 11:
                    for back in range(2):
                        turns += 1
                        pe.wait_ge(s_turn, turns)
                        cur = key_at(a, back)
                        for q in range(GCOLS // P):
                            t = pe.transpose(psT[:, q * P:(q + 1) * P], key[:, cur, q * P:(q + 1) * P], m.ident[:])
                        t.then_inc(s_turned, 1)
            pe.wait_ge(s_turn, 1 + turns)
            pe.matmul(psD[:, 0:2], shift_dn[:], lastd[:], start=True, stop=True).then_inc(s_turned, 1)

        @block.vector
        def _(v):
            c = Count(v, s_s)

            def one_hots(s, par, first=False):
                g = v.value_load(m.step_group[0:1, ds(s, 1)], min_val=0, max_val=GROUPS - 1)
                if not first:
                    v.wait_ge(s_mm, s - 1)
                v.tensor_scalar(rel[:, par, :], m.dst_t[:, ds(g * GT, GT)], m.step_base[:, ds(s, 1)], None,
                                ALU.subtract).then_inc(s_rel, 1)
                v.wait_ge(s_rel, s + 1)
                for j in range(GT):
                    t = v.tensor_scalar(hot[:, par, j, :], m.iota[:], rel[:, par, j:j + 1],
                                        m.ew_t[:, ds(g * GT + j, 1)], ALU.is_equal, ALU.mult)
                t.then_inc(s_hot, 1)

            def add(s, par, first=False):
                d = v.value_load(m.step_tile[0:1, ds(s, 1)], min_val=0, max_val=TILES - 1)
                v.wait_ge(s_mm, s + 1)
                if not first:
                    v.wait_ge(s_acc, s)
                v.tensor_tensor(m.acc[:, ds(d, 1), :], m.acc[:, ds(d, 1), :], psA[par][:, 0:FEAT],
                                ALU.add).then_inc(s_acc, 1)

            def sort_init():
                v.wait_ge(s_ei, 32)
                c.done(v.tensor_scalar(key_i[0], key_i[0], KEY_SHIFT, KEY_TOP, ALU.logical_shift_left,
                                       ALU.bitwise_or))
                c.done(v.tensor_tensor(key_i[2], key_i[0], key_i[1], ALU.bitwise_or))
                v.wait_ge(s_pc, 3)
                c.done(v.tensor_copy(m.dst_first[:], sign[:, 1:2]))
                c.done(v.tensor_scalar(m.dst_first[:], m.dst_first[:], 1, None, ALU.bitwise_and))
                c.done(v.tensor_copy(sign[:, 0:1], m.dst_first[:]))
                c.done(v.tensor_scalar(sign[:, 0:1], sign[:, 0:1], -2.0, 1.0, ALU.mult, ALU.add))

            def flip(buf, k, col_bits):
                t = key[:, buf, :]
                hb, lb = k - col_bits, k - 1 - col_bits
                if k == 1:
                    w = t.rearrange("p (a h w) -> p a h w", h=2, w=1 << hb)
                    c.done(v.tensor_scalar(w[:, :, 1, :], w[:, :, 1, :], -1.0, None, ALU.mult))
                elif k == 17:
                    w = t.rearrange("p (a h w) -> p a h w", h=2, w=1 << lb)
                    c.done(v.tensor_scalar(w[:, :, 1, :], w[:, :, 1, :], -1.0, None, ALU.mult))
                elif k == 10:
                    w = t.rearrange("p (a h w) -> p a h w", h=2, w=1 << lb)
                    c.done(v.tensor_scalar(w[:, :, 1, :], w[:, :, 1, :], -1.0, None, ALU.mult))
                    c.done(v.tensor_scalar(t, t, sign[:, 0:1], None, ALU.mult))
                else:
                    w = t.rearrange("p (a h l w) -> p a h l w", h=2, l=2, w=1 << lb)
                    c.inc(v.tensor_scalar(w[:, :, 0, 1, :], w[:, :, 0, 1, :], -1.0, None, ALU.mult))
                    c.done(v.tensor_scalar(w[:, :, 1, 0, :], w[:, :, 1, 0, :], -1.0, None, ALU.mult))

            def exchange(buf, bit):
                to = 1 if buf == 2 else 1 - buf
                a = key[:, buf, :].rearrange("p (a h w) -> p a h w", h=2, w=1 << bit)
                o = key[:, to, :].rearrange("p (a h w) -> p a h w", h=2, w=1 << bit)
                c.inc(v.tensor_tensor(o[:, :, 0, :], a[:, :, 0, :], a[:, :, 1, :], ALU.min))
                c.done(v.tensor_tensor(o[:, :, 1, :], a[:, :, 0, :], a[:, :, 1, :], ALU.max))
                return to

            state = {"buf": 2, "turns": 0}

            def sort_phase(k):
                buf = state["buf"]
                if k < 11:
                    flip(buf, k, 0)
                    for bit in range(k - 1, -1, -1):
                        buf = exchange(buf, bit)
                else:
                    v.sem_inc(s_turn, 1)
                    state["turns"] += 1
                    v.wait_ge(s_turned, state["turns"])
                    to = 1 if buf != 1 else 0
                    c.done(v.tensor_copy(key[:, to, :], psT[:]))
                    buf = to
                    flip(buf, k, 10)
                    for bit in range(k - 11, -1, -1):
                        buf = exchange(buf, bit)
                    v.sem_inc(s_turn, 1)
                    state["turns"] += 1
                    v.wait_ge(s_turned, state["turns"])
                    c.done(v.tensor_copy(key[:, 1 - buf, :], psT[:]))
                    buf = 1 - buf
                    for bit in range(9, -1, -1):
                        buf = exchange(buf, bit)
                state["buf"] = buf

            def sort_end():
                buf = state["buf"]
                k = key_i[buf]
                d = key_i[1 - buf]
                c.inc(v.tensor_scalar(m.src_sorted[:], k, (1 << KEY_SHIFT) - 1, None, ALU.bitwise_and))
                c.done(v.tensor_scalar(d, k, KEY_SHIFT, (1 << KEY_SHIFT) - 1, ALU.logical_shift_right,
                                       ALU.bitwise_and))
                c.inc(v.tensor_copy(m.dst_first[:], d[:, 0:1]))
                c.done(v.tensor_copy(key[:, 2, :], d))
                c.inc(v.tensor_copy(lastd[:, 0:1], key[:, 2, GCOLS - 1:GCOLS]))
                c.done(v.tensor_copy(lastd[:, 1:2], key[:, 2, 0:1]))
                v.sem_inc(s_turn, 1)
                c.inc(v.tensor_tensor(m.seg_keep[:, 1:GCOLS], key[:, 2, 1:GCOLS], key[:, 2, 0:GCOLS - 1],
                                      ALU.is_equal))
                c.inc(v.memset(m.seg_keep[:, 0:1], 1.0))
                v.wait_ge(s_s, c.n)
                c.done(v.tensor_reduce(m.link[:, 1:2], m.seg_keep[:], AX_X, ALU.min))
                v.wait_ge(s_turned, state["turns"] + 1)
                c.done(v.tensor_tensor(m.link[:, 0:1], psD[:, 0:1], key[:, 2, 0:1], ALU.is_equal))
                c.done(v.memset(m.link[0:1, 0:1], 0.0))

            one_hots(0, 0, first=True)
            one_hots(1, 1, first=True)
            add(0, 0, first=True)
            sort_init()
            for n, a in enumerate(range(1, PHASES + 1)):
                with v.Fori(1 + CUT[n], 1 + CUT[n + 1]) as u:
                    for par in range(2):
                        one_hots(u * 2 + par, par)
                        add(u * 2 + (par - 1), 1 - par)
                sort_phase(a)
            add(STEPS - 1, 1)
            sort_end()
            v.wait_ge(s_acc, STEPS)


def node_update(nc, sem, x, W, b, W_gat, att_src, att_dst, m):
    with ExitStack() as ctx:
        def sb(name, shape, dt):
            return ctx.enter_context(nc.sbuf_tensor(name, shape, dt))

        w_raw = sb("w_raw", [P, HALVES, FEAT], F32)
        w_t = sb("w_t", [P, HALVES, FEAT], F32)
        wg = sb("wg", [P, HALVES, HE], F32)
        brow = sb("brow", [1, FEAT], F32)
        att = sb("att", [P, 2, HE], F32)
        prod = sb("prod", [P, TILES, HE], F32)
        xin = sb("c_xin", [P, 2, CH, FEAT], F32)
        y = sb("c_y", [P, CH, FEAT], F32)
        yt = sb("c_yt", [P, HALVES, CH * P], F32)
        sums = sb("c_sums", [P, 2, FEAT], F32)
        sums_t = sb("c_sums_t", [P, 2, FEAT], F32)
        stats = sb("c_stats", [P, CH, 6], F32)
        mv = sb("c_mv", [P, CH, 2], F32)
        rstd = sb("c_rstd", [P, CH], F32)
        zeros = sb("c_zeros", [P, 512], F32)
        psT = [ctx.enter_context(nc.psum_tensor(f"c_turn{n}", [P, 512], F32)) for n in range(2)]
        psX = [ctx.enter_context(nc.psum_tensor(f"c_out{n}", [P, 512], F32)) for n in range(2)]
        psY = [ctx.enter_context(nc.psum_tensor(f"c_yturn{n}", [P, 512], F32)) for n in range(2)]
        psH = [ctx.enter_context(nc.psum_tensor(f"c_h{n}", [P, 512], F32)) for n in range(2)]

        s_w, s_wt, s_wte = sem("c_weights"), sem("c_w_turned"), sem("c_w_ready")
        s_xin = [sem("c_x0"), sem("c_x1")]
        s_x1o = [sem("c_x1_stored0"), sem("c_x1_stored1")]
        s_yto = sem("c_yt_stored")
        s_clear = sem("c_cleared")
        s_past = sem("c_past")
        s_stage, s_tt, s_te = sem("c_staged"), sem("c_sums_turned"), sem("c_sums_t_ready")
        s_mm, s_x1 = sem("c_multiplied"), sem("c_x1_ready")
        s_v, s_var, s_std, s_y = sem("c_vector"), sem("c_var"), sem("c_std"), sem("c_y_ready")
        s_yt, s_yte, s_h, s_he = sem("c_y_turned"), sem("c_yt_ready"), sem("c_h_multiplied"), sem("c_h_ready")
        s_z, s_zo, s_fin = sem("c_zero"), sem("c_zero_stored"), sem("c_rows_stored")
        s_row = sem("c_rows_ready")

        x_tiles = x[0:FULL_TILES * P, :].rearrange("(t p) f -> p t f", p=P)
        x1_tiles = m.x1_dram.rearrange("(t p) f -> p t f", p=P)
        block = ctx.enter_context(nc.Block())

        @block.sync
        def _(sp):
            sp.dma_start(w_raw[:], W.rearrange("(o p) i -> p o i", p=P)).then_inc(s_w, 16)
            sp.dma_start(wg[:], W_gat.rearrange("(k p) c -> p k c", p=P)).then_inc(s_w, 16)
            sp.dma_start(brow[:], b.rearrange("(a n) -> a n", a=1)).then_inc(s_w, 16)
            for n, a in enumerate((att_src, att_dst)):
                sp.dma_start(att[:, n, :], a.rearrange("(o h) e -> o (h e)", o=1).to_broadcast([P, HE])
                             ).then_inc(s_w, 16)

            def load(c, k):
                sp.dma_start(xin[:, k, :, :], x_tiles[:, ds(c * CH, CH), :]).then_inc(s_xin[k], 16)

            def store_x1(c, k):
                sp.wait_ge(s_y, c + 1)
                sp.dma_start(x1_tiles[:, ds(c * CH, CH), :], xin[:, k, :, :]).then_inc(s_x1o[k], 16)

            load(0, 0)
            load(1, 1)
            with sp.Fori(1, CHUNKS // 2 - 1) as i:
                for k in range(2):
                    store_x1(i * 2 + (k - 2), k)
                    sp.wait_ge(s_x1o[k], i * 16)
                    load(i * 2 + k, k)
            c = CHUNKS - 2
            store_x1(c - 2, 0)
            sp.wait_ge(s_x1o[0], 16 * (CHUNKS // 2 - 1))
            load(c, 0)
            store_x1(c - 1, 1)
            sp.wait_ge(s_x1o[1], 16 * (CHUNKS // 2 - 1))
            sp.sem_inc(s_clear, 1)
            sp.dma_start(xin[:, 1, 0:CH - 1, :], x_tiles[:, (c + 1) * CH:FULL_TILES, :]).then_inc(s_xin[1], 16)
            sp.wait_ge(s_clear, 2)
            sp.dma_start(xin[0:LAST_ROWS, 1, CH - 1, :], x[FULL_TILES * P:NODES, :]).then_inc(s_xin[1], 16)
            store_x1(c, 0)
            store_x1(c + 1, 1)
            sp.wait_ge(s_row, 2)
            sp.dma_start(m.row_dram.rearrange("(t p) c -> p t c", p=P), m.node_row[:]).then_inc(s_fin, 16)
            sp.dma_start(m.adst_dram.rearrange("(t p) c -> p t c", p=P), m.node_dst[:]).then_inc(s_fin, 16)
            for k in range(2):
                sp.wait_ge(s_x1o[k], 16 * (CHUNKS // 2))
            sp.wait_ge(s_fin, 32)

        @block.gpsimd
        def _(pool):
            pool.memset(zeros[:], 0.0).then_inc(s_z, 1)

            def stage(n, k, first=False):
                if not first:
                    pool.wait_ge(s_tt, n - 1)
                pool.tensor_copy(sums[:, k, :], m.acc[:, ds(n, 1), :]).then_inc(s_stage, 1)

            stage(0, 0, first=True)
            stage(1, 1, first=True)
            with pool.Fori(1, TILES // 2) as i:
                for k in range(2):
                    stage(i * 2 + k, k)

        @block.scalar
        def _(act):
            act.wait_ge(s_z, 1)
            flat = m.adst_first.rearrange("(q p n) c -> q p (n c)", q=8, p=P)
            for q in range(8):
                act.dma_start(flat[q], zeros[:]).then_inc(s_zo, 16)

            act.wait_ge(s_wt, 1)
            act.copy(w_t[:], psT[0][:, :].rearrange("p (k o) -> p k o", k=HALVES)).then_inc(s_wte, 1)

            def sums_out(n, par, first=False):
                act.wait_ge(s_tt, n + 1)
                if not first:
                    act.wait_ge(s_mm, n - 1)
                act.copy(sums_t[:, par, :], psT[par][:, 0:FEAT]).then_inc(s_te, 1)

            def yt_out(c, k, t, first=False):
                n = c * CH + t
                act.wait_ge(s_yt, n + 1)
                if t == 0 and not first:
                    act.wait_ge(s_yto, c * 16)
                act.copy(yt[:, :, t * P:(t + 1) * P],
                         psY[(k * CH + t) % 2][:, 0:FEAT].rearrange("p (k n) -> p k n", k=HALVES)
                         ).then_inc(s_yte, 1)
                if t == CH - 1:
                    act.wait_ge(s_yte, n + 1)
                    act.dma_start(m.yt_dram[:, :, ds(c * (CH * P), CH * P)], yt[:]).then_inc(s_yto, 16)

            def chunk(c, k, first=False):
                for t in range(CH):
                    sums_out(c * CH + t, (k * CH + t) % 2, first=first and t < 2)
                act.wait_ge(s_var, c + 1)
                act.activation(rstd[:], mv[:, :, 1], ACT.Sqrt, bias=m.eps[:, 0:1]).then_inc(s_std, 1)
                for t in range(CH):
                    yt_out(c, k, t, first=first)

            chunk(0, 0, first=True)
            chunk(1, 1)
            with act.Fori(1, CHUNKS // 2) as i:
                for k in range(2):
                    chunk(i * 2 + k, k)
            act.wait_ge(s_yto, 16 * CHUNKS)
            act.wait_ge(s_zo, 16 * 8)

        @block.vector
        def _(v):
            def chunk(c, k, i, last=False, first=False):
                v.wait_ge(s_xin[k], i * 16 + (32 if last else 16))
                for t in range(CH):
                    v.wait_ge(s_mm, c * CH + (t + 1))
                    v.tensor_tensor(xin[:, k, t, :], xin[:, k, t, :], psX[(k * CH + t) % 2][:, 0:FEAT],
                                    ALU.add).then_inc(s_x1, 1)
                v.wait_ge(s_x1, c * CH + CH)
                for t in range(CH):
                    q = v.bn_stats(stats[:, t, :], xin[:, k, t, :])
                q.then_inc(s_v, 1)
                v.wait_ge(s_v, c * 2 + 1)
                v.sem_inc(s_past, 1)
                for t in range(CH):
                    q = v.bn_aggr(mv[:, t, :], stats[:, t, :])
                q.then_inc(s_var, 1)
                v.wait_ge(s_std, c + 1)
                v.reciprocal(rstd[:], rstd[:]).then_inc(s_v, 1)
                v.wait_ge(s_v, c * 2 + 2)
                if not first:
                    v.wait_ge(s_yt, c * CH)
                for t in range(CH):
                    q = v.tensor_scalar(y[:, t, :], xin[:, k, t, :], mv[:, t, 0:1],
                                        rstd[:, t:t + 1], ALU.subtract, ALU.mult)
                q.then_inc(s_y, 1)
                for t in range(CH):
                    v.wait_ge(s_h, c * CH + (t + 1))
                    v.tensor_copy(m.node_row[:, ds(c * CH + t, 1), 0:HE],
                                  psH[(k * CH + t) % 2][:, None, 0:HE]).then_inc(s_he, 1)

            chunk(0, 0, 0, first=True)
            chunk(1, 1, 0)
            with v.Fori(1, CHUNKS // 2 - 1) as i:
                for k in range(2):
                    chunk(i * 2 + k, k, i)
            chunk(CHUNKS - 2, 0, CHUNKS // 2 - 1)
            v.wait_ge(s_clear, 1)
            v.memset(xin[:, 1, CH - 1, :], 0.0).then_inc(s_clear, 1)
            chunk(CHUNKS - 1, 1, CHUNKS // 2 - 1, last=True)
            v.wait_ge(s_he, TILES)
            v.wait_ge(s_w, 16 * 5)
            n = 2 * CHUNKS
            for q, o in enumerate((m.node_row[:, :, HE:ROWF], m.node_dst[:])):
                v.tensor_tensor(prod[:], m.node_row[:, :, 0:HE],
                                att[:, q:q + 1, :].to_broadcast([P, TILES, HE]), ALU.mult).then_inc(s_v, 1)
                n += 1
                v.wait_ge(s_v, n)
                v.tensor_reduce(o, prod[:].rearrange("p t (h e) -> p t h e", e=EXPERTS), AX_X,
                                ALU.add).then_inc(s_v, 1)
                n += 1
                v.wait_ge(s_v, n)
                v.sem_inc(s_row, 1)

        @block.tensor
        def _(pe):
            pe.wait_ge(s_w, 16 * 5)
            for k in range(HALVES):
                for o in range(HALVES):
                    t = pe.transpose(psT[0][:, k * FEAT + o * P:k * FEAT + (o + 1) * P],
                                     w_raw[:, o, k * P:(k + 1) * P], m.ident[:])
            t.then_inc(s_wt, 1)
            pe.wait_ge(s_wte, 1)

            def turn(n, par, first=False):
                pe.wait_ge(s_stage, n + 1)
                if not first:
                    pe.wait_ge(s_te, n - 1)
                for k in range(HALVES):
                    t = pe.transpose(psT[par][:, k * P:(k + 1) * P], sums[:, par, k * P:(k + 1) * P], m.ident[:])
                t.then_inc(s_tt, 1)

            def multiply(n, par, first=False):
                pe.wait_ge(s_te, n + 1)
                if not first:
                    pe.wait_ge(s_x1, n - 1)
                for k in range(HALVES):
                    pe.matmul(psX[par][:, 0:FEAT], sums_t[:, par, k * P:(k + 1) * P], w_t[:, k, :],
                              start=(k == 0), stop=False)
                pe.matmul(psX[par][:, 0:FEAT], m.ones[0:1, :], brow[:], start=False, stop=True).then_inc(s_mm, 1)

            def turn_y(n, t, par, first=False):
                if not first:
                    pe.wait_ge(s_yte, n - 1)
                for k in range(HALVES):
                    q = pe.transpose(psY[par][:, k * P:(k + 1) * P], y[:, t, k * P:(k + 1) * P], m.ident[:])
                q.then_inc(s_yt, 1)

            def h_out(n, t, par, first=False):
                pe.wait_ge(s_yte, n + 1)
                if not first:
                    pe.wait_ge(s_he, n - 1)
                for k in range(HALVES):
                    q = pe.matmul(psH[par][:, 0:HE], yt[:, k, t * P:(t + 1) * P], wg[:, k, :],
                                  start=(k == 0), stop=(k == HALVES - 1))
                q.then_inc(s_h, 1)

            def chunk(c, k, first=False):
                for t in range(CH + 1):
                    if t < CH:
                        turn(c * CH + t, (k * CH + t) % 2, first=first and t < 2)
                    if t >= 1:
                        multiply(c * CH + (t - 1), (k * CH + t - 1) % 2, first=first and t < 3)
                pe.wait_ge(s_y, c + 1)
                for t in range(CH + 1):
                    if t < CH:
                        turn_y(c * CH + t, t, (k * CH + t) % 2, first=first and t < 2)
                    if t >= 1:
                        h_out(c * CH + (t - 1), t - 1, (k * CH + t - 1) % 2, first=first and t < 3)

            chunk(0, 0, first=True)
            chunk(1, 1)
            with pe.Fori(1, CHUNKS // 2) as i:
                for k in range(2):
                    chunk(i * 2 + k, k)


def gather_and_experts(nc, sem, W1, b1, W2, b2, edge_index, m):
    with ExitStack() as ctx:
        def sb(name, shape, dt):
            return ctx.enter_context(nc.sbuf_tensor(name, shape, dt))

        FB = HID // P
        PAIRS = TILES // 2
        N2 = 2 * P
        GB, SLOTS = 16, 4
        BATCHES = GCOLS // GB
        WEIGHT_LOADS = HALVES + FB + 2 * EXPERTS

        w1 = sb("w1", [P, HALVES, EXPERTS, HID], F32)
        w2 = sb("w2", [P, FB, EXPERTS, FEAT], F32)
        b1c = sb("b1c", [P, EXPERTS, FB], F32)
        b2r = sb("b2r", [P, EXPERTS, FEAT], F32)
        yt = sb("d_yt", [P, 2, HALVES, N2], F32)
        hid = sb("hid", [P, 2, FB, N2], F32)
        yo = sb("yo", [P, EXPERTS, 2, FEAT], F32)
        got = sb("got", [P, SLOTS, GB, STATE], F32)
        idx = sb("d_idx", [P, SLOTS, GB], I32)
        lo = sb("lo", [P, GCOLS], BF16)
        hi = sb("hi", [P, GCOLS], BF16)
        hot_lo = sb("hot_lo", [P, HCOLS, P], BF16)
        hot_hi = sb("hot_hi", [P, HCOLS, TILES], BF16)
        di = hot_lo[:].rearrange("p a b -> p (a b)").bitcast(I32)[:, 0:2 * GCOLS].rearrange("p (n j) -> p n j", n=2)
        iota_b = sb("iota_b", [P, P], BF16)
        zero_b = sb("zero_b", [P, P], BF16)
        before = sb("before", [P, P], F32)
        cnt = sb("cnt", [P, TILES], F32)
        tot = sb("tot", [P, TILES], F32)
        pos = sb("pos", [P, 2, TILES], F32)
        sidx = sb("sidx", [P, 2, CH], I32)
        sdat = sb("sdat", [P, 2, CH, HEADS], F32)
        psL = [ctx.enter_context(nc.psum_tensor(f"d_hidden{n}", [P, 2, N2], F32)) for n in range(4)]
        psO = [ctx.enter_context(nc.psum_tensor(f"d_expert{n}", [P, 2, FEAT], F32)) for n in range(2)]
        psC = ctx.enter_context(nc.psum_tensor("counts", [P, 512], F32))
        psD = ctx.enter_context(nc.psum_tensor("d_prefix", [P, 512], F32))

        s_w, s_ei = sem("d_weights"), sem("d_edges")
        s_yt = [sem("d_yt0"), sem("d_yt1")]
        s_l1, s_hid, s_l2, s_yo = sem("d_l1"), sem("d_hidden_ready"), sem("d_l2"), sem("d_out_ready")
        s_st = [sem(f"d_stored{e}") for e in range(EXPERTS)]
        s_pc, s_pi = sem("d_pool_const"), sem("d_idx_ready")
        s_got = [sem(f"d_gathered{k}") for k in range(SLOTS)]
        s_past = sem("d_past")
        s_mv = [sem(f"d_moved{k}") for k in range(SLOTS)]
        s_v, s_hh, s_hm = sem("d_count_vector"), sem("d_hot"), sem("d_hist")
        s_cnt, s_pos = sem("d_counts_read"), sem("d_positions")
        s_sc, s_sd = [sem("d_scattered0"), sem("d_scattered1")], sem("d_scatter_staged")

        block = ctx.enter_context(nc.Block())

        @block.sync
        def _(sp):
            sp.dma_start(di[:, 0, :], edge_index[1, :].rearrange("(p j) -> p j", p=P)).then_inc(s_ei, 16)
            for k in range(HALVES):
                sp.dma_start(w1[:, k, :, :], W1[:, k * P:(k + 1) * P, :].rearrange("e p n -> p e n")).then_inc(s_w, 16)
            for k in range(FB):
                sp.dma_start(w2[:, k, :, :], W2[:, k * P:(k + 1) * P, :].rearrange("e p n -> p e n")).then_inc(s_w, 16)
            for e in range(EXPERTS):
                sp.dma_start(b2r[:, e, :], b2[e:e + 1, :].to_broadcast([P, FEAT])).then_inc(s_w, 16)
            with nc.allow_non_contiguous_dma(reason="a bias of 8 KB, once"):
                for e in range(EXPERTS):
                    sp.dma_start(b1c[:, e, :], b1[e, :].rearrange("(k p) -> p k", p=P)).then_inc(s_w, 16)

            def move(i, k):
                sp.wait_ge(s_got[k], i * (16 * GB) + 16 * GB)
                sp.dma_start(m.states[:, ds(i * (SLOTS * GB) + k * GB, GB), :], got[:, k, :, :]
                             ).then_inc(s_mv[k], 16)

            with sp.Fori(0, BATCHES // SLOTS) as i:
                for k in range(SLOTS):
                    move(i, k)
            for k in range(SLOTS):
                sp.wait_ge(s_mv[k], 16 * (BATCHES // SLOTS))

        @block.gpsimd
        def _(pool):
            c = Count(pool, s_pc)
            c.inc(pool.iota(iota_b[:], pattern=[[1, P]], base=0, channel_multiplier=0,
                            allow_small_or_imprecise_dtypes=True))
            c.inc(pool.memset(zero_b[:], 0.0))
            c.inc(pool.memset(before[:], 1.0))
            c.inc(pool.memset(got[:], 0.0))
            pool.wait_ge(s_pc, c.n)
            c.inc(pool.affine_select(out=before[:], in_=before[:], compare_op=ALU.is_gt, fill=0.0, base=0,
                                     pattern=[[1, P]], channel_multiplier=-1))

            def batch(i, k, first=False):
                if not first:
                    pool.wait_ge(s_mv[k], i * 16)
                pool.tensor_copy(idx[:, k, :], m.src_sorted[:, ds(i * (SLOTS * GB) + k * GB, GB)]
                                 ).then_inc(s_pi, 1)
                pool.wait_ge(s_pi, i * SLOTS + (k + 1))
                pool.sem_inc(s_past, 1)
                for j in range(GB):
                    pool.indirect_dma_start(got[:, k, j, 0:ROWF], None, m.row_dram,
                                            bass.IndirectOffsetOnAxis(ap=idx[:, k, j:j + 1], axis=0)
                                            ).then_inc(s_got[k], 16)

            for k in range(SLOTS):
                batch(0, k, first=True)
            with pool.Fori(1, BATCHES // SLOTS) as i:
                for k in range(SLOTS):
                    batch(i, k)

            pool.wait_ge(s_pos, 1)

            def spread(i, k, first=False):
                if not first:
                    pool.wait_ge(s_sc[k], i * (16 * CH))
                pool.tensor_copy(sidx[:, k, :], m.first_pos[:, ds((i * 2 + k) * CH, CH)])
                pool.tensor_copy(sdat[:, k, :, :], m.node_dst[:, ds((i * 2 + k) * CH, CH), :]).then_inc(s_sd, 1)
                pool.wait_ge(s_sd, i * 2 + (k + 1))
                pool.sem_inc(s_past, 1)
                for j in range(CH):
                    pool.indirect_dma_start(m.adst_first, bass.IndirectOffsetOnAxis(ap=sidx[:, k, j:j + 1], axis=0),
                                            sdat[:, k, j, :], None, bounds_check=GEDGES - 1, oob_is_err=False
                                            ).then_inc(s_sc[k], 16)

            for k in range(2):
                spread(0, k, first=True)
            with pool.Fori(1, CHUNKS // 2) as i:
                for k in range(2):
                    spread(i, k)
            for k in range(2):
                pool.wait_ge(s_sc[k], 16 * CH * (CHUNKS // 2))

        @block.scalar
        def _(act):
            act.wait_ge(s_w, 16 * WEIGHT_LOADS)

            def load(i, k):
                act.dma_start(yt[:, k, :, :], m.yt_dram[:, :, ds(i * N2, N2)]).then_inc(s_yt[k], 16)

            def hidden(n, e, first=False):
                for q in range(2):
                    act.wait_ge(s_l1, n * 2 + (q + 1))
                    if q == 0 and not first:
                        act.wait_ge(s_l2, n - 1)
                    for f in range(2):
                        t = act.activation(hid[:, e % 2, 2 * q + f, :], psL[(e % 2) * 2 + q][:, f, :], ACT.Gelu,
                                           bias=b1c[:, e, 2 * q + f:2 * q + f + 1])
                    t.then_inc(s_hid, 1)

            def store(n, e, i):
                act.wait_ge(s_yo, n + 1)
                act.dma_start(m.y_dram.rearrange("(t p) e f -> p t e f", p=P)[:, ds(i * 2, 2), e, :], yo[:, e, :, :]
                              ).then_inc(s_st[e], 16)

            def pair(i, k, first=False, last=False):
                for e in range(EXPERTS):
                    hidden(i * EXPERTS + e, e, first=first and e < 2)
                    if e == 0 and not last:
                        load(i + 1, 1 - k)
                    if e >= 1:
                        store(i * EXPERTS + (e - 1), e - 1, i)
                    elif not first:
                        store(i * EXPERTS - 1, EXPERTS - 1, i - 1)

            load(0, 0)
            pair(0, 0, first=True)
            with act.Fori(0, PAIRS // 2 - 1) as u:
                for k in range(2):
                    pair(u * 2 + (k + 1), (k + 1) % 2)
            pair(PAIRS - 2, 1)
            pair(PAIRS - 1, 0, last=True)
            store(PAIRS * EXPERTS - 1, EXPERTS - 1, PAIRS - 1)
            for e in range(EXPERTS):
                act.wait_ge(s_st[e], 16 * PAIRS)

        HLOOP = HPIECES // 2

        @block.tensor
        def _(pe):
            pe.wait_ge(s_pc, 5)
            pe.wait_ge(s_w, 16 * WEIGHT_LOADS)
            pe.matmul(psC[:, 0:TILES], zero_b[:], zero_b[:, 0:TILES], start=True, stop=False)

            def layer1(i, k, n, e, first=False):
                if e == 0:
                    pe.wait_ge(s_yt[k], (i // 2) * 16 + 16 if isinstance(i, int) else i * 8 + 16 - 8 * k)
                for q in range(2):
                    if not first:
                        pe.wait_ge(s_hid, n * 2 + (q - 3))
                    for f in range(2):
                        for h in range(HALVES):
                            t = pe.matmul(psL[(e % 2) * 2 + q][:, f, :],
                                          w1[:, h, e, (2 * q + f) * P:(2 * q + f + 1) * P], yt[:, k, h, :],
                                          start=(h == 0), stop=(h == HALVES - 1))
                    t.then_inc(s_l1, 1)

            def layer2(n, e, first=False):
                pe.wait_ge(s_hid, n * 2 + 2)
                if not first:
                    pe.wait_ge(s_yo, n - 1)
                for t in range(2):
                    for f in range(FB):
                        q = pe.matmul(psO[e % 2][:, t, :], hid[:, e % 2, f, t * P:(t + 1) * P], w2[:, f, e, :],
                                      start=(f == 0), stop=(f == FB - 1))
                q.then_inc(s_l2, 1)

            def pair(i, k, first=False):
                for e in range(EXPERTS):
                    layer1(i, k, i * EXPERTS + e, e, first=first and e < 2)
                    if e >= 1:
                        layer2(i * EXPERTS + (e - 1), e - 1, first=first and e < 3)
                    elif not first:
                        layer2(i * EXPERTS - 1, EXPERTS - 1)

            def count(q):
                pe.wait_ge(s_hh, q + 1)
                for j in range(HCOLS):
                    t = pe.matmul(psC[:, 0:TILES], hot_lo[:, j, :], hot_hi[:, j, :], start=False, stop=False)
                t.then_inc(s_hm, 1)

            pair(0, 0, first=True)
            with pe.Fori(0, HLOOP) as u:
                for k in range(2):
                    count(u * 2 + k)
                    pair(u * 2 + (k + 1), (k + 1) % 2)
            pe.matmul(psC[:, 0:TILES], zero_b[:], zero_b[:, 0:TILES], start=False, stop=True).then_inc(s_hm, 1)
            pe.wait_ge(s_cnt, 1)
            pe.matmul(psD[:, 0:TILES], m.ones[:], cnt[:], start=True, stop=True)
            pe.matmul(psD[:, P:P + TILES], before[:], cnt[:], start=True, stop=True).then_inc(s_hm, 1)
            with pe.Fori(HLOOP, (PAIRS - 1) // 2) as u:
                for k in range(2):
                    pair(u * 2 + (k + 1), (k + 1) % 2)
            layer2(PAIRS * EXPERTS - 1, EXPERTS - 1)

        @block.vector
        def _(v):
            c = Count(v, s_v)
            v.wait_ge(s_ei, 16)
            c.done(v.tensor_scalar(di[:, 1, :], di[:, 0, :], P - 1, None, ALU.bitwise_and))
            c.done(v.tensor_copy(lo[:], di[:, 1, :]))
            c.done(v.tensor_scalar(di[:, 1, :], di[:, 0, :], 7, None, ALU.arith_shift_right))
            c.done(v.tensor_copy(hi[:], di[:, 1, :]))
            v.wait_ge(s_pc, 5)
            v.wait_ge(s_w, 16 * WEIGHT_LOADS)

            def hots(q, first=False):
                if not first:
                    v.wait_ge(s_hm, q)
                for part, wide, t in ((lo, P, hot_lo), (hi, TILES, hot_hi)):
                    o = v.tensor_tensor(t[:], iota_b[:, None, 0:wide].to_broadcast([P, HCOLS, wide]),
                                        part[:, ds(q * HCOLS, HCOLS)][:, :, None].to_broadcast([P, HCOLS, wide]),
                                        ALU.is_equal)
                o.then_inc(s_hh, 1)

            def outs(n, e, i, first=False):
                v.wait_ge(s_l2, n + 1)
                if not first:
                    v.wait_ge(s_st[e], i * 16)
                v.tensor_tensor(yo[:, e, :, :], psO[e % 2][:], b2r[:, e:e + 1, :].to_broadcast([P, 2, FEAT]),
                                ALU.add).then_inc(s_yo, 1)

            def pair(i, first=False):
                for e in range(EXPERTS):
                    outs(i * EXPERTS + e, e, i, first=first)

            hots(0, first=True)
            pair(0, first=True)
            with v.Fori(0, HLOOP - 1) as u:
                for k in range(2):
                    hots(u * 2 + (k + 1))
                    pair(u * 2 + (k + 1))
            hots(HPIECES - 1)
            pair(HPIECES - 1)
            for e in range(EXPERTS - 1):
                outs(HPIECES * EXPERTS + e, e, HPIECES)
            v.wait_ge(s_hm, HPIECES + 1)
            c.done(v.tensor_copy(cnt[:], psC[:, 0:TILES]))
            v.sem_inc(s_cnt, 1)
            v.wait_ge(s_hm, HPIECES + 2)
            c.done(v.tensor_copy(tot[:], psD[:, 0:TILES]))
            c.done(v.tensor_tensor_scan(pos[:, 0, :], m.ones[:, 0:TILES], tot[:], 0.0, ALU.mult, ALU.add))
            c.done(v.tensor_tensor(pos[:, 0, :], pos[:, 0, :], tot[:], ALU.subtract))
            c.done(v.tensor_tensor(pos[:, 0, :], pos[:, 0, :], psD[:, P:P + TILES], ALU.add))
            c.inc(v.tensor_scalar(m.has_edges[:], cnt[:], 0.5, None, ALU.is_gt))
            c.done(v.tensor_tensor(pos[:, 1, :], pos[:, 0, :], cnt[:], ALU.add))
            c.done(v.tensor_scalar(cnt[:], m.has_edges[:], -4.0 * GEDGES, 4.0 * GEDGES, ALU.mult, ALU.add))
            c.inc(v.tensor_tensor(m.first_pos[:], pos[:, 0, :], cnt[:], ALU.add))
            c.done(v.scalar_tensor_tensor(m.last_pos[:], pos[:, 1, :], -1.0, cnt[:], ALU.add, ALU.add))
            v.sem_inc(s_pos, 1)
            outs(HPIECES * EXPERTS + EXPERTS - 1, EXPERTS - 1, HPIECES)
            with v.Fori(HPIECES + 1, PAIRS) as i:
                pair(i)


def segment_softmax(nc, sem, m):
    with ExitStack() as ctx:
        def sb(name, shape, dt=F32):
            return ctx.enter_context(nc.sbuf_tensor(name, shape, dt))

        adst = sb("adst", [P, GCOLS, HEADS])
        adfirst = sb("adfirst", [P, HEADS])
        e = sb("e", [P, HEADS, GCOLS])
        decay = sb("decay", [P, HEADS, GCOLS])
        limit = sb("limit", [P, GCOLS])
        tail = sb("tail", [P, 2, ROWF])
        tail_t = sb("tail_t", [ROWF, 2, P])
        carried = sb("carried", [ROWF, P + 1])
        cin = sb("cin", [P, 2, ROWF])
        whole = sb("whole", [P, 1])
        psT = ctx.enter_context(nc.psum_tensor("e_turn", [P, 512], F32))
        psB = ctx.enter_context(nc.psum_tensor("e_back", [P, 512], F32))

        s_ad, s_af = sem("e_adst"), sem("e_adst_first")
        s_v, s_t, s_a, s_ask, s_go = sem("e_vector"), sem("e_turned"), sem("e_scalar"), sem("e_ask_pe"), sem("e_ask_act")
        s_st = sem("e_stored")
        s_fin = sem("e_states_ready")
        states = m.states
        mx = states[:, :, ROWF:STATE]
        by_head = lambda a: a.rearrange("p j h -> p h j")

        block = ctx.enter_context(nc.Block())

        @block.sync
        def _(sp):
            sp.dma_start(adst[:], m.adst_first.rearrange("(p j) h -> p j h", p=P)).then_inc(s_ad, 16)
            sp.wait_ge(s_fin, 1)
            sp.dma_start(m.state_dram.rearrange("(p j) c -> p j c", p=P), states[:]).then_inc(s_st, 16)
            sp.wait_ge(s_st, 16)

        @block.gpsimd
        def _(pool):
            pool.indirect_dma_start(adfirst[:], None, m.adst_dram,
                                    bass.IndirectOffsetOnAxis(ap=m.dst_first[:], axis=0)).then_inc(s_af, 16)

        @block.scalar
        def _(act):
            act.wait_ge(s_go, 1)
            act.activation(decay[:], decay[:], ACT.Exp).then_inc(s_a, 1)
            act.activation(by_head(states[:, :, HE:ROWF]), e[:], ACT.Exp).then_inc(s_a, 1)
            act.wait_ge(s_go, 2)
            act.activation(tail[:, 1, 0:HEADS], tail[:, 1, 0:HEADS], ACT.Exp).then_inc(s_a, 1)

        @block.tensor
        def _(pe):
            for n, w in enumerate((HEADS, ROWF)):
                pe.wait_ge(s_ask, 2 * n + 1)
                for k in range(2):
                    t = pe.transpose(psT[0:w, k * P:(k + 1) * P], tail[:, k, 0:w], m.ident[:])
                t.then_inc(s_t, 1)
                pe.wait_ge(s_ask, 2 * n + 2)
                pe.transpose(psB[:, 0:w], carried[0:w, 0:P], m.ident[0:w, 0:w]).then_inc(s_t, 1)

        @block.vector
        def _(v):
            c = Count(v, s_v)

            def carry(n, w, start, op0, op1):
                v.sem_inc(s_ask, 1)
                v.wait_ge(s_t, 2 * n + 1)
                c.done(v.tensor_copy(tail_t[0:w, :, :], psT[0:w, 0:2 * P].rearrange("p (k n) -> p k n", k=2)))
                c.inc(v.memset(carried[0:w, 0:1], start))
                c.done(v.tensor_tensor_scan(carried[0:w, 1:P + 1], tail_t[0:w, 1, :], tail_t[0:w, 0, :], start,
                                            op0, op1))
                v.sem_inc(s_ask, 1)
                v.wait_ge(s_t, 2 * n + 2)
                c.done(v.tensor_copy(cin[:, n, 0:w], psB[:, 0:w]))

            v.wait_ge(s_ad, 16)
            v.wait_ge(s_af, 16)
            c.inc(v.memset(m.seg_keep[:, 0:1], 0.0))
            c.inc(v.tensor_copy(adst[:, 0, :], adfirst[:]))
            c.done(v.tensor_tensor(whole[:], m.link[:, 0:1], m.link[:, 1:2], ALU.mult))
            for h in range(HEADS):
                c.inc(v.tensor_tensor_scan(adst[:, :, h], m.seg_keep[:], adst[:, :, h], 0.0, ALU.mult, ALU.add))
            c.inc(v.tensor_scalar(limit[:], m.seg_keep[:], 2 * BIG, -BIG, ALU.mult, ALU.add))
            v.wait_ge(s_v, c.n)
            c.done(v.tensor_tensor(e[:], by_head(states[:, :, HE:ROWF]), by_head(adst[:]), ALU.add))
            c.done(v.scalar_tensor_tensor(e[:], e[:], SLOPE, e[:], ALU.mult, ALU.max))
            for h in range(HEADS):
                c.inc(v.tensor_tensor_scan(mx[:, :, h], limit[:], e[:, h, :], -BIG, ALU.min, ALU.max))
            v.wait_ge(s_v, c.n)
            c.inc(v.tensor_copy(tail[:, 0, 0:HEADS], mx[:, GCOLS - 1, :]))
            c.inc(v.tensor_scalar(tail[:, 1, 0:HEADS], whole[:].to_broadcast([P, HEADS]), 2 * BIG, -BIG,
                                  ALU.mult, ALU.add))
            c.inc(v.tensor_scalar(limit[:, 0:1], m.link[:, 0:1], 2 * BIG, -BIG, ALU.mult, ALU.add))
            c.done(v.tensor_copy(m.seg_keep[:, 0:1], m.link[:, 0:1]))
            carry(0, HEADS, -BIG, ALU.min, ALU.max)
            for h in range(HEADS):
                c.inc(v.tensor_tensor_scan(mx[:, :, h], limit[:], e[:, h, :], cin[:, 0, h:h + 1], ALU.min, ALU.max))
            v.wait_ge(s_v, c.n)
            c.inc(v.tensor_tensor(decay[:, :, 1:GCOLS], by_head(mx[:, 0:GCOLS - 1, :]), by_head(mx[:, 1:GCOLS, :]),
                                  ALU.subtract))
            c.inc(v.tensor_tensor(decay[:, :, 0], cin[:, 0, 0:HEADS], mx[:, 0, :], ALU.subtract))
            c.inc(v.tensor_tensor(e[:], e[:], by_head(mx), ALU.subtract))
            c.inc(v.tensor_tensor(tail[:, 1, 0:HEADS], cin[:, 0, 0:HEADS], mx[:, GCOLS - 1, :], ALU.subtract))
            v.wait_ge(s_v, c.n)
            c.inc(v.tensor_scalar(tail[:, 1, 0:HEADS], tail[:, 1, 0:HEADS], 0.0, None, ALU.min))
            c.done(v.tensor_scalar(decay[:], decay[:], 0.0, None, ALU.min))
            v.sem_inc(s_go, 1)
            v.sem_inc(s_go, 1)
            v.wait_ge(s_a, 1)
            c.inc(v.tensor_tensor(decay[:], decay[:], m.seg_keep[:, None, :].to_broadcast([P, HEADS, GCOLS]),
                                  ALU.mult))
            v.wait_ge(s_a, 2)
            msg = states[:, :, 0:HE].rearrange("p j (h x) -> p j h x", x=EXPERTS)
            c.done(v.tensor_tensor(msg, msg, states[:, :, HE:ROWF][:, :, :, None].to_broadcast(
                [P, GCOLS, HEADS, EXPERTS]), ALU.mult))
            head = [ch // EXPERTS if ch < HE else ch - HE for ch in range(ROWF)]
            for q in range(ROWF // HEADS):
                for k in range(HEADS):
                    ch = q * HEADS + k
                    c.inc(v.tensor_tensor_scan(e[:, k, :], decay[:, head[ch], :], states[:, :, ch], 0.0,
                                               ALU.mult, ALU.add))
                v.wait_ge(s_v, c.n)
                c.done(v.tensor_copy(tail[:, 0, q * HEADS:(q + 1) * HEADS], e[:, :, GCOLS - 1]))
            v.wait_ge(s_a, 3)
            c.done(v.tensor_scalar(cin[:, 1, 0:HEADS], tail[:, 1, 0:HEADS], whole[:, 0:1], None, ALU.mult))
            c.inc(v.tensor_copy(tail[:, 1, 0:HE].rearrange("p (h x) -> p h x", x=EXPERTS),
                                cin[:, 1, 0:HEADS][:, :, None].to_broadcast([P, HEADS, EXPERTS])))
            c.done(v.tensor_copy(tail[:, 1, HE:ROWF], cin[:, 1, 0:HEADS]))
            carry(1, ROWF, 0.0, ALU.mult, ALU.add)
            for ch in range(ROWF):
                c.inc(v.tensor_tensor_scan(states[:, :, ch], decay[:, head[ch], :], states[:, :, ch],
                                           cin[:, 1, ch:ch + 1], ALU.mult, ALU.add))
            v.wait_ge(s_v, c.n)
            v.sem_inc(s_fin, 1)


def combine(nc, sem, b_gat, gamma, beta, out, m):
    with ExitStack() as ctx:
        def sb(name, shape, dt=F32):
            return ctx.enter_context(nc.sbuf_tensor(name, shape, dt))

        T = TILES
        SLOTS = 7
        PAIRS = T // 2
        ROUNDS = PAIRS // SLOTS
        assert PAIRS % SLOTS == 0
        got = sb("f_got", [P, 2, CH, STATE])
        idx = sb("f_idx", [P, 2, CH], I32)
        ns = sb("ns", [P, T, STATE])
        mxm = sb("mxm", [P, T, HEADS])
        e0 = sb("e0", [P, T, HEADS])
        top_ = sb("top_", [P, T, HEADS])
        w1 = sb("f_w1", [P, T, HEADS])
        w0 = sb("f_w0", [P, T, HEADS])
        den = sb("den", [P, T, HEADS])
        num = sb("num", [P, T, HE])
        tmp = sb("f_tmp", [P, T, HE])
        vec = sb("vec", [P, 3, HE])
        one = sb("one", [P, 4, T])
        sc = sb("sc", [P, T, EXPERTS])
        rank = sb("rank", [P, T, EXPERTS])
        ge = sb("f_ge", [P, T, EXPERTS])
        ys = sb("ys", [P, SLOTS, 2, EXPERTS, FEAT])
        xs = sb("xs", [P, SLOTS, 2, FEAT])

        s_c, s_i = sem("f_const"), sem("f_idx_ready")
        s_got = [sem("f_gathered0"), sem("f_gathered1")]
        s_past = sem("f_past")
        s_ns, s_mv = sem("f_states_ready"), sem("f_moved")
        s_v, s_go, s_a = sem("f_vector"), sem("f_ask_act"), sem("f_act")
        s_in = [sem(f"f_loaded{k}") for k in range(SLOTS)]
        s_out = [sem(f"f_stored{k}") for k in range(SLOTS)]
        s_g, s_sum, s_done = sem("f_gates"), sem("f_summing"), sem("f_pair_done")

        y_t = m.y_dram.rearrange("(t p) e f -> p t e f", p=P)
        x1_t = m.x1_dram.rearrange("(t p) f -> p t f", p=P)
        out_t = out[0:FULL_TILES * P, :].rearrange("(t p) f -> p t f", p=P)
        block = ctx.enter_context(nc.Block())

        @block.sync
        def _(sp):
            for n, a in enumerate((b_gat, gamma, beta)):
                sp.dma_start(vec[:, n, :], a.rearrange("(o c) -> o c", o=1).to_broadcast([P, HE])).then_inc(s_c, 16)

            def load(i, k):
                sp.dma_start(ys[:, k, :, :, :], y_t[:, ds(i * (2 * SLOTS) + 2 * k, 2), :, :]).then_inc(s_in[k], 16)
                sp.dma_start(xs[:, k, :, :], x1_t[:, ds(i * (2 * SLOTS) + 2 * k, 2), :]).then_inc(s_in[k], 16)

            for k in range(SLOTS):
                load(0, k)
            with sp.Fori(1, ROUNDS) as i:
                for k in range(SLOTS):
                    sp.wait_ge(s_out[k], i * 16)
                    load(i, k)

        @block.gpsimd
        def _(pool):
            pool.memset(got[:], 0.0).then_inc(s_i, 1)
            pool.wait_ge(s_i, 1)

            def fetch(i, k):
                pool.tensor_copy(idx[:, k, :], m.last_pos[:, ds((i * 2 + k) * CH, CH)]).then_inc(s_i, 1)
                pool.wait_ge(s_i, i * 2 + (k + 2))
                pool.sem_inc(s_past, 1)
                for j in range(CH):
                    pool.indirect_dma_start(got[:, k, j, :], None, m.state_dram,
                                            bass.IndirectOffsetOnAxis(ap=idx[:, k, j:j + 1], axis=0),
                                            bounds_check=GEDGES - 1, oob_is_err=False).then_inc(s_got[k], 16)

            def move(i, k):
                pool.wait_ge(s_got[k], i * (16 * CH) + 16 * CH)
                pool.tensor_copy(ns[:, ds((i * 2 + k) * CH, CH), :], got[:, k, :, :]).then_inc(s_mv, 1)
                pool.wait_ge(s_mv, i * 2 + (k + 1))
                pool.sem_inc(s_past, 1)

            fetch(0, 0)
            with pool.Fori(0, CHUNKS // 2 - 1) as i:
                fetch(i, 1)
                move(i, 0)
                fetch(i + 1, 0)
                move(i, 1)
            fetch(CHUNKS // 2 - 1, 1)
            move(CHUNKS // 2 - 1, 0)
            move(CHUNKS // 2 - 1, 1)
            pool.sem_inc(s_ns, 1)

        @block.scalar
        def _(act):
            act.wait_ge(s_go, 1)
            act.activation(w1[:], w1[:], ACT.Exp).then_inc(s_a, 1)
            act.activation(w0[:], w0[:], ACT.Exp).then_inc(s_a, 1)
            act.wait_ge(s_go, 2)
            act.activation(one[:, 1, :], one[:, 1, :], ACT.Sqrt, bias=m.eps[:, 0:1]).then_inc(s_a, 1)
            act.wait_ge(s_go, 3)
            act.activation(ge[:], ge[:], ACT.Exp).then_inc(s_a, 1)

            def store(i, k):
                act.wait_ge(s_done, i * SLOTS + (k + 1))
                act.dma_start(out_t[:, ds(i * (2 * SLOTS) + 2 * k, 2), :], xs[:, k, :, :]).then_inc(s_out[k], 16)

            with act.Fori(0, ROUNDS - 1) as i:
                for k in range(SLOTS):
                    store(i, k)
            for k in range(SLOTS - 1):
                store(ROUNDS - 1, k)
            k = SLOTS - 1
            act.wait_ge(s_done, PAIRS)
            act.dma_start(out_t[:, T - 2, :], xs[:, k, 0, :]).then_inc(s_out[k], 16)
            act.dma_start(out[FULL_TILES * P:NODES, :], xs[0:LAST_ROWS, k, 1, :]).then_inc(s_out[k], 16)
            for k in range(SLOTS):
                act.wait_ge(s_out[k], 16 * (ROUNDS + (k == SLOTS - 1)))

        @block.vector
        def _(v):
            c = Count(v, s_v)
            heads4 = lambda a: a[:, :, :, None].to_broadcast([P, T, HEADS, EXPERTS])
            wide = lambda a: a.rearrange("p t (h x) -> p t h x", x=EXPERTS)
            per16 = lambda a: a[:, :, None].to_broadcast([P, T, HE])
            row = lambda n: vec[:, n:n + 1, :].to_broadcast([P, T, HE])
            has4 = m.has_edges[:, :, None].to_broadcast([P, T, HEADS])

            c.done(v.tensor_tensor(e0[:], m.node_row[:, :, HE:ROWF], m.node_dst[:], ALU.add))
            c.done(v.scalar_tensor_tensor(e0[:], e0[:], SLOPE, e0[:], ALU.mult, ALU.max))
            c.done(v.tensor_scalar(one[:, 0, :], m.has_edges[:], BIG, -BIG, ALU.mult, ALU.add))
            v.wait_ge(s_ns, 1)
            c.done(v.tensor_tensor(mxm[:], ns[:, :, ROWF:STATE], has4, ALU.mult))
            c.done(v.tensor_tensor(mxm[:], mxm[:], one[:, 0, :][:, :, None].to_broadcast([P, T, HEADS]), ALU.add))
            c.done(v.tensor_tensor(top_[:], mxm[:], e0[:], ALU.max))
            c.inc(v.tensor_tensor(w1[:], mxm[:], top_[:], ALU.subtract))
            c.done(v.tensor_tensor(w0[:], e0[:], top_[:], ALU.subtract))
            v.sem_inc(s_go, 1)
            v.wait_ge(s_a, 2)
            c.done(v.tensor_tensor(w1[:], w1[:], has4, ALU.mult))
            c.inc(v.tensor_tensor(wide(num[:]), wide(ns[:, :, 0:HE]), heads4(w1[:]), ALU.mult))
            c.inc(v.tensor_tensor(wide(tmp[:]), wide(m.node_row[:, :, 0:HE]), heads4(w0[:]), ALU.mult))
            c.done(v.tensor_tensor(den[:], ns[:, :, HE:ROWF], w1[:], ALU.mult))
            c.inc(v.tensor_tensor(num[:], num[:], tmp[:], ALU.add))
            c.done(v.tensor_tensor(den[:], den[:], w0[:], ALU.add))
            c.done(v.tensor_scalar(den[:], den[:], 1e-16, None, ALU.add))
            c.done(v.reciprocal(den[:], den[:]))
            c.done(v.tensor_tensor(wide(num[:]), wide(num[:]), heads4(den[:]), ALU.mult))
            v.wait_ge(s_c, 48)
            c.done(v.tensor_tensor(num[:], num[:], row(0), ALU.add))
            c.done(v.tensor_reduce(one[:, 0, :], num[:], AX_X, ALU.add))
            c.done(v.tensor_scalar(one[:, 0, :], one[:, 0, :], 1.0 / HE, None, ALU.mult))
            c.done(v.tensor_tensor(num[:], num[:], per16(one[:, 0, :]), ALU.subtract))
            c.done(v.tensor_tensor(tmp[:], num[:], num[:], ALU.mult))
            c.done(v.tensor_reduce(one[:, 1, :], tmp[:], AX_X, ALU.add))
            c.done(v.tensor_scalar(one[:, 1, :], one[:, 1, :], 1.0 / HE, None, ALU.mult))
            v.sem_inc(s_go, 1)
            v.wait_ge(s_a, 3)
            c.done(v.reciprocal(one[:, 1, :], one[:, 1, :]))
            c.done(v.tensor_tensor(num[:], num[:], per16(one[:, 1, :]), ALU.mult))
            c.done(v.tensor_tensor(num[:], num[:], row(1), ALU.mult))
            c.done(v.tensor_tensor(num[:], num[:], row(2), ALU.add))
            c.done(v.tensor_reduce(sc[:], num[:].rearrange("p t (h x) -> p t x h", x=EXPERTS), AX_X, ALU.add))
            c.done(v.tensor_scalar(sc[:], sc[:], 1.0 / HEADS, None, ALU.mult))
            c.done(v.memset(rank[:], 0.0))
            for a in range(EXPERTS - 1):
                n = EXPERTS - 1 - a
                c.done(v.tensor_tensor(ge[:, :, 0:n], sc[:, :, a:a + 1].to_broadcast([P, T, n]), sc[:, :, a + 1:EXPERTS],
                                       ALU.is_ge))
                c.inc(v.tensor_reduce(one[:, 2, :], ge[:, :, 0:n], AX_X, ALU.add))
                c.done(v.tensor_tensor(rank[:, :, a + 1:EXPERTS], rank[:, :, a + 1:EXPERTS], ge[:, :, 0:n], ALU.add))
                c.done(v.tensor_scalar(one[:, 2, :], one[:, 2, :], -1.0, float(n), ALU.mult, ALU.add))
                c.done(v.tensor_tensor(rank[:, :, a], rank[:, :, a], one[:, 2, :], ALU.add))
            c.done(v.tensor_scalar(rank[:], rank[:], 1.5, None, ALU.is_lt))
            c.done(v.tensor_reduce(one[:, 3, :], sc[:], AX_X, ALU.max))
            c.done(v.tensor_tensor(ge[:], sc[:], one[:, 3, :][:, :, None].to_broadcast([P, T, EXPERTS]), ALU.subtract))
            v.sem_inc(s_go, 1)
            v.wait_ge(s_a, 4)
            c.done(v.tensor_tensor(ge[:], ge[:], rank[:], ALU.mult))
            c.done(v.tensor_reduce(one[:, 3, :], ge[:], AX_X, ALU.add))
            c.done(v.reciprocal(one[:, 3, :], one[:, 3, :]))
            c.done(v.tensor_tensor(sc[:], ge[:], one[:, 3, :][:, :, None].to_broadcast([P, T, EXPERTS]), ALU.mult))
            base = c.n

            def pair(i, k):
                v.wait_ge(s_in[k], i * 32 + 32)
                for e in range(EXPERTS):
                    for t in range(2):
                        q = v.scalar_tensor_tensor(xs[:, k, t, :], ys[:, k, t, e, :],
                                                   sc[:, ds(i * (2 * SLOTS) + (2 * k + t), 1), e],
                                                   xs[:, k, t, :], ALU.mult, ALU.add)
                    if e < EXPERTS - 1:
                        q.then_inc(s_v, 1)
                        v.wait_ge(s_v, (i * SLOTS + k) * (EXPERTS - 1) + (base + e + 1))
                q.then_inc(s_done, 1)

            with v.Fori(0, ROUNDS) as i:
                for k in range(SLOTS):
                    pair(i, k)


_INS = ["x", "src", "dst", "edge_weight", "L0_gnn_W", "L0_gnn_b", "L0_ffn_W_gat", "L0_ffn_att_src",
        "L0_ffn_att_dst", "L0_ffn_b_gat", "L0_ffn_ln_gamma", "L0_ffn_ln_beta", "L0_ffn_W1", "L0_ffn_b1",
        "L0_ffn_W2", "L0_ffn_b2", "L0_ffn_edge_index"]


def kernel(**inputs):
    import numpy as _np
    import concourse.bacc as _bacc
    from concourse import mybir as _mybir
    from concourse.bass_utils import run_bass_kernel_spmd as _run

    nc = _bacc.Bacc("TRN2", target_bir_lowering=False, num_devices=1)
    arrays, args = {}, []
    for name in _INS:
        a = _np.ascontiguousarray(inputs[name])
        arrays[f"in_{name}"] = a
        args.append(nc.dram_tensor(f"in_{name}", a.shape, _mybir.dt.from_np(a.dtype), kind="ExternalInput").ap())
    out = nc.dram_tensor("out_0", (NODES, FEAT), F32, kind="ExternalOutput").ap()
    build(nc, *args, out)
    r = _run(nc, [arrays], core_ids=[0])
    return r.results[0]["out_0"]
```

```python
from contextlib import ExitStack

import concourse.bass as bass
from concourse import mybir

F32 = mybir.dt.float32
BF16 = mybir.dt.bfloat16
I32 = mybir.dt.int32
ALU = mybir.AluOpType
ACT = mybir.ActivationFunctionType
AX_X = mybir.AxisListType.X
ds = bass.ds

P = 128
NODES = 12500
FEAT = 256
TILES = -(-NODES // P)
NPAD = TILES * P
FULL_TILES = NODES // P
LAST_ROWS = NODES - FULL_TILES * P
CH = 7
CHUNKS = TILES // CH
LN_EPS = 1e-5

EDGES = 200000
ETILES = -(-EDGES // P)
GT = 4
GROUPS = -(-ETILES // GT)
EBLOCKS = -(-ETILES // P)
ECOLS = EBLOCKS * P
STEPS = GROUPS + TILES - 1
RING = 8
HALVES = FEAT // P

GEDGES = 131072
GCOLS = GEDGES // P
KEY_SHIFT = 14
KEY_TOP = 1 << 28
HCOLS = 32
HPIECES = GCOLS // HCOLS

HEADS, EXPERTS = 4, 4
HID = 2 * FEAT
HE = HEADS * EXPERTS
ROWF = HE + HEADS
STATE = HE + 2 * HEADS
BIG = 1.5e38
SLOPE = 0.2


class Shared:
    pass


class Count:

    def __init__(self, eng, sem, start=0):
        self.eng, self.sem, self.n = eng, sem, start

    def inc(self, ins):
        self.n += 1
        return ins.then_inc(self.sem, 1)

    def done(self, ins):
        self.inc(ins)
        self.eng.wait_ge(self.sem, self.n)


def build(nc, x, src, dst, edge_weight, W, b, W_gat, att_src, att_dst, b_gat, gamma, beta,
          W1, b1, W2, b2, edge_index, out):
    m = Shared()

    def dram(name, shape):
        return nc.dram_tensor(name, shape, F32).ap()

    feats = dram("feats", (NPAD, FEAT))
    m.x1_dram = dram("x1_dram", (NPAD, FEAT))
    m.y_dram = dram("y_dram", (NPAD, EXPERTS, FEAT))
    m.row_dram = dram("row_dram", (NPAD, ROWF))
    m.adst_dram = dram("adst_dram", (NPAD, HEADS))
    m.adst_first = dram("adst_first", (GEDGES, HEADS))
    m.state_dram = dram("state_dram", (GEDGES, STATE))

    with ExitStack() as top:
        def sem(name):
            return top.enter_context(nc.semaphore(name))

        def keep(name, shape, dt=F32):
            return top.enter_context(nc.sbuf_tensor(name, shape, dt))

        m.ident = keep("ident", [P, P])
        m.ones = keep("ones", [P, P])
        m.iota = keep("iota", [P, P])
        m.eps = keep("eps", [P, 1])
        m.src_sorted = keep("src_sorted", [P, GCOLS], I32)
        m.seg_keep = keep("seg_keep", [P, GCOLS])
        m.dst_first = keep("dst_first", [P, 1], I32)
        m.link = keep("link", [P, 2])
        m.first_pos = keep("first_pos", [P, TILES], I32)
        m.last_pos = keep("last_pos", [P, TILES], I32)
        m.has_edges = keep("has_edges", [P, TILES])
        m.node_row = keep("node_row", [P, TILES, ROWF])
        m.node_dst = keep("node_dst", [P, TILES, HEADS])
        m.mean = keep("mean", [P, TILES])
        m.rstd = keep("rstd_all", [P, TILES])

        with ExitStack() as part1:
            def sb(name, shape, dt=F32):
                return part1.enter_context(nc.sbuf_tensor(name, shape, dt))

            m.dst_t = sb("dst_t", [P, ECOLS])
            m.src_t = sb("src_t", [P, ECOLS], I32)
            m.ew_t = sb("ew_t", [P, ECOLS])
            m.step_group = sb("step_group", [P, STEPS], I32)
            m.step_tile = sb("step_tile", [P, STEPS], I32)
            m.step_code = sb("step_code", [P, STEPS], I32)
            m.step_base = sb("step_base", [P, STEPS])
            m.group_end = sb("group_end", [P, GROUPS], I32)
            layernorm_and_plan(nc, sem, x, src, dst, edge_weight, feats, m)
            weighted_sums(nc, sem, feats, edge_index, x, W, b, W_gat, m)
            attention_terms(nc, sem, att_src, att_dst, m)
        with nc.sbuf_tensor("states", [P, GCOLS, STATE], F32) as states:
            m.states = states
            gather_and_experts(nc, sem, W1, b1, W2, b2, edge_index, m)
            segment_softmax(nc, sem, m)
        combine(nc, sem, b_gat, gamma, beta, out, m)


def layernorm_and_plan(nc, sem, x, src, dst, ew, feats, m):
    with ExitStack() as ctx:
        def sb(name, shape, dt):
            return ctx.enter_context(nc.sbuf_tensor(name, shape, dt))

        xin = sb("xin", [P, 2, CH, FEAT], F32)
        xout = sb("xout", [P, 2, CH, FEAT], F32)
        stats = sb("stats", [P, 2, CH, 6], F32)
        mv = sb("mv", [P, 2, CH, 2], F32)
        rstd = sb("rstd", [P, 2, CH], F32)
        lent = sb("raw", [P, 5 * ECOLS], F32)
        raw_i = lent[:, 0:2 * ECOLS].bitcast(I32).rearrange("p (a b e) -> p a b e", a=2, e=P)
        raw_f = lent[:, 2 * ECOLS:5 * ECOLS].rearrange("p (a b e) -> p a b e", a=3, e=P)
        last_sel = sb("last_sel", [P, P], F32)
        gi = sb("gi", [P, GROUPS], I32)
        gf = sb("gf", [P, GROUPS], F32)
        ge = sb("ge", [P, GROUPS], F32)
        giota = sb("giota", [P, STEPS], F32)
        gend = sb("gend", [P, 4], F32)
        last = sb("last", [P, STEPS], I32)
        odd = sb("odd", [P, STEPS], I32)
        spent = lent[:, 2 * ECOLS:5 * ECOLS]
        passed = spent[:, 0:4 * STEPS].rearrange("p (q s) -> p q s", q=4)
        gdiag = spent[:, 4 * STEPS:4 * STEPS + 4 * P].rearrange("p (q n) -> p q n", q=4)
        stepf = spent[:, 4 * STEPS + 4 * P:6 * STEPS + 4 * P].rearrange("p (q s) -> p q s", q=2)
        turn = ctx.enter_context(nc.psum_tensor("turn", [P, 2, 2048], F32))

        s_const, s_raw0, s_raw = sem("a_const"), sem("a_raw_cleared"), sem("a_raw_loaded")
        s_xin = [sem("a_x0"), sem("a_x1")]
        s_out = [sem("a_out0"), sem("a_out1")]
        s_clear = sem("a_x_cleared")
        s_past = sem("a_past")
        s_var, s_std, s_norm = sem("a_var"), sem("a_std"), sem("a_norm")
        s_v, s_t, s_ev = sem("a_vector"), sem("a_turned"), sem("a_turn_read")
        s_pl = sem("a_pool")
        s_edge = sem("a_edge_vector")

        x_tiles = x[0:FULL_TILES * P, :].rearrange("(t p) f -> p t f", p=P)
        f_tiles = feats.rearrange("(t p) f -> p t f", p=P)
        main = (EBLOCKS - 1) * P * P
        rest = (EDGES - main) // P
        tail = EDGES - main - rest * P

        block = ctx.enter_context(nc.Block())

        @block.sync
        def _(sp):
            sp.wait_ge(s_raw0, 3)
            for a, t in ((dst, raw_i[:, 0]), (src, raw_i[:, 1]), (ew, raw_f[:, 2])):
                sp.dma_start(t[:, 0:EBLOCKS - 1, :],
                             a[0:main].rearrange("(b q e) -> q b e", q=P, e=P)).then_inc(s_raw, 16)
                sp.dma_start(t[0:rest, EBLOCKS - 1, :],
                             a[main:main + rest * P].rearrange("(q e) -> q e", e=P)).then_inc(s_raw, 16)
                sp.dma_start(t[rest:rest + 1, EBLOCKS - 1, 0:tail],
                             a[main + rest * P:EDGES].rearrange("(q e) -> q e", q=1)).then_inc(s_raw, 16)

            def load(c, k):
                sp.dma_start(xin[:, k, :, :], x_tiles[:, ds(c * CH, CH), :]).then_inc(s_xin[k], 16)

            def store(c, k, n):
                sp.wait_ge(s_norm, n)
                sp.dma_start(f_tiles[:, ds(c * CH, CH), :], xout[:, k, :, :]).then_inc(s_out[k], 16)

            load(0, 0)
            load(1, 1)
            with sp.Fori(1, CHUNKS // 2 - 1) as i:
                for k in range(2):
                    store(i * 2 + k - 2, k, i * 2 + k - 1)
                    load(i * 2 + k, k)
            for k in range(2):
                c = CHUNKS - 2 + k
                store(c - 2, k, c - 1)
                if k == 0:
                    load(c, k)
                else:
                    sp.dma_start(xin[:, k, 0:CH - 1, :], x_tiles[:, c * CH:FULL_TILES, :]).then_inc(s_xin[k], 16)
                    sp.wait_ge(s_clear, 1)
                    sp.dma_start(xin[0:LAST_ROWS, k, CH - 1, :], x[FULL_TILES * P:NODES, :]).then_inc(s_xin[k], 16)
            for k in range(2):
                store(CHUNKS - 2 + k, k, CHUNKS - 1 + k)
            for k in range(2):
                sp.wait_ge(s_out[k], 16 * (CHUNKS // 2))

        @block.gpsimd
        def _(pool):
            pool.memset(raw_i[:, 0, :, :], -1).then_inc(s_raw0, 1)
            pool.memset(raw_i[:, 1, :, :], 0).then_inc(s_raw0, 1)
            pool.memset(raw_f[:, 2, :, :], 0.0).then_inc(s_raw0, 1)
            c = Count(pool, s_pl)
            c.inc(pool.memset(m.ident[:], 0.0))
            c.inc(pool.memset(m.ones[:], 1.0))
            c.inc(pool.memset(last_sel[:], 0.0))
            pool.memset(m.eps[:], LN_EPS).then_inc(s_const, 1)
            pool.iota(m.iota[:], pattern=[[1, P]], base=0, channel_multiplier=0,
                      allow_small_or_imprecise_dtypes=True).then_inc(s_const, 1)
            pool.iota(giota[:], pattern=[[1, STEPS]], base=0, channel_multiplier=0,
                      allow_small_or_imprecise_dtypes=True).then_inc(s_const, 1)
            pool.wait_ge(s_pl, c.n)
            pool.affine_select(out=m.ident[:], in_=m.ident[:], compare_op=ALU.not_equal, fill=1.0, base=0,
                               pattern=[[-1, P]], channel_multiplier=1).then_inc(s_const, 1)
            pool.affine_select(out=last_sel[:], in_=last_sel[:], compare_op=ALU.not_equal, fill=1.0,
                               base=1 - P, pattern=[[0, P]], channel_multiplier=1).then_inc(s_const, 1)

        @block.scalar
        def _(act):
            act.wait_ge(s_const, 1)
            with act.Fori(0, CHUNKS // 2) as i:
                for k in range(2):
                    act.wait_ge(s_var, i * 2 + (k + 1))
                    act.activation(rstd[:, k, :], mv[:, k, :, 1], ACT.Sqrt, bias=m.eps[:, 0:1]).then_inc(s_std, 1)

        @block.vector
        def _(v):
            c = Count(v, s_edge)

            v.wait_ge(s_raw, 9 * 16)
            for a in range(2):
                c.inc(v.tensor_copy(raw_f[:, a, :, :], raw_i[:, a, :, :]))
            for n, t in enumerate((m.dst_t, m.src_t, m.ew_t)):
                v.wait_ge(s_t, n + 1)
                c.inc(v.tensor_copy(t[:], turn[:, n % 2, 0:ECOLS]))
                v.wait_ge(s_edge, c.n)
                v.sem_inc(s_ev, 1)
            v.wait_ge(s_t, 4)
            c.done(v.tensor_copy(gi[:], turn[:, 1, 0:GROUPS]))
            c.done(v.tensor_scalar(gi[:], gi[:], 7, None, ALU.arith_shift_right))
            c.done(v.tensor_copy(gf[:], gi[:]))
            c.done(v.memset(gf[:, GROUPS - 1:GROUPS], float(TILES - 1)))
            v.wait_ge(s_const, 5)
            c.done(v.tensor_tensor(ge[:], gf[:], giota[:, 0:GROUPS], ALU.add))
            c.inc(v.tensor_scalar(m.group_end[:], ge[:], 1.0, None, ALU.add))
            for q in range(4):
                w = min(P, GROUPS - q * P)
                c.inc(v.tensor_tensor(gdiag[:, q, 0:w], ge[:, q * P:q * P + w], m.ident[:, 0:w], ALU.mult))
            v.wait_ge(s_edge, c.n)
            for q in range(4):
                w = min(P, GROUPS - q * P)
                c.inc(v.tensor_reduce(gend[:, q:q + 1], gdiag[:, q, 0:w], AX_X, ALU.add))
            v.wait_ge(s_edge, c.n)
            for q in range(4):
                c.inc(v.tensor_scalar(passed[:, q, :], giota[:], gend[:, q:q + 1], None, ALU.is_gt))
            v.wait_ge(s_edge, c.n)
            v.sem_inc(s_ev, 1)
            v.wait_ge(s_t, 5)
            c.done(v.tensor_copy(stepf[:, 0, :], turn[:, 0, 0:STEPS]))
            c.inc(v.tensor_copy(m.step_group[:], stepf[:, 0, :]))
            c.done(v.tensor_tensor(stepf[:, 1, :], giota[:], stepf[:, 0, :], ALU.subtract))
            c.inc(v.tensor_copy(m.step_tile[:], stepf[:, 1, :]))
            c.inc(v.tensor_tensor(last[:, 0:STEPS - 1], stepf[:, 1, 1:STEPS], stepf[:, 1, 0:STEPS - 1],
                                  ALU.subtract))
            c.inc(v.memset(last[:, STEPS - 1:STEPS], 1))
            c.inc(v.tensor_scalar(m.step_base[:], stepf[:, 1, :], float(P), None, ALU.mult))
            v.wait_ge(s_edge, c.n)
            c.inc(v.tensor_scalar(odd[:], m.step_tile[:], 1, 1, ALU.bitwise_and, ALU.logical_shift_left))
            c.done(v.tensor_scalar(m.step_code[:], m.step_group[:], 2, None, ALU.logical_shift_left))
            c.done(v.tensor_tensor(m.step_code[:], m.step_code[:], odd[:], ALU.bitwise_or))
            c.done(v.tensor_tensor(m.step_code[:], m.step_code[:], last[:], ALU.bitwise_or))
            v.sem_inc(s_ev, 1)

            def normalise(i, k, last=False):
                n = i * 2 + k
                v.wait_ge(s_xin[k], i * 16 + (32 if last else 16))
                for t in range(CH):
                    q = v.bn_stats(stats[:, k, t, :], xin[:, k, t, :])
                q.then_inc(s_v, 1)
                v.wait_ge(s_v, n * 3 + 1)
                v.sem_inc(s_past, 1)
                for t in range(CH):
                    q = v.bn_aggr(mv[:, k, t, :], stats[:, k, t, :])
                q.then_inc(s_var, 1)
                v.wait_ge(s_std, n + 1)
                v.reciprocal(rstd[:, k, :], rstd[:, k, :]).then_inc(s_v, 1)
                v.wait_ge(s_v, n * 3 + 2)
                if not (isinstance(i, int) and i == 0):
                    v.wait_ge(s_out[k], i * 16)
                for t in range(CH):
                    q = v.tensor_scalar(xout[:, k, t, :], xin[:, k, t, :], mv[:, k, t, 0:1],
                                        rstd[:, k, t:t + 1], ALU.subtract, ALU.mult)
                    if t == CH - 2:
                        q.then_inc(s_v, 1)
                q.then_inc(s_norm, 1)

            normalise(0, 0)
            normalise(0, 1)
            with v.Fori(1, CHUNKS // 2 - 1) as i:
                for k in range(2):
                    normalise(i, k)
            normalise(CHUNKS // 2 - 1, 0)
            v.wait_ge(s_norm, CHUNKS - 2)
            v.memset(xin[:, 1, CH - 1, :], 0.0).then_inc(s_clear, 1)
            normalise(CHUNKS // 2 - 1, 1, last=True)
            v.wait_ge(s_norm, CHUNKS)

        @block.tensor
        def _(pe):
            pe.wait_ge(s_edge, 2)
            pe.wait_ge(s_const, 5)
            for n in range(3):
                if n == 2:
                    pe.wait_ge(s_ev, 1)
                for q in range(EBLOCKS):
                    t = pe.transpose(turn[:, n % 2, q * P:(q + 1) * P], raw_f[:, n, q, :], m.ident[:])
                t.then_inc(s_t, 1)
            pe.wait_ge(s_ev, 2)
            pe.matmul(turn[:, 1, 0:GROUPS], last_sel[:], m.dst_t[:, GT - 1:GROUPS * GT:GT],
                      start=True, stop=True).then_inc(s_t, 1)
            pe.wait_ge(s_ev, 4)
            for q in range(4):
                w = min(P, GROUPS - q * P)
                t = pe.matmul(turn[:, 0, 0:STEPS], m.ones[0:w, :], passed[0:w, q, :], start=(q == 0), stop=(q == 3))
            t.then_inc(s_t, 1)


def weighted_sums(nc, sem, feats, edge_index, x, W, b, W_gat, m):
    XS = 4
    with ExitStack() as ctx:
        def sb(name, shape, dt=F32):
            return ctx.enter_context(nc.sbuf_tensor(name, shape, dt))

        def pb(name, cols=512):
            return ctx.enter_context(nc.psum_tensor(name, [P, cols], F32))

        rows = sb("rows", [P, RING, GT, FEAT])
        idx = sb("idx", [P, 2, RING, GT], I32)
        rel = sb("rel", [P, XS, GT])
        hot = sb("hot", [P, XS, GT, P])
        key = [m.seg_keep[:], m.src_sorted[:].bitcast(F32), sb("key", [P, GCOLS])[:]]
        key_i = [m.seg_keep[:].bitcast(I32), m.src_sorted[:], key[2].bitcast(I32)]
        sign = sb("sign", [P, 2])
        shift_dn = sb("shift_dn", [P, P])
        lastd = sb("lastd", [P, 2])
        w_raw = sb("w_raw", [P, HALVES, FEAT])
        w_t = sb("w_t", [P, HALVES, FEAT])
        wg = sb("wg", [P, HALVES, HE])
        brow = sb("brow", [1, FEAT])
        zero_b = sb("b_zeros", [1, FEAT], BF16)
        sums = sb("sums", [P, FEAT])
        sums_t = sb("sums_t", [P, FEAT])
        xs = sb("x_ring", [P, XS, FEAT])
        x1 = sb("x1", [P, 2, FEAT])
        xc = sb("xc", [P, FEAT])
        xc_t = sb("xc_t", [P, FEAT])
        squares = sb("squares", [P, FEAT])
        psA = pb("node_sums", 1024)
        psT = pb("turned", GCOLS)
        psS, psX, psY, psH = pb("sums_turned"), pb("x1_product"), pb("xc_turned"), pb("h_product")

        s_ei = sem("b_edge_index")
        s_idx, s_ready = sem("b_idx_ready"), sem("b_rows_ready")
        s_got = [sem(f"b_gathered{k}") for k in range(RING)]
        s_past = sem("b_past")
        s_rel, s_hot, s_mm = sem("b_rel"), sem("b_hot_ready"), sem("b_step_multiplied")
        s_s = sem("b_sort")
        s_turn, s_turned = sem("b_turn_ask"), sem("b_turned")
        s_pc = sem("b_pool_const")
        s_w, s_wt, s_wte = sem("b_weights"), sem("b_w_turned"), sem("b_w_ready")
        s_tile = sem("b_tile_summed")
        s_evac = sem("b_tile_out_of_psum")
        s_a = sem("b_scalar")
        s_xin, s_x1o = sem("b_x_loaded"), [sem("b_x1_stored0"), sem("b_x1_stored1")]

        block = ctx.enter_context(nc.Block())
        full_rounds = GROUPS // RING
        left = GROUPS - full_rounds * RING
        QUADS = STEPS // XS
        PIECES = 24
        CUT = [1 + (QUADS - 1) * n // PIECES for n in range(PIECES + 1)]
        assert STEPS % XS == 0 and TILES % 2 == 0 and full_rounds % 2 == 0 and RING == 8

        turned_keys, cur = [], 2
        for k in range(1, 18):
            if k >= 11:
                turned_keys.append(cur)
                cur = 1 if cur != 1 else 0
                for _ in range(k - 10):
                    cur = 1 - cur
                turned_keys.append(cur)
                cur = 1 - cur
                for _ in range(10):
                    cur = 1 - cur
            else:
                for _ in range(k):
                    cur = 1 if cur == 2 else 1 - cur

        @block.sync
        def _(sp):
            sp.dma_start(key_i[0], edge_index[1, :].rearrange("(p j) -> p j", p=P)).then_inc(s_ei, 16)
            sp.dma_start(key_i[1], edge_index[0, :].rearrange("(p j) -> p j", p=P)).then_inc(s_ei, 16)
            sp.dma_start(w_raw[:], W.rearrange("(o p) i -> p o i", p=P)).then_inc(s_w, 16)
            sp.dma_start(wg[:], W_gat.rearrange("(k p) c -> p k c", p=P)).then_inc(s_w, 16)
            sp.dma_start(brow[:], b.rearrange("(a n) -> a n", a=1)).then_inc(s_w, 16)
            with sp.Fori(1, full_rounds + 1) as i:
                for k in range(RING):
                    sp.wait_ge(s_got[k], i * (16 * GT))
                    sp.sem_inc(s_ready, 1)
            for k in range(left):
                sp.wait_ge(s_got[k], (full_rounds + 1) * 16 * GT)
                sp.sem_inc(s_ready, 1)

        @block.gpsimd
        def _(pool):
            def indices(i, half):
                pool.tensor_copy(idx[:, half, :, :].rearrange("p r t -> p (r t)"),
                                 m.src_t[:, ds(i * (RING * GT), RING * GT)]).then_inc(s_idx, 1)
                pool.wait_ge(s_idx, i + 1)
                pool.sem_inc(s_past, 1)

            def gather(k, half):
                for j in range(GT):
                    pool.indirect_dma_start(rows[:, k, j, :], None, feats,
                                            bass.IndirectOffsetOnAxis(ap=idx[:, half, k, j:j + 1], axis=0)
                                            ).then_inc(s_got[k], 16)

            def refill(i, k, half):
                end = pool.value_load(m.group_end[0:1, ds(i * RING + (k - RING), 1)], min_val=1, max_val=STEPS)
                pool.wait_ge(s_mm, end)
                pool.sem_inc(s_past, 1)
                gather(k, half)

            indices(0, 0)
            for k in range(RING):
                gather(k, 0)
            c = Count(pool, s_pc)
            c.inc(pool.memset(zero_b[:], 0.0))
            c.inc(pool.memset(shift_dn[:], 0.0))
            c.inc(pool.iota(sign[:, 1:2], pattern=[[0, 1]], base=0, channel_multiplier=1,
                            allow_small_or_imprecise_dtypes=True))
            pool.wait_ge(s_pc, c.n)
            for t in (sums, sums_t, xc, xc_t, xs[:, 2:XS, :]):
                c.inc(pool.memset(t[:], 0.0))
            c.inc(pool.affine_select(out=shift_dn[:], in_=shift_dn[:], compare_op=ALU.not_equal, fill=1.0,
                                     base=1, pattern=[[-1, P]], channel_multiplier=1))
            with pool.Fori(0, full_rounds // 2 - 1) as u:
                for half in (1, 0):
                    i = u * 2 + (2 - half)
                    indices(i, half)
                    for k in range(RING):
                        refill(i, k, half)
            i = full_rounds - 1
            indices(i, 1)
            for k in range(RING):
                refill(i, k, 1)
            indices(full_rounds, 0)
            for k in range(left):
                refill(full_rounds, k, 0)

        @block.scalar
        def _(act):
            def load(d, slot):
                if isinstance(d, int) and d == TILES - 1:
                    act.dma_start(xs[0:LAST_ROWS, slot, :], x[FULL_TILES * P:NODES, :]).then_inc(s_xin, 16)
                else:
                    act.dma_start(xs[:, slot, :], x[0:FULL_TILES * P, :].rearrange("(t p) f -> t p f", p=P)[
                        ds(d, 1), :, :].rearrange("t p f -> p (t f)")).then_inc(s_xin, 16)

            def tile(j, r):
                real = isinstance(j, int)
                par = r % 2
                act.wait_ge(s_tile, j + 1)
                if not real or j < TILES:
                    t = act.copy(sums[:], psA[:, par * 512:par * 512 + FEAT])
                if not real or 1 <= j < TILES + 1:
                    t = act.copy(sums_t[:], psS[:, 0:FEAT])
                if not real or 2 <= j < TILES + 2:
                    n = j - 2
                    if not real or n >= 2:
                        act.wait_ge(s_x1o[par], j * 8 - (16 + 8 * par))
                        act.sem_inc(s_past, 1)
                    act.activation(x1[:, par, :], psX[:, 0:FEAT], ACT.Copy, accum_out=m.mean[:, ds(n, 1)]
                                   ).then_inc(s_a, 1)
                    act.wait_ge(s_a, j * 2 - 3)
                    act.sem_inc(s_past, 1)
                    act.mul(m.mean[:, ds(n, 1)], m.mean[:, ds(n, 1)], -1.0 / FEAT).then_inc(s_a, 1)
                    act.dma_start(m.x1_dram.rearrange("(t p) f -> t p f", p=P)[ds(n, 1), :, :].rearrange(
                        "t p f -> p (t f)"), x1[:, par, :]).then_inc(s_x1o[par], 16)
                    act.wait_ge(s_a, j * 2 - 2)
                    act.sem_inc(s_past, 1)
                    act.activation(xc[:], psX[:, 0:FEAT], ACT.Identity, bias=m.mean[:, ds(n, 1)])
                    t = act.activation(squares[:], psX[:, 0:FEAT], ACT.Square, bias=m.mean[:, ds(n, 1)],
                                       accum_out=m.rstd[:, ds(n, 1)])
                if not real or 3 <= j < TILES + 3:
                    t = act.copy(xc_t[:], psY[:, 0:FEAT])
                if not real or 4 <= j < TILES + 4:
                    t = act.copy(m.node_row[:, ds(j - 4, 1), 0:HE], psH[:, 0:HE])
                t.then_inc(s_evac, 1)
                if not real or j + 2 <= TILES:
                    act.wait_ge(s_xin, j * 16 + 32)
                if not real or j + 2 < TILES:
                    load(j + 2, (r + 2) % XS)

            act.sem_inc(s_evac, 1)
            act.wait_ge(s_w, 16 * 3)
            load(0, 0)
            act.wait_ge(s_xin, 16)
            load(1, 1)
            act.wait_ge(s_wt, 1)
            act.copy(w_t[:], psX[:, :].rearrange("p (k o) -> p k o", k=HALVES)).then_inc(s_wte, 1)
            for j in range(XS):
                tile(j, j)
            LOOPED = (TILES - 3) // XS
            with act.Fori(1, LOOPED) as u:
                for r in range(XS):
                    tile(u * XS + r, r)
            for j in range(LOOPED * XS, TILES + 4):
                tile(j, j % XS)
            for par in range(2):
                act.wait_ge(s_x1o[par], 16 * (TILES // 2))

        @block.tensor
        def _(pe):
            pe.wait_ge(s_w, 16 * 3)
            for k in range(HALVES):
                for o in range(HALVES):
                    t = pe.transpose(psX[:, k * FEAT + o * P:k * FEAT + (o + 1) * P],
                                     w_raw[:, o, k * P:(k + 1) * P], m.ident[:])
            t.then_inc(s_wt, 1)
            pe.wait_ge(s_wte, 1)
            pe.wait_ge(s_pc, 9)

            def open_or_close(bank, start):
                pe.matmul(psA[:, ds(bank * 512, FEAT)], zero_b[:, 0:P], zero_b[:], start=start, stop=not start)

            def stages(d):
                pe.wait_ge(s_evac, d + 1)
                for k in range(HALVES):
                    pe.matmul(psH[:, 0:HE], xc_t[:, k * P:(k + 1) * P], wg[:, k, :],
                              start=(k == 0), stop=(k == HALVES - 1))
                for k in range(HALVES):
                    pe.transpose(psY[:, k * P:(k + 1) * P], xc[:, k * P:(k + 1) * P], m.ident[:])
                pe.matmul(psX[:, 0:FEAT], m.ones[0:1, :], brow[:], start=True, stop=False)
                pe.matmul(psX[:, 0:FEAT], m.ident[:], xs[:, ds((d + 2) % XS, 1), :], start=False, stop=False)
                for k in range(HALVES):
                    pe.matmul(psX[:, 0:FEAT], sums_t[:, k * P:(k + 1) * P], w_t[:, k, :],
                              start=False, stop=(k == HALVES - 1))
                for k in range(HALVES):
                    t = pe.transpose(psS[:, k * P:(k + 1) * P], sums[:, k * P:(k + 1) * P], m.ident[:])
                t.then_inc(s_tile, 1)

            def step(s, r):
                code = pe.value_load(m.step_code[0:1, ds(s, 1)], min_val=0, max_val=GROUPS * 4 - 1)
                pe.wait_ge(s_hot, s + 1)
                pe.wait_ge(s_ready, (code >> 2) + 1)
                for j in range(GT):
                    t = pe.matmul(psA[:, ds(((code >> 1) & 1) * 512, FEAT)], hot[:, r, j, :],
                                  rows[:, ds((code >> 2) & (RING - 1), 1), j, :], start=False, stop=False)
                t.then_inc(s_mm, 1)
                with pe.If((code & 1) == 1):
                    d = pe.value_load(m.step_tile[0:1, ds(s, 1)], min_val=0, max_val=TILES - 1)
                    open_or_close(d & 1, False)
                    stages(d)
                    open_or_close((d + 1) & 1, True)

            open_or_close(0, True)
            for r in range(XS):
                step(r, r)
            for n in range(PIECES):
                with pe.Fori(CUT[n], CUT[n + 1]) as u:
                    for r in range(XS):
                        step(u * XS + r, r)
                if n >= 9 and n < PIECES - 1:
                    pe.wait_ge(s_turn, n - 8)
                    for q in range(GCOLS // P):
                        t = pe.transpose(psT[:, q * P:(q + 1) * P], key[turned_keys[n - 9]][:, q * P:(q + 1) * P],
                                         m.ident[:])
                    t.then_inc(s_turned, 1)
            open_or_close(TILES & 1, False)
            for d in range(TILES, TILES + 4):
                stages(d)
            pe.wait_ge(s_turn, PIECES - 9)
            pe.matmul(psT[:, 0:2], shift_dn[:], lastd[:], start=True, stop=True).then_inc(s_turned, 1)

        @block.vector
        def _(v):
            c = Count(v, s_s)

            def one_hots(s, r, first=False):
                g = v.value_load(m.step_group[0:1, ds(s, 1)], min_val=0, max_val=GROUPS - 1)
                if not first:
                    v.wait_ge(s_mm, s - (XS - 1))
                v.tensor_scalar(rel[:, r, :], m.dst_t[:, ds(g * GT, GT)], m.step_base[:, ds(s, 1)], None,
                                ALU.subtract).then_inc(s_rel, 1)
                v.wait_ge(s_rel, s + 1)
                for j in range(GT):
                    t = v.tensor_scalar(hot[:, r, j, :], m.iota[:], rel[:, r, j:j + 1],
                                        m.ew_t[:, ds(g * GT + j, 1)], ALU.is_equal, ALU.mult)
                t.then_inc(s_hot, 1)

            def sort_init():
                v.wait_ge(s_ei, 32)
                c.done(v.tensor_scalar(key_i[0], key_i[0], KEY_SHIFT, KEY_TOP, ALU.logical_shift_left,
                                       ALU.bitwise_or))
                c.done(v.tensor_tensor(key_i[2], key_i[0], key_i[1], ALU.bitwise_or))
                v.wait_ge(s_pc, 9)
                c.done(v.tensor_copy(m.dst_first[:], sign[:, 1:2]))
                c.done(v.tensor_scalar(m.dst_first[:], m.dst_first[:], 1, None, ALU.bitwise_and))
                c.done(v.tensor_copy(sign[:, 0:1], m.dst_first[:]))
                c.done(v.tensor_scalar(sign[:, 0:1], sign[:, 0:1], -2.0, 1.0, ALU.mult, ALU.add))

            def flip(buf, k, col_bits):
                t = key[buf]
                hb, lb = k - col_bits, k - 1 - col_bits
                if k == 1:
                    w = t.rearrange("p (a h w) -> p a h w", h=2, w=1 << hb)
                    c.done(v.tensor_scalar(w[:, :, 1, :], w[:, :, 1, :], -1.0, None, ALU.mult))
                elif k == 17:
                    w = t.rearrange("p (a h w) -> p a h w", h=2, w=1 << lb)
                    c.done(v.tensor_scalar(w[:, :, 1, :], w[:, :, 1, :], -1.0, None, ALU.mult))
                elif k == 10:
                    w = t.rearrange("p (a h w) -> p a h w", h=2, w=1 << lb)
                    c.done(v.tensor_scalar(w[:, :, 1, :], w[:, :, 1, :], -1.0, None, ALU.mult))
                    c.done(v.tensor_scalar(t, t, sign[:, 0:1], None, ALU.mult))
                else:
                    w = t.rearrange("p (a h l w) -> p a h l w", h=2, l=2, w=1 << lb)
                    c.inc(v.tensor_scalar(w[:, :, 0, 1, :], w[:, :, 0, 1, :], -1.0, None, ALU.mult))
                    c.done(v.tensor_scalar(w[:, :, 1, 0, :], w[:, :, 1, 0, :], -1.0, None, ALU.mult))

            def exchange(buf, bit):
                to = 1 if buf == 2 else 1 - buf
                a = key[buf].rearrange("p (a h w) -> p a h w", h=2, w=1 << bit)
                o = key[to].rearrange("p (a h w) -> p a h w", h=2, w=1 << bit)
                c.inc(v.tensor_tensor(o[:, :, 0, :], a[:, :, 0, :], a[:, :, 1, :], ALU.min))
                c.done(v.tensor_tensor(o[:, :, 1, :], a[:, :, 0, :], a[:, :, 1, :], ALU.max))
                return to

            def columns(buf, bits):
                for bit in range(bits - 1, -1, -1):
                    buf = exchange(buf, bit)
                return buf

            def take(buf, n):
                v.wait_ge(s_turned, n)
                c.done(v.tensor_copy(key[buf], psT[:]))
                return buf

            def sort_piece(n, buf):
                if n < 10:
                    flip(buf, n + 1, 0)
                    buf = columns(buf, n + 1)
                else:
                    k, back = 11 + (n - 10) // 2, (n - 10) % 2
                    if back:
                        buf = columns(take(1 - buf, n - 9), 10)
                    else:
                        buf = take(1 if buf != 1 else 0, n - 9)
                        flip(buf, k, 10)
                        buf = columns(buf, k - 10)
                if 9 <= n < PIECES - 1:
                    v.sem_inc(s_turn, 1)
                return buf

            def sort_end(buf):
                k, d = key_i[buf], key_i[2]
                c.done(v.tensor_scalar(d, k, KEY_SHIFT, (1 << KEY_SHIFT) - 1, ALU.logical_shift_right,
                                       ALU.bitwise_and))
                c.inc(v.tensor_scalar(m.src_sorted[:], k, (1 << KEY_SHIFT) - 1, None, ALU.bitwise_and))
                c.done(v.tensor_copy(m.dst_first[:], d[:, 0:1]))
                c.done(v.tensor_copy(key[2], d))
                c.inc(v.tensor_copy(lastd[:, 0:1], key[2][:, GCOLS - 1:GCOLS]))
                c.done(v.tensor_copy(lastd[:, 1:2], key[2][:, 0:1]))
                v.sem_inc(s_turn, 1)
                c.inc(v.tensor_tensor(m.seg_keep[:, 1:GCOLS], key[2][:, 1:GCOLS], key[2][:, 0:GCOLS - 1],
                                      ALU.is_equal))
                c.done(v.memset(m.seg_keep[:, 0:1], 1.0))
                c.done(v.tensor_reduce(m.link[:, 1:2], m.seg_keep[:], AX_X, ALU.min))
                v.wait_ge(s_turned, PIECES - 9)
                c.done(v.tensor_tensor(m.link[:, 0:1], psT[:, 0:1], key[2][:, 0:1], ALU.is_equal))
                c.done(v.memset(m.link[0:1, 0:1], 0.0))

            for r in range(XS):
                one_hots(r, r, first=True)
            sort_init()
            buf = 2
            for n in range(PIECES):
                with v.Fori(CUT[n], CUT[n + 1]) as u:
                    for r in range(XS):
                        one_hots(u * XS + r, r)
                buf = sort_piece(n, buf)
            sort_end(buf)

def attention_terms(nc, sem, att_src, att_dst, m):
    with ExitStack() as ctx:
        def sb(name, shape, dt=F32):
            return ctx.enter_context(nc.sbuf_tensor(name, shape, dt))

        att = sb("att", [P, 2, HE])
        prod = sb("prod", [P, 2, TILES, HE])
        zeros = sb("zeros", [P, 512])
        std = sb("std_all", [P, TILES])
        s_std = sem("c_std")
        s_att, s_v, s_row = sem("c_att"), sem("c_vector"), sem("c_rows_ready")
        s_z, s_zo, s_fin = sem("c_zero"), sem("c_zero_stored"), sem("c_rows_stored")
        block = ctx.enter_context(nc.Block())

        @block.sync
        def _(sp):
            for n, a in enumerate((att_src, att_dst)):
                sp.dma_start(att[:, n, :], a.rearrange("(o h) e -> o (h e)", o=1).to_broadcast([P, HE])
                             ).then_inc(s_att, 16)
            for n, (d, t) in enumerate(((m.row_dram, m.node_row), (m.adst_dram, m.node_dst))):
                sp.wait_ge(s_row, n + 1)
                sp.dma_start(d.rearrange("(t p) c -> p t c", p=P), t[:]).then_inc(s_fin, 16)
            sp.wait_ge(s_fin, 32)

        @block.gpsimd
        def _(pool):
            pool.memset(zeros[:], 0.0).then_inc(s_z, 1)

        @block.scalar
        def _(act):
            act.activation(std[:], m.rstd[:], ACT.Sqrt, bias=m.eps[:, 0:1], scale=1.0 / FEAT).then_inc(s_std, 1)
            act.wait_ge(s_z, 1)
            flat = m.adst_first.rearrange("(q p n) c -> q p (n c)", q=8, p=P)
            for q in range(8):
                act.dma_start(flat[q], zeros[:]).then_inc(s_zo, 16)
            act.wait_ge(s_zo, 16 * 8)

        @block.vector
        def _(v):
            c = Count(v, s_v)
            c.inc(v.tensor_scalar(m.mean[:], m.mean[:], -1.0, None, ALU.mult))
            v.wait_ge(s_std, 1)
            c.done(v.reciprocal(m.rstd[:], std[:]))
            c.done(v.tensor_tensor(m.node_row[:, :, 0:HE], m.node_row[:, :, 0:HE],
                                   m.rstd[:, :, None].to_broadcast([P, TILES, HE]), ALU.mult))
            v.wait_ge(s_att, 32)
            for q, o in enumerate((m.node_row[:, :, HE:ROWF], m.node_dst[:])):
                c.done(v.tensor_tensor(prod[:, q, :, :], m.node_row[:, :, 0:HE],
                                       att[:, q:q + 1, :].to_broadcast([P, TILES, HE]), ALU.mult))
                c.done(v.tensor_reduce(o, prod[:, q, :, :].rearrange("p t (h e) -> p t h e", e=EXPERTS), AX_X,
                                       ALU.add))
                v.sem_inc(s_row, 1)


def gather_and_experts(nc, sem, W1, b1, W2, b2, edge_index, m):
    with ExitStack() as ctx:
        def sb(name, shape, dt):
            return ctx.enter_context(nc.sbuf_tensor(name, shape, dt))

        FB = HID // P
        PAIRS = TILES // 2
        N2 = 2 * P
        GB, SLOTS = 16, 4
        BATCHES = GCOLS // GB
        WEIGHT_LOADS = HALVES + FB + 2 * EXPERTS

        w1 = sb("w1", [P, HALVES, EXPERTS, HID], F32)
        w2 = sb("w2", [P, FB, EXPERTS, FEAT], F32)
        b1c = sb("b1c", [P, EXPERTS, FB], F32)
        b2r = sb("b2r", [P, EXPERTS, FEAT], F32)
        xd = sb("d_x", [P, 2, 2, FEAT], F32)
        yn = sb("d_y", [P, 2, FEAT], F32)
        yt = sb("d_yt", [P, 2, HALVES, N2], F32)
        hid = sb("hid", [P, 2, FB, N2], F32)
        yo = sb("yo", [P, EXPERTS, 2, FEAT], F32)
        got = sb("got", [P, SLOTS, GB, STATE], F32)
        idx = sb("d_idx", [P, SLOTS, GB], I32)
        lo = sb("lo", [P, GCOLS], BF16)
        hi = sb("hi", [P, GCOLS], BF16)
        hot_lo = sb("hot_lo", [P, HCOLS, P], BF16)
        hot_hi = sb("hot_hi", [P, HCOLS, TILES], BF16)
        di = hot_lo[:].rearrange("p a b -> p (a b)").bitcast(I32)[:, 0:2 * GCOLS].rearrange("p (n j) -> p n j", n=2)
        iota_b = sb("iota_b", [P, P], BF16)
        zero_b = sb("zero_b", [P, P], BF16)
        before = sb("before", [P, P], F32)
        cnt = sb("cnt", [P, TILES], F32)
        tot = sb("tot", [P, TILES], F32)
        pos = sb("pos", [P, 2, TILES], F32)
        sidx = sb("sidx", [P, 2, CH], I32)
        sdat = sb("sdat", [P, 2, CH, HEADS], F32)
        psL = [ctx.enter_context(nc.psum_tensor(f"d_hidden{n}", [P, 2, N2], F32)) for n in range(4)]
        psO = [ctx.enter_context(nc.psum_tensor(f"d_expert{n}", [P, 2, FEAT], F32)) for n in range(2)]
        psC = ctx.enter_context(nc.psum_tensor("counts", [P, 512], F32))
        psY = ctx.enter_context(nc.psum_tensor("d_y_turned", [P, HALVES, N2], F32))

        s_w, s_ei = sem("d_weights"), sem("d_edges")
        s_x = [sem("d_x0"), sem("d_x1")]
        s_yn, s_ty, s_yt = sem("d_normed"), sem("d_y_turned"), sem("d_yt_ready")
        s_l1, s_hid, s_l2, s_yo = sem("d_l1"), sem("d_hidden_ready"), sem("d_l2"), sem("d_out_ready")
        s_st = [sem(f"d_stored{e}") for e in range(EXPERTS)]
        s_pc, s_pi = sem("d_pool_const"), sem("d_idx_ready")
        s_got = [sem(f"d_gathered{k}") for k in range(SLOTS)]
        s_past = sem("d_past")
        s_mv = [sem(f"d_moved{k}") for k in range(SLOTS)]
        s_v, s_hh, s_hm = sem("d_count_vector"), sem("d_hot"), sem("d_hist")
        s_cnt, s_pos = sem("d_counts_read"), sem("d_positions")
        s_sc, s_sd = [sem("d_scattered0"), sem("d_scattered1")], sem("d_scatter_staged")

        block = ctx.enter_context(nc.Block())

        @block.sync
        def _(sp):
            sp.dma_start(di[:, 0, :], edge_index[1, :].rearrange("(p j) -> p j", p=P)).then_inc(s_ei, 16)
            for k in range(HALVES):
                sp.dma_start(w1[:, k, :, :], W1[:, k * P:(k + 1) * P, :].rearrange("e p n -> p e n")).then_inc(s_w, 16)
            for k in range(FB):
                sp.dma_start(w2[:, k, :, :], W2[:, k * P:(k + 1) * P, :].rearrange("e p n -> p e n")).then_inc(s_w, 16)
            for e in range(EXPERTS):
                sp.dma_start(b2r[:, e, :], b2[e:e + 1, :].to_broadcast([P, FEAT])).then_inc(s_w, 16)
            with nc.allow_non_contiguous_dma(reason="a bias of 8 KB, once"):
                for e in range(EXPERTS):
                    sp.dma_start(b1c[:, e, :], b1[e, :].rearrange("(k p) -> p k", p=P)).then_inc(s_w, 16)

            def move(i, k):
                sp.wait_ge(s_got[k], i * (16 * GB) + 16 * GB)
                sp.dma_start(m.states[:, ds(i * (SLOTS * GB) + k * GB, GB), :], got[:, k, :, :]
                             ).then_inc(s_mv[k], 16)

            with sp.Fori(0, BATCHES // SLOTS) as i:
                for k in range(SLOTS):
                    move(i, k)
            for k in range(SLOTS):
                sp.wait_ge(s_mv[k], 16 * (BATCHES // SLOTS))

        @block.gpsimd
        def _(pool):
            c = Count(pool, s_pc)
            c.inc(pool.iota(iota_b[:], pattern=[[1, P]], base=0, channel_multiplier=0,
                            allow_small_or_imprecise_dtypes=True))
            c.inc(pool.memset(zero_b[:], 0.0))
            c.inc(pool.memset(before[:], 1.0))
            c.inc(pool.memset(got[:], 0.0))
            pool.wait_ge(s_pc, c.n)
            c.inc(pool.affine_select(out=before[:], in_=before[:], compare_op=ALU.is_gt, fill=0.0, base=0,
                                     pattern=[[1, P]], channel_multiplier=-1))

            def batch(i, k, first=False):
                if not first:
                    pool.wait_ge(s_mv[k], i * 16)
                pool.tensor_copy(idx[:, k, :], m.src_sorted[:, ds(i * (SLOTS * GB) + k * GB, GB)]
                                 ).then_inc(s_pi, 1)
                pool.wait_ge(s_pi, i * SLOTS + (k + 1))
                pool.sem_inc(s_past, 1)
                for j in range(GB):
                    pool.indirect_dma_start(got[:, k, j, 0:ROWF], None, m.row_dram,
                                            bass.IndirectOffsetOnAxis(ap=idx[:, k, j:j + 1], axis=0)
                                            ).then_inc(s_got[k], 16)

            for k in range(SLOTS):
                batch(0, k, first=True)
            with pool.Fori(1, BATCHES // SLOTS) as i:
                for k in range(SLOTS):
                    batch(i, k)

            pool.wait_ge(s_pos, 1)

            def spread(i, k, first=False):
                if not first:
                    pool.wait_ge(s_sc[k], i * (16 * CH))
                pool.tensor_copy(sidx[:, k, :], m.first_pos[:, ds((i * 2 + k) * CH, CH)])
                pool.tensor_copy(sdat[:, k, :, :], m.node_dst[:, ds((i * 2 + k) * CH, CH), :]).then_inc(s_sd, 1)
                pool.wait_ge(s_sd, i * 2 + (k + 1))
                pool.sem_inc(s_past, 1)
                for j in range(CH):
                    pool.indirect_dma_start(m.adst_first, bass.IndirectOffsetOnAxis(ap=sidx[:, k, j:j + 1], axis=0),
                                            sdat[:, k, j, :], None, bounds_check=GEDGES - 1, oob_is_err=False
                                            ).then_inc(s_sc[k], 16)

            for k in range(2):
                spread(0, k, first=True)
            with pool.Fori(1, CHUNKS // 2) as i:
                for k in range(2):
                    spread(i, k)
            for k in range(2):
                pool.wait_ge(s_sc[k], 16 * CH * (CHUNKS // 2))

        @block.scalar
        def _(act):
            act.wait_ge(s_w, 16 * WEIGHT_LOADS)

            def load(i, k):
                act.dma_start(xd[:, k, :, :], m.x1_dram.rearrange("(t p) f -> p t f", p=P)[:, ds(i * 2, 2), :]
                              ).then_inc(s_x[k], 16)

            def hidden(n, e, first=False):
                for q in range(2):
                    act.wait_ge(s_l1, n * 2 + (q + 1))
                    if q == 0 and not first:
                        act.wait_ge(s_l2, n - 1)
                    for f in range(2):
                        t = act.activation(hid[:, e % 2, 2 * q + f, :], psL[(e % 2) * 2 + q][:, f, :], ACT.Gelu,
                                           bias=b1c[:, e, 2 * q + f:2 * q + f + 1])
                    t.then_inc(s_hid, 1)

            def store(n, e, i):
                act.wait_ge(s_yo, n + 1)
                act.dma_start(m.y_dram.rearrange("(t p) e f -> p t e f", p=P)[:, ds(i * 2, 2), e, :], yo[:, e, :, :]
                              ).then_inc(s_st[e], 16)

            def pair(i, k, first=False, last=False):
                for e in range(EXPERTS):
                    hidden(i * EXPERTS + e, e, first=first and e < 2)
                    if e == 0 and not last:
                        load(i + 2, k)
                    if e >= 1:
                        store(i * EXPERTS + (e - 1), e - 1, i)
                    elif not first:
                        store(i * EXPERTS - 1, EXPERTS - 1, i - 1)

            load(0, 0)
            load(1, 1)
            pair(0, 0, first=True)
            with act.Fori(0, PAIRS // 2 - 1) as u:
                for k in range(2):
                    pair(u * 2 + (k + 1), (k + 1) % 2)
            pair(PAIRS - 2, 1, last=True)
            pair(PAIRS - 1, 0, last=True)
            store(PAIRS * EXPERTS - 1, EXPERTS - 1, PAIRS - 1)
            for e in range(EXPERTS):
                act.wait_ge(s_st[e], 16 * PAIRS)

        HLOOP = HPIECES // 2

        @block.tensor
        def _(pe):
            pe.wait_ge(s_pc, 5)
            pe.wait_ge(s_w, 16 * WEIGHT_LOADS)
            pe.matmul(psC[:, 0:TILES], zero_b[:], zero_b[:, 0:TILES], start=True, stop=False)

            def layer1(i, k, n, e, first=False):
                if e == 0:
                    pe.wait_ge(s_yt, i + 1)
                for q in range(2):
                    if not first:
                        pe.wait_ge(s_hid, n * 2 + (q - 3))
                    for f in range(2):
                        for h in range(HALVES):
                            t = pe.matmul(psL[(e % 2) * 2 + q][:, f, :],
                                          w1[:, h, e, (2 * q + f) * P:(2 * q + f + 1) * P], yt[:, k, h, :],
                                          start=(h == 0), stop=(h == HALVES - 1))
                    t.then_inc(s_l1, 1)

            def layer2(n, e, first=False):
                pe.wait_ge(s_hid, n * 2 + 2)
                if not first:
                    pe.wait_ge(s_yo, n - 1)
                for t in range(2):
                    for f in range(FB):
                        q = pe.matmul(psO[e % 2][:, t, :], hid[:, e % 2, f, t * P:(t + 1) * P], w2[:, f, e, :],
                                      start=(f == 0), stop=(f == FB - 1))
                q.then_inc(s_l2, 1)

            def turn(i):
                pe.wait_ge(s_yn, i + 1)
                if not isinstance(i, int) or i >= 1:
                    pe.wait_ge(s_yt, i)
                for t in range(2):
                    for h in range(HALVES):
                        q = pe.transpose(psY[:, h, t * P:(t + 1) * P], yn[:, t, h * P:(h + 1) * P], m.ident[:])
                q.then_inc(s_ty, 1)

            def pair(i, k, first=False):
                for e in range(EXPERTS):
                    if e == 2 and not (isinstance(i, int) and i == PAIRS - 1):
                        turn(i + 1)
                    layer1(i, k, i * EXPERTS + e, e, first=first and e < 2)
                    if e >= 1:
                        layer2(i * EXPERTS + (e - 1), e - 1, first=first and e < 3)
                    elif not first:
                        layer2(i * EXPERTS - 1, EXPERTS - 1)

            def count(q):
                pe.wait_ge(s_hh, q + 1)
                for j in range(HCOLS):
                    t = pe.matmul(psC[:, 0:TILES], hot_lo[:, j, :], hot_hi[:, j, :], start=False, stop=False)
                t.then_inc(s_hm, 1)

            turn(0)
            pair(0, 0, first=True)
            with pe.Fori(0, HLOOP) as u:
                for k in range(2):
                    count(u * 2 + k)
                    pair(u * 2 + (k + 1), (k + 1) % 2)
            pe.matmul(psC[:, 0:TILES], zero_b[:], zero_b[:, 0:TILES], start=False, stop=True).then_inc(s_hm, 1)
            pe.wait_ge(s_cnt, 1)
            pe.matmul(psC[:, P:P + TILES], m.ones[:], cnt[:], start=True, stop=True)
            pe.matmul(psC[:, 2 * P:2 * P + TILES], before[:], cnt[:], start=True, stop=True).then_inc(s_hm, 1)
            with pe.Fori(HLOOP, (PAIRS - 1) // 2 - 1) as u:
                for k in range(2):
                    pair(u * 2 + (k + 1), (k + 1) % 2)
            pair(PAIRS - 2, 1)
            pair(PAIRS - 1, 0)
            layer2(PAIRS * EXPERTS - 1, EXPERTS - 1)

        @block.vector
        def _(v):
            c = Count(v, s_v)
            v.wait_ge(s_ei, 16)
            c.done(v.tensor_scalar(di[:, 1, :], di[:, 0, :], P - 1, None, ALU.bitwise_and))
            c.done(v.tensor_copy(lo[:], di[:, 1, :]))
            c.done(v.tensor_scalar(di[:, 1, :], di[:, 0, :], 7, None, ALU.arith_shift_right))
            c.done(v.tensor_copy(hi[:], di[:, 1, :]))
            v.wait_ge(s_pc, 5)
            v.wait_ge(s_w, 16 * WEIGHT_LOADS)

            def hots(q, first=False):
                if not first:
                    v.wait_ge(s_hm, q)
                for part, wide, t in ((lo, P, hot_lo), (hi, TILES, hot_hi)):
                    o = v.tensor_tensor(t[:], iota_b[:, None, 0:wide].to_broadcast([P, HCOLS, wide]),
                                        part[:, ds(q * HCOLS, HCOLS)][:, :, None].to_broadcast([P, HCOLS, wide]),
                                        ALU.is_equal)
                o.then_inc(s_hh, 1)

            def outs(n, e, i, first=False):
                v.wait_ge(s_l2, n + 1)
                if not first:
                    v.wait_ge(s_st[e], i * 16)
                v.tensor_tensor(yo[:, e, :, :], psO[e % 2][:], b2r[:, e:e + 1, :].to_broadcast([P, 2, FEAT]),
                                ALU.add).then_inc(s_yo, 1)

            def normalise(i, k):
                v.wait_ge(s_x[k], (i // 2) * 16 + 16 if isinstance(i, int) else i * 8 + (16 - 8 * k))
                if not isinstance(i, int) or i >= 1:
                    v.wait_ge(s_ty, i)
                for t in range(2):
                    o = v.tensor_scalar(yn[:, t, :], xd[:, k, t, :], m.mean[:, ds(i * 2 + t, 1)],
                                        m.rstd[:, ds(i * 2 + t, 1)], ALU.subtract, ALU.mult)
                o.then_inc(s_yn, 1)

            def out_of_psum(i, k):
                v.wait_ge(s_ty, i + 1)
                v.tensor_copy(yt[:, k, :, :], psY[:]).then_inc(s_yt, 1)

            def pair(i, k, first=False, between=None):
                more = not (isinstance(i, int) and i == PAIRS - 1)
                if more:
                    normalise(i + 1, 1 - k)
                for e in range(EXPERTS):
                    if e == 3 and between:
                        between()
                    outs(i * EXPERTS + e, e, i, first=first)
                    if e == 1 and more:
                        out_of_psum(i + 1, 1 - k)

            def positions():
                v.wait_ge(s_hm, HPIECES + 1)
                c.done(v.tensor_copy(cnt[:], psC[:, 0:TILES]))
                v.sem_inc(s_cnt, 1)
                v.wait_ge(s_hm, HPIECES + 2)
                c.done(v.tensor_copy(tot[:], psC[:, P:P + TILES]))
                c.done(v.tensor_tensor_scan(pos[:, 0, :], m.ones[:, 0:TILES], tot[:], 0.0, ALU.mult, ALU.add))
                c.done(v.tensor_tensor(pos[:, 0, :], pos[:, 0, :], tot[:], ALU.subtract))
                c.done(v.tensor_tensor(pos[:, 0, :], pos[:, 0, :], psC[:, 2 * P:2 * P + TILES], ALU.add))
                c.inc(v.tensor_scalar(m.has_edges[:], cnt[:], 0.5, None, ALU.is_gt))
                c.done(v.tensor_tensor(pos[:, 1, :], pos[:, 0, :], cnt[:], ALU.add))
                c.done(v.tensor_scalar(cnt[:], m.has_edges[:], -4.0 * GEDGES, 4.0 * GEDGES, ALU.mult, ALU.add))
                c.inc(v.tensor_tensor(m.first_pos[:], pos[:, 0, :], cnt[:], ALU.add))
                c.done(v.scalar_tensor_tensor(m.last_pos[:], pos[:, 1, :], -1.0, cnt[:], ALU.add, ALU.add))
                v.sem_inc(s_pos, 1)

            normalise(0, 0)
            out_of_psum(0, 0)
            hots(0, first=True)
            pair(0, 0, first=True)
            with v.Fori(0, HLOOP - 1) as u:
                for k in range(2):
                    hots(u * 2 + (k + 1))
                    pair(u * 2 + (k + 1), 1 - k)
            hots(HPIECES - 1)
            pair(HPIECES - 1, 1)
            pair(HPIECES, 0, between=positions)
            with v.Fori(HLOOP, (PAIRS - 1) // 2 - 1) as u:
                for k in range(2):
                    pair(u * 2 + (k + 1), 1 - k)
            pair(PAIRS - 2, 1)
            pair(PAIRS - 1, 0)


def segment_softmax(nc, sem, m):
    with ExitStack() as ctx:
        def sb(name, shape, dt=F32):
            return ctx.enter_context(nc.sbuf_tensor(name, shape, dt))

        adst = sb("adst", [P, GCOLS, HEADS])
        adfirst = sb("adfirst", [P, HEADS])
        e = sb("e", [P, HEADS, GCOLS])
        decay = sb("decay", [P, HEADS, GCOLS])
        limit = sb("limit", [P, GCOLS])
        tail = sb("tail", [P, 2, ROWF])
        tail_t = sb("tail_t", [ROWF, 2, P])
        carried = sb("carried", [ROWF, P + 1])
        cin = sb("cin", [P, 2, ROWF])
        whole = sb("whole", [P, 1])
        psT = ctx.enter_context(nc.psum_tensor("e_turn", [P, 512], F32))
        psB = ctx.enter_context(nc.psum_tensor("e_back", [P, 512], F32))

        s_ad, s_af = sem("e_adst"), sem("e_adst_first")
        s_v, s_t, s_a, s_ask, s_go = sem("e_vector"), sem("e_turned"), sem("e_scalar"), sem("e_ask_pe"), sem("e_ask_act")
        s_st = sem("e_stored")
        s_fin = sem("e_states_ready")
        states = m.states
        mx = states[:, :, ROWF:STATE]
        by_head = lambda a: a.rearrange("p j h -> p h j")

        block = ctx.enter_context(nc.Block())

        @block.sync
        def _(sp):
            sp.dma_start(adst[:], m.adst_first.rearrange("(p j) h -> p j h", p=P)).then_inc(s_ad, 16)
            sp.wait_ge(s_fin, 1)
            sp.dma_start(m.state_dram.rearrange("(p j) c -> p j c", p=P), states[:]).then_inc(s_st, 16)
            sp.wait_ge(s_st, 16)

        @block.gpsimd
        def _(pool):
            pool.indirect_dma_start(adfirst[:], None, m.adst_dram,
                                    bass.IndirectOffsetOnAxis(ap=m.dst_first[:], axis=0)).then_inc(s_af, 16)

        @block.scalar
        def _(act):
            act.wait_ge(s_go, 1)
            act.activation(decay[:], decay[:], ACT.Exp).then_inc(s_a, 1)
            act.activation(by_head(states[:, :, HE:ROWF]), e[:], ACT.Exp).then_inc(s_a, 1)
            act.wait_ge(s_go, 2)
            act.activation(tail[:, 1, 0:HEADS], tail[:, 1, 0:HEADS], ACT.Exp).then_inc(s_a, 1)

        @block.tensor
        def _(pe):
            for n, w in enumerate((HEADS, ROWF)):
                pe.wait_ge(s_ask, 2 * n + 1)
                for k in range(2):
                    t = pe.transpose(psT[0:w, k * P:(k + 1) * P], tail[:, k, 0:w], m.ident[:])
                t.then_inc(s_t, 1)
                pe.wait_ge(s_ask, 2 * n + 2)
                pe.transpose(psB[:, 0:w], carried[0:w, 0:P], m.ident[0:w, 0:w]).then_inc(s_t, 1)

        @block.vector
        def _(v):
            c = Count(v, s_v)

            def carry(n, w, start, op0, op1):
                v.sem_inc(s_ask, 1)
                v.wait_ge(s_t, 2 * n + 1)
                c.done(v.tensor_copy(tail_t[0:w, :, :], psT[0:w, 0:2 * P].rearrange("p (k n) -> p k n", k=2)))
                c.inc(v.memset(carried[0:w, 0:1], start))
                c.done(v.tensor_tensor_scan(carried[0:w, 1:P + 1], tail_t[0:w, 1, :], tail_t[0:w, 0, :], start,
                                            op0, op1))
                v.sem_inc(s_ask, 1)
                v.wait_ge(s_t, 2 * n + 2)
                c.done(v.tensor_copy(cin[:, n, 0:w], psB[:, 0:w]))

            v.wait_ge(s_ad, 16)
            v.wait_ge(s_af, 16)
            c.inc(v.memset(m.seg_keep[:, 0:1], 0.0))
            c.inc(v.tensor_copy(adst[:, 0, :], adfirst[:]))
            c.done(v.tensor_tensor(whole[:], m.link[:, 0:1], m.link[:, 1:2], ALU.mult))
            for h in range(HEADS):
                c.inc(v.tensor_tensor_scan(adst[:, :, h], m.seg_keep[:], adst[:, :, h], 0.0, ALU.mult, ALU.add))
            c.inc(v.tensor_scalar(limit[:], m.seg_keep[:], 2 * BIG, -BIG, ALU.mult, ALU.add))
            v.wait_ge(s_v, c.n)
            c.done(v.tensor_tensor(e[:], by_head(states[:, :, HE:ROWF]), by_head(adst[:]), ALU.add))
            c.done(v.scalar_tensor_tensor(e[:], e[:], SLOPE, e[:], ALU.mult, ALU.max))
            for h in range(HEADS):
                c.inc(v.tensor_tensor_scan(mx[:, :, h], limit[:], e[:, h, :], -BIG, ALU.min, ALU.max))
            v.wait_ge(s_v, c.n)
            c.inc(v.tensor_copy(tail[:, 0, 0:HEADS], mx[:, GCOLS - 1, :]))
            c.inc(v.tensor_scalar(tail[:, 1, 0:HEADS], whole[:].to_broadcast([P, HEADS]), 2 * BIG, -BIG,
                                  ALU.mult, ALU.add))
            c.inc(v.tensor_scalar(limit[:, 0:1], m.link[:, 0:1], 2 * BIG, -BIG, ALU.mult, ALU.add))
            c.done(v.tensor_copy(m.seg_keep[:, 0:1], m.link[:, 0:1]))
            carry(0, HEADS, -BIG, ALU.min, ALU.max)
            for h in range(HEADS):
                c.inc(v.tensor_tensor_scan(mx[:, :, h], limit[:], e[:, h, :], cin[:, 0, h:h + 1], ALU.min, ALU.max))
            v.wait_ge(s_v, c.n)
            c.inc(v.tensor_tensor(decay[:, :, 1:GCOLS], by_head(mx[:, 0:GCOLS - 1, :]), by_head(mx[:, 1:GCOLS, :]),
                                  ALU.subtract))
            c.inc(v.tensor_tensor(decay[:, :, 0], cin[:, 0, 0:HEADS], mx[:, 0, :], ALU.subtract))
            c.inc(v.tensor_tensor(e[:], e[:], by_head(mx), ALU.subtract))
            c.inc(v.tensor_tensor(tail[:, 1, 0:HEADS], cin[:, 0, 0:HEADS], mx[:, GCOLS - 1, :], ALU.subtract))
            v.wait_ge(s_v, c.n)
            c.inc(v.tensor_scalar(tail[:, 1, 0:HEADS], tail[:, 1, 0:HEADS], 0.0, None, ALU.min))
            c.done(v.tensor_scalar(decay[:], decay[:], 0.0, None, ALU.min))
            v.sem_inc(s_go, 1)
            v.sem_inc(s_go, 1)
            v.wait_ge(s_a, 1)
            c.inc(v.tensor_tensor(decay[:], decay[:], m.seg_keep[:, None, :].to_broadcast([P, HEADS, GCOLS]),
                                  ALU.mult))
            v.wait_ge(s_a, 2)
            msg = states[:, :, 0:HE].rearrange("p j (h x) -> p j h x", x=EXPERTS)
            c.done(v.tensor_tensor(msg, msg, states[:, :, HE:ROWF][:, :, :, None].to_broadcast(
                [P, GCOLS, HEADS, EXPERTS]), ALU.mult))
            head = [ch // EXPERTS if ch < HE else ch - HE for ch in range(ROWF)]
            for q in range(ROWF // HEADS):
                for k in range(HEADS):
                    ch = q * HEADS + k
                    c.inc(v.tensor_tensor_scan(e[:, k, :], decay[:, head[ch], :], states[:, :, ch], 0.0,
                                               ALU.mult, ALU.add))
                v.wait_ge(s_v, c.n)
                c.done(v.tensor_copy(tail[:, 0, q * HEADS:(q + 1) * HEADS], e[:, :, GCOLS - 1]))
            v.wait_ge(s_a, 3)
            c.done(v.tensor_scalar(cin[:, 1, 0:HEADS], tail[:, 1, 0:HEADS], whole[:, 0:1], None, ALU.mult))
            c.inc(v.tensor_copy(tail[:, 1, 0:HE].rearrange("p (h x) -> p h x", x=EXPERTS),
                                cin[:, 1, 0:HEADS][:, :, None].to_broadcast([P, HEADS, EXPERTS])))
            c.done(v.tensor_copy(tail[:, 1, HE:ROWF], cin[:, 1, 0:HEADS]))
            carry(1, ROWF, 0.0, ALU.mult, ALU.add)
            for ch in range(ROWF):
                c.inc(v.tensor_tensor_scan(states[:, :, ch], decay[:, head[ch], :], states[:, :, ch],
                                           cin[:, 1, ch:ch + 1], ALU.mult, ALU.add))
            v.wait_ge(s_v, c.n)
            v.sem_inc(s_fin, 1)


def combine(nc, sem, b_gat, gamma, beta, out, m):
    with ExitStack() as ctx:
        def sb(name, shape, dt=F32):
            return ctx.enter_context(nc.sbuf_tensor(name, shape, dt))

        T = TILES
        SLOTS = 7
        PAIRS = T // 2
        ROUNDS = PAIRS // SLOTS
        assert PAIRS % SLOTS == 0
        got = sb("f_got", [P, 2, CH, STATE])
        idx = sb("f_idx", [P, 2, CH], I32)
        ns = sb("ns", [P, T, STATE])
        mxm = sb("mxm", [P, T, HEADS])
        e0 = sb("e0", [P, T, HEADS])
        top_ = sb("top_", [P, T, HEADS])
        w1 = sb("f_w1", [P, T, HEADS])
        w0 = sb("f_w0", [P, T, HEADS])
        den = sb("den", [P, T, HEADS])
        num = sb("num", [P, T, HE])
        tmp = sb("f_tmp", [P, T, HE])
        vec = sb("vec", [P, 3, HE])
        one = sb("one", [P, 4, T])
        sc = sb("sc", [P, T, EXPERTS])
        rank = sb("rank", [P, T, EXPERTS])
        ge = sb("f_ge", [P, T, EXPERTS])
        ys = sb("ys", [P, SLOTS, 2, EXPERTS, FEAT])
        xs = sb("xs", [P, SLOTS, 2, FEAT])

        s_c, s_i = sem("f_const"), sem("f_idx_ready")
        s_got = [sem("f_gathered0"), sem("f_gathered1")]
        s_past = sem("f_past")
        s_ns, s_mv = sem("f_states_ready"), sem("f_moved")
        s_v, s_go, s_a = sem("f_vector"), sem("f_ask_act"), sem("f_act")
        s_in = [sem(f"f_loaded{k}") for k in range(SLOTS)]
        s_out = [sem(f"f_stored{k}") for k in range(SLOTS)]
        s_g, s_sum, s_done = sem("f_gates"), sem("f_summing"), sem("f_pair_done")

        y_t = m.y_dram.rearrange("(t p) e f -> p t e f", p=P)
        x1_t = m.x1_dram.rearrange("(t p) f -> p t f", p=P)
        out_t = out[0:FULL_TILES * P, :].rearrange("(t p) f -> p t f", p=P)
        block = ctx.enter_context(nc.Block())

        @block.sync
        def _(sp):
            for n, a in enumerate((b_gat, gamma, beta)):
                sp.dma_start(vec[:, n, :], a.rearrange("(o c) -> o c", o=1).to_broadcast([P, HE])).then_inc(s_c, 16)

            def load(i, k):
                sp.dma_start(ys[:, k, :, :, :], y_t[:, ds(i * (2 * SLOTS) + 2 * k, 2), :, :]).then_inc(s_in[k], 16)
                sp.dma_start(xs[:, k, :, :], x1_t[:, ds(i * (2 * SLOTS) + 2 * k, 2), :]).then_inc(s_in[k], 16)

            for k in range(SLOTS):
                load(0, k)
            with sp.Fori(1, ROUNDS) as i:
                for k in range(SLOTS):
                    sp.wait_ge(s_out[k], i * 16)
                    load(i, k)

        @block.gpsimd
        def _(pool):
            pool.memset(got[:], 0.0).then_inc(s_i, 1)
            pool.wait_ge(s_i, 1)

            def fetch(i, k):
                pool.tensor_copy(idx[:, k, :], m.last_pos[:, ds((i * 2 + k) * CH, CH)]).then_inc(s_i, 1)
                pool.wait_ge(s_i, i * 2 + (k + 2))
                pool.sem_inc(s_past, 1)
                for j in range(CH):
                    pool.indirect_dma_start(got[:, k, j, :], None, m.state_dram,
                                            bass.IndirectOffsetOnAxis(ap=idx[:, k, j:j + 1], axis=0),
                                            bounds_check=GEDGES - 1, oob_is_err=False).then_inc(s_got[k], 16)

            def move(i, k):
                pool.wait_ge(s_got[k], i * (16 * CH) + 16 * CH)
                pool.tensor_copy(ns[:, ds((i * 2 + k) * CH, CH), :], got[:, k, :, :]).then_inc(s_mv, 1)
                pool.wait_ge(s_mv, i * 2 + (k + 1))
                pool.sem_inc(s_past, 1)

            fetch(0, 0)
            with pool.Fori(0, CHUNKS // 2 - 1) as i:
                fetch(i, 1)
                move(i, 0)
                fetch(i + 1, 0)
                move(i, 1)
            fetch(CHUNKS // 2 - 1, 1)
            move(CHUNKS // 2 - 1, 0)
            move(CHUNKS // 2 - 1, 1)
            pool.sem_inc(s_ns, 1)

        @block.scalar
        def _(act):
            act.wait_ge(s_go, 1)
            act.activation(w1[:], w1[:], ACT.Exp).then_inc(s_a, 1)
            act.activation(w0[:], w0[:], ACT.Exp).then_inc(s_a, 1)
            act.wait_ge(s_go, 2)
            act.activation(one[:, 1, :], one[:, 1, :], ACT.Sqrt, bias=m.eps[:, 0:1]).then_inc(s_a, 1)
            act.wait_ge(s_go, 3)
            act.activation(ge[:], ge[:], ACT.Exp).then_inc(s_a, 1)

            def store(i, k):
                act.wait_ge(s_done, i * SLOTS + (k + 1))
                act.dma_start(out_t[:, ds(i * (2 * SLOTS) + 2 * k, 2), :], xs[:, k, :, :]).then_inc(s_out[k], 16)

            with act.Fori(0, ROUNDS - 1) as i:
                for k in range(SLOTS):
                    store(i, k)
            for k in range(SLOTS - 1):
                store(ROUNDS - 1, k)
            k = SLOTS - 1
            act.wait_ge(s_done, PAIRS)
            act.dma_start(out_t[:, T - 2, :], xs[:, k, 0, :]).then_inc(s_out[k], 16)
            act.dma_start(out[FULL_TILES * P:NODES, :], xs[0:LAST_ROWS, k, 1, :]).then_inc(s_out[k], 16)
            for k in range(SLOTS):
                act.wait_ge(s_out[k], 16 * (ROUNDS + (k == SLOTS - 1)))

        @block.vector
        def _(v):
            c = Count(v, s_v)
            heads4 = lambda a: a[:, :, :, None].to_broadcast([P, T, HEADS, EXPERTS])
            wide = lambda a: a.rearrange("p t (h x) -> p t h x", x=EXPERTS)
            per16 = lambda a: a[:, :, None].to_broadcast([P, T, HE])
            row = lambda n: vec[:, n:n + 1, :].to_broadcast([P, T, HE])
            has4 = m.has_edges[:, :, None].to_broadcast([P, T, HEADS])

            c.done(v.tensor_tensor(e0[:], m.node_row[:, :, HE:ROWF], m.node_dst[:], ALU.add))
            c.done(v.scalar_tensor_tensor(e0[:], e0[:], SLOPE, e0[:], ALU.mult, ALU.max))
            c.done(v.tensor_scalar(one[:, 0, :], m.has_edges[:], BIG, -BIG, ALU.mult, ALU.add))
            v.wait_ge(s_ns, 1)
            c.done(v.tensor_tensor(mxm[:], ns[:, :, ROWF:STATE], has4, ALU.mult))
            c.done(v.tensor_tensor(mxm[:], mxm[:], one[:, 0, :][:, :, None].to_broadcast([P, T, HEADS]), ALU.add))
            c.done(v.tensor_tensor(top_[:], mxm[:], e0[:], ALU.max))
            c.inc(v.tensor_tensor(w1[:], mxm[:], top_[:], ALU.subtract))
            c.done(v.tensor_tensor(w0[:], e0[:], top_[:], ALU.subtract))
            v.sem_inc(s_go, 1)
            v.wait_ge(s_a, 2)
            c.done(v.tensor_tensor(w1[:], w1[:], has4, ALU.mult))
            c.inc(v.tensor_tensor(wide(num[:]), wide(ns[:, :, 0:HE]), heads4(w1[:]), ALU.mult))
            c.inc(v.tensor_tensor(wide(tmp[:]), wide(m.node_row[:, :, 0:HE]), heads4(w0[:]), ALU.mult))
            c.done(v.tensor_tensor(den[:], ns[:, :, HE:ROWF], w1[:], ALU.mult))
            c.inc(v.tensor_tensor(num[:], num[:], tmp[:], ALU.add))
            c.done(v.tensor_tensor(den[:], den[:], w0[:], ALU.add))
            c.done(v.tensor_scalar(den[:], den[:], 1e-16, None, ALU.add))
            c.done(v.reciprocal(den[:], den[:]))
            c.done(v.tensor_tensor(wide(num[:]), wide(num[:]), heads4(den[:]), ALU.mult))
            v.wait_ge(s_c, 48)
            c.done(v.tensor_tensor(num[:], num[:], row(0), ALU.add))
            c.done(v.tensor_reduce(one[:, 0, :], num[:], AX_X, ALU.add))
            c.done(v.tensor_scalar(one[:, 0, :], one[:, 0, :], 1.0 / HE, None, ALU.mult))
            c.done(v.tensor_tensor(num[:], num[:], per16(one[:, 0, :]), ALU.subtract))
            c.done(v.tensor_tensor(tmp[:], num[:], num[:], ALU.mult))
            c.done(v.tensor_reduce(one[:, 1, :], tmp[:], AX_X, ALU.add))
            c.done(v.tensor_scalar(one[:, 1, :], one[:, 1, :], 1.0 / HE, None, ALU.mult))
            v.sem_inc(s_go, 1)
            v.wait_ge(s_a, 3)
            c.done(v.reciprocal(one[:, 1, :], one[:, 1, :]))
            c.done(v.tensor_tensor(num[:], num[:], per16(one[:, 1, :]), ALU.mult))
            c.done(v.tensor_tensor(num[:], num[:], row(1), ALU.mult))
            c.done(v.tensor_tensor(num[:], num[:], row(2), ALU.add))
            c.done(v.tensor_reduce(sc[:], num[:].rearrange("p t (h x) -> p t x h", x=EXPERTS), AX_X, ALU.add))
            c.done(v.tensor_scalar(sc[:], sc[:], 1.0 / HEADS, None, ALU.mult))
            c.done(v.memset(rank[:], 0.0))
            for a in range(EXPERTS - 1):
                n = EXPERTS - 1 - a
                c.done(v.tensor_tensor(ge[:, :, 0:n], sc[:, :, a:a + 1].to_broadcast([P, T, n]), sc[:, :, a + 1:EXPERTS],
                                       ALU.is_ge))
                c.inc(v.tensor_reduce(one[:, 2, :], ge[:, :, 0:n], AX_X, ALU.add))
                c.done(v.tensor_tensor(rank[:, :, a + 1:EXPERTS], rank[:, :, a + 1:EXPERTS], ge[:, :, 0:n], ALU.add))
                c.done(v.tensor_scalar(one[:, 2, :], one[:, 2, :], -1.0, float(n), ALU.mult, ALU.add))
                c.done(v.tensor_tensor(rank[:, :, a], rank[:, :, a], one[:, 2, :], ALU.add))
            c.done(v.tensor_scalar(rank[:], rank[:], 1.5, None, ALU.is_lt))
            c.done(v.tensor_reduce(one[:, 3, :], sc[:], AX_X, ALU.max))
            c.done(v.tensor_tensor(ge[:], sc[:], one[:, 3, :][:, :, None].to_broadcast([P, T, EXPERTS]), ALU.subtract))
            v.sem_inc(s_go, 1)
            v.wait_ge(s_a, 4)
            c.done(v.tensor_tensor(ge[:], ge[:], rank[:], ALU.mult))
            c.done(v.tensor_reduce(one[:, 3, :], ge[:], AX_X, ALU.add))
            c.done(v.reciprocal(one[:, 3, :], one[:, 3, :]))
            c.done(v.tensor_tensor(sc[:], ge[:], one[:, 3, :][:, :, None].to_broadcast([P, T, EXPERTS]), ALU.mult))
            base = c.n

            def pair(i, k):
                v.wait_ge(s_in[k], i * 32 + 32)
                for e in range(EXPERTS):
                    for t in range(2):
                        q = v.scalar_tensor_tensor(xs[:, k, t, :], ys[:, k, t, e, :],
                                                   sc[:, ds(i * (2 * SLOTS) + (2 * k + t), 1), e],
                                                   xs[:, k, t, :], ALU.mult, ALU.add)
                    if e < EXPERTS - 1:
                        q.then_inc(s_v, 1)
                        v.wait_ge(s_v, (i * SLOTS + k) * (EXPERTS - 1) + (base + e + 1))
                q.then_inc(s_done, 1)

            with v.Fori(0, ROUNDS) as i:
                for k in range(SLOTS):
                    pair(i, k)


_INS = ["x", "src", "dst", "edge_weight", "L0_gnn_W", "L0_gnn_b", "L0_ffn_W_gat", "L0_ffn_att_src",
        "L0_ffn_att_dst", "L0_ffn_b_gat", "L0_ffn_ln_gamma", "L0_ffn_ln_beta", "L0_ffn_W1", "L0_ffn_b1",
        "L0_ffn_W2", "L0_ffn_b2", "L0_ffn_edge_index"]


def kernel(**inputs):
    import numpy as _np
    import concourse.bacc as _bacc
    from concourse import mybir as _mybir
    from concourse.bass_utils import run_bass_kernel_spmd as _run

    nc = _bacc.Bacc("TRN2", target_bir_lowering=False, num_devices=1)
    arrays, args = {}, []
    for name in _INS:
        a = _np.ascontiguousarray(inputs[name])
        arrays[f"in_{name}"] = a
        args.append(nc.dram_tensor(f"in_{name}", a.shape, _mybir.dt.from_np(a.dtype), kind="ExternalInput").ap())
    out = nc.dram_tensor("out_0", (NODES, FEAT), F32, kind="ExternalOutput").ap()
    build(nc, *args, out)
    r = _run(nc, [arrays], core_ids=[0])
    return r.results[0]["out_0"]
```

```python
from contextlib import ExitStack

import concourse.bass as bass
from concourse import mybir

F32 = mybir.dt.float32
BF16 = mybir.dt.bfloat16
I32 = mybir.dt.int32
ALU = mybir.AluOpType
ACT = mybir.ActivationFunctionType
AX_X = mybir.AxisListType.X
ds = bass.ds

P = 128
NODES = 12500
FEAT = 256
TILES = -(-NODES // P)
NPAD = TILES * P
FULL_TILES = NODES // P
LAST_ROWS = NODES - FULL_TILES * P
CH = 7
CHUNKS = TILES // CH
LN_EPS = 1e-5

EDGES = 200000
ETILES = -(-EDGES // P)
GT = 4
GROUPS = -(-ETILES // GT)
EBLOCKS = -(-ETILES // P)
ECOLS = EBLOCKS * P
STEPS = GROUPS + TILES - 1
RING = 8
HALVES = FEAT // P

GEDGES = 131072
GCOLS = GEDGES // P
KEY_SHIFT = 14
KEY_TOP = 1 << 28
HCOLS = 32
HPIECES = GCOLS // HCOLS

HEADS, EXPERTS = 4, 4
HID = 2 * FEAT
HE = HEADS * EXPERTS
FB = HID // P
PAIRS = TILES // 2
N2 = 2 * P
EARLY_PAIRS = 39
SCAN_PAIRS = 4
ROWF = HE + HEADS
STATE = HE + 2 * HEADS
BIG = 1.5e38
SLOPE = 0.2


class Shared:
    pass


class Count:

    def __init__(self, eng, sem, start=0):
        self.eng, self.sem, self.n = eng, sem, start

    def inc(self, ins):
        self.n += 1
        return ins.then_inc(self.sem, 1)

    def done(self, ins):
        self.inc(ins)
        self.eng.wait_ge(self.sem, self.n)


def build(nc, x, src, dst, edge_weight, W, b, W_gat, att_src, att_dst, b_gat, gamma, beta,
          W1, b1, W2, b2, edge_index, out):
    m = Shared()

    def dram(name, shape):
        return nc.dram_tensor(name, shape, F32).ap()

    feats = dram("feats", (NPAD, FEAT))
    m.x1_dram = dram("x1_dram", (NPAD, FEAT))
    m.y_dram = dram("y_dram", (NPAD, EXPERTS, FEAT))
    m.row_dram = dram("row_dram", (NPAD, ROWF))
    m.adst_dram = dram("adst_dram", (NPAD, HEADS))
    m.adst_first = dram("adst_first", (GEDGES, HEADS))
    m.state_dram = dram("state_dram", (GEDGES, STATE))

    with ExitStack() as top:
        def sem(name):
            return top.enter_context(nc.semaphore(name))

        def keep(name, shape, dt=F32):
            return top.enter_context(nc.sbuf_tensor(name, shape, dt))

        m.ident = keep("ident", [P, P])
        m.ones = keep("ones", [P, P])
        m.iota = keep("iota", [P, P])
        m.eps = keep("eps", [P, 1])
        m.src_sorted = keep("src_sorted", [P, GCOLS], I32)
        m.seg_keep = keep("seg_keep", [P, GCOLS])
        m.dst_first = keep("dst_first", [P, 1], I32)
        m.link = keep("link", [P, 2])
        m.first_pos = keep("first_pos", [P, TILES], I32)
        m.last_pos = keep("last_pos", [P, TILES], I32)
        m.has_edges = keep("has_edges", [P, TILES])
        m.node_row = keep("node_row", [P, TILES, ROWF])
        m.node_dst = keep("node_dst", [P, TILES, HEADS])
        m.mean = keep("mean", [P, TILES])
        m.rstd = keep("rstd_all", [P, TILES])
        m.shift = keep("shift", [P, TILES])

        with ExitStack() as part1:
            def sb(name, shape, dt=F32):
                return part1.enter_context(nc.sbuf_tensor(name, shape, dt))

            m.dst_t = sb("dst_t", [P, ECOLS])
            m.src_t = sb("src_t", [P, ECOLS], I32)
            m.ew_t = sb("ew_t", [P, ECOLS])
            m.step_group = sb("step_group", [P, STEPS], I32)
            m.step_tile = sb("step_tile", [P, STEPS], I32)
            m.step_code = sb("step_code", [P, STEPS], I32)
            m.step_base = sb("step_base", [P, STEPS])
            m.group_end = sb("group_end", [P, GROUPS], I32)
            layernorm_and_plan(nc, sem, x, src, dst, edge_weight, feats, m)
            weighted_sums(nc, sem, feats, edge_index, x, W, b, W_gat, m)
            attention_terms(nc, sem, att_src, att_dst, m)
        m.w1 = keep("w1", [P, HALVES, EXPERTS, HID])
        m.w2 = keep("w2", [P, FB, EXPERTS, FEAT])
        m.b1c = keep("b1c", [P, EXPERTS, FB])
        m.b2r = keep("b2r", [P, EXPERTS, FEAT])
        with nc.sbuf_tensor("states", [P, GCOLS, STATE], F32) as states:
            m.states = states
            gather_and_experts(nc, sem, W1, b1, W2, b2, edge_index, m)
            segment_softmax(nc, sem, m)
        combine(nc, sem, b_gat, gamma, beta, out, m)


def layernorm_and_plan(nc, sem, x, src, dst, ew, feats, m):
    with ExitStack() as ctx:
        def sb(name, shape, dt):
            return ctx.enter_context(nc.sbuf_tensor(name, shape, dt))

        XB = 4
        xin = sb("xin", [P, XB, CH, FEAT], F32)
        xout = sb("xout", [P, XB, CH, FEAT], F32)
        stats = sb("stats", [P, XB, CH, 6], F32)
        mv = sb("mv", [P, XB, CH, 2], F32)
        rstd = sb("rstd", [P, XB, CH], F32)
        shift = sb("a_shift", [P, XB, CH], F32)
        lent = sb("raw", [P, 5 * ECOLS], F32)
        raw_i = lent[:, 0:2 * ECOLS].bitcast(I32).rearrange("p (a b e) -> p a b e", a=2, e=P)
        raw_f = lent[:, 2 * ECOLS:5 * ECOLS].rearrange("p (a b e) -> p a b e", a=3, e=P)
        last_sel = sb("last_sel", [P, P], F32)
        gi = sb("gi", [P, GROUPS], I32)
        gf = sb("gf", [P, GROUPS], F32)
        ge = sb("ge", [P, GROUPS], F32)
        giota = sb("giota", [P, STEPS], F32)
        gend = sb("gend", [P, 4], F32)
        last = sb("last", [P, STEPS], I32)
        odd = sb("odd", [P, STEPS], I32)
        spent = lent[:, 2 * ECOLS:5 * ECOLS]
        passed = spent[:, 0:4 * STEPS].rearrange("p (q s) -> p q s", q=4)
        gdiag = spent[:, 4 * STEPS:4 * STEPS + 4 * P].rearrange("p (q n) -> p q n", q=4)
        stepf = spent[:, 4 * STEPS + 4 * P:6 * STEPS + 4 * P].rearrange("p (q s) -> p q s", q=2)
        turn = ctx.enter_context(nc.psum_tensor("turn", [P, 2, 2048], F32))

        s_const, s_raw0, s_raw = sem("a_const"), sem("a_raw_cleared"), sem("a_raw_loaded")
        s_xin = [sem(f"a_x{k}") for k in range(XB)]
        s_out = [sem(f"a_out{k}") for k in range(XB)]
        s_scale = sem("a_scale")
        s_clear = sem("a_x_cleared")
        s_past = sem("a_past")
        s_var, s_std, s_norm = sem("a_var"), sem("a_std"), sem("a_norm")
        s_rcp = sem("a_reciprocal")
        s_v, s_t, s_ev = sem("a_statistics"), sem("a_turned"), sem("a_turn_read")
        s_pl = sem("a_pool")
        s_edge = sem("a_edge_vector")

        x_tiles = x[0:FULL_TILES * P, :].rearrange("(t p) f -> p t f", p=P)
        f_tiles = feats.rearrange("(t p) f -> p t f", p=P)
        main = (EBLOCKS - 1) * P * P
        rest = (EDGES - main) // P
        tail = EDGES - main - rest * P

        block = ctx.enter_context(nc.Block())

        @block.sync
        def _(sp):
            def load(n, k):
                if isinstance(n, int) and n == CHUNKS - 1:
                    sp.dma_start(xin[:, k, 0:CH - 1, :], x_tiles[:, n * CH:FULL_TILES, :]).then_inc(s_xin[k], 16)
                    sp.wait_ge(s_clear, 1)
                    sp.dma_start(xin[0:LAST_ROWS, k, CH - 1, :], x[FULL_TILES * P:NODES, :]).then_inc(s_xin[k], 16)
                else:
                    sp.dma_start(xin[:, k, :, :], x_tiles[:, ds(n * CH, CH), :]).then_inc(s_xin[k], 16)

            def store(n, k):
                sp.wait_ge(s_norm, n + 1)
                sp.dma_start(f_tiles[:, ds(n * CH, CH), :], xout[:, k, :, :]).then_inc(s_out[k], 16)

            for k in range(XB):
                load(k, k)
            FULL = (CHUNKS - 1) // XB - 1
            with sp.Fori(0, FULL) as i:
                for k in range(XB):
                    store(i * XB + k, k)
                    load(i * XB + (k + XB), k)
            for n in range(FULL * XB, CHUNKS):
                store(n, n % XB)
                if n + XB < CHUNKS:
                    load(n + XB, n % XB)
            for k in range(XB):
                sp.wait_ge(s_out[k], 16 * len(range(k, CHUNKS, XB)))

        @block.gpsimd
        def _(pool):
            pool.memset(raw_i[:, 0, :, :], -1).then_inc(s_raw0, 1)
            pool.memset(raw_i[:, 1, :, :], 0).then_inc(s_raw0, 1)
            pool.memset(raw_f[:, 2, :, :], 0.0).then_inc(s_raw0, 1)
            c = Count(pool, s_pl)
            c.inc(pool.memset(m.ident[:], 0.0))
            c.inc(pool.memset(m.ones[:], 1.0))
            c.inc(pool.memset(last_sel[:], 0.0))
            pool.memset(m.eps[:], LN_EPS).then_inc(s_const, 1)
            pool.iota(m.iota[:], pattern=[[1, P]], base=0, channel_multiplier=0,
                      allow_small_or_imprecise_dtypes=True).then_inc(s_const, 1)
            pool.iota(giota[:], pattern=[[1, STEPS]], base=0, channel_multiplier=0,
                      allow_small_or_imprecise_dtypes=True).then_inc(s_const, 1)
            pool.wait_ge(s_pl, c.n)
            pool.affine_select(out=m.ident[:], in_=m.ident[:], compare_op=ALU.not_equal, fill=1.0, base=0,
                               pattern=[[-1, P]], channel_multiplier=1).then_inc(s_const, 1)
            pool.affine_select(out=last_sel[:], in_=last_sel[:], compare_op=ALU.not_equal, fill=1.0,
                               base=1 - P, pattern=[[0, P]], channel_multiplier=1).then_inc(s_const, 1)

        @block.scalar
        def _(act):
            act.wait_ge(s_raw0, 3)
            for a, t in ((dst, raw_i[:, 0]), (src, raw_i[:, 1]), (ew, raw_f[:, 2])):
                act.dma_start(t[:, 0:EBLOCKS - 1, :],
                              a[0:main].rearrange("(b q e) -> q b e", q=P, e=P)).then_inc(s_raw, 16)
                act.dma_start(t[0:rest, EBLOCKS - 1, :],
                              a[main:main + rest * P].rearrange("(q e) -> q e", e=P)).then_inc(s_raw, 16)
                act.dma_start(t[rest:rest + 1, EBLOCKS - 1, 0:tail],
                              a[main + rest * P:EDGES].rearrange("(q e) -> q e", q=1)).then_inc(s_raw, 16)

            def deviation(n, k):
                act.wait_ge(s_var, n + 1)
                act.activation(rstd[:, k, :], mv[:, k, :, 1], ACT.Sqrt, bias=m.eps[:, 0:1]).then_inc(s_std, 1)

            def normalise(n, k):
                act.wait_ge(s_scale, n + 1)
                if not isinstance(n, int) or n >= XB:
                    act.wait_ge(s_out[k], n * (16 // XB) - k * (16 // XB))
                    act.sem_inc(s_past, 1)
                for t in range(CH):
                    q = act.activation(xout[:, k, t, :], xin[:, k, t, :], ACT.Identity,
                                       scale=rstd[:, k, t:t + 1], bias=shift[:, k, t:t + 1])
                q.then_inc(s_norm, 1)

            act.wait_ge(s_const, 1)
            deviation(0, 0)
            for n in range(XB):
                deviation(n + 1, (n + 1) % XB)
                normalise(n, n)
            with act.Fori(1, CHUNKS // XB) as i:
                for k in range(XB):
                    deviation(i * XB + (k + 1), (k + 1) % XB)
                    normalise(i * XB + k, k)
            for n in range(CHUNKS // XB * XB, CHUNKS):
                if n + 1 < CHUNKS:
                    deviation(n + 1, (n + 1) % XB)
                normalise(n, n % XB)

        @block.vector
        def _(v):
            c = Count(v, s_edge)

            def statistics(n, k):
                last = isinstance(n, int) and n == CHUNKS - 1
                v.wait_ge(s_xin[k], n * (16 // XB) + (32 if last else 16) - k * (16 // XB))
                v.sem_inc(s_past, 1)
                for t in range(CH):
                    q = v.bn_stats(stats[:, k, t, :], xin[:, k, t, :])
                q.then_inc(s_v, 1)
                v.wait_ge(s_v, n + 1)
                v.sem_inc(s_past, 1)
                for t in range(CH):
                    q = v.bn_aggr(mv[:, k, t, :], stats[:, k, t, :])
                q.then_inc(s_var, 1)

            def scale(n, k):
                v.wait_ge(s_std, n + 1)
                v.reciprocal(rstd[:, k, :], rstd[:, k, :]).then_inc(s_rcp, 1)
                v.wait_ge(s_rcp, n + 1)
                v.scalar_tensor_tensor(shift[:, k, :], mv[:, k, :, 0], -1.0, rstd[:, k, :], ALU.mult, ALU.mult
                                       ).then_inc(s_scale, 1)

            statistics(0, 0)
            statistics(1, 1)
            scale(0, 0)
            v.wait_ge(s_raw, 9 * 16)
            for a in range(2):
                c.inc(v.tensor_copy(raw_f[:, a, :, :], raw_i[:, a, :, :]))
            statistics(2, 2)
            scale(1, 1)
            for n, t in enumerate((m.dst_t, m.src_t, m.ew_t)):
                v.wait_ge(s_t, n + 1)
                c.inc(v.tensor_copy(t[:], turn[:, n % 2, 0:ECOLS]))
                v.wait_ge(s_edge, c.n)
                v.sem_inc(s_ev, 1)
            v.wait_ge(s_t, 4)
            c.done(v.tensor_copy(gi[:], turn[:, 1, 0:GROUPS]))
            c.done(v.tensor_scalar(gi[:], gi[:], 7, None, ALU.arith_shift_right))
            c.done(v.tensor_copy(gf[:], gi[:]))
            c.done(v.memset(gf[:, GROUPS - 1:GROUPS], float(TILES - 1)))
            v.wait_ge(s_const, 5)
            c.done(v.tensor_tensor(ge[:], gf[:], giota[:, 0:GROUPS], ALU.add))
            c.inc(v.tensor_scalar(m.group_end[:], ge[:], 1.0, None, ALU.add))
            for q in range(4):
                w = min(P, GROUPS - q * P)
                c.inc(v.tensor_tensor(gdiag[:, q, 0:w], ge[:, q * P:q * P + w], m.ident[:, 0:w], ALU.mult))
            v.wait_ge(s_edge, c.n)
            for q in range(4):
                w = min(P, GROUPS - q * P)
                c.inc(v.tensor_reduce(gend[:, q:q + 1], gdiag[:, q, 0:w], AX_X, ALU.add))
            v.wait_ge(s_edge, c.n)
            for q in range(4):
                c.inc(v.tensor_scalar(passed[:, q, :], giota[:], gend[:, q:q + 1], None, ALU.is_gt))
            v.wait_ge(s_edge, c.n)
            v.sem_inc(s_ev, 1)
            statistics(3, 3)
            scale(2, 2)
            v.wait_ge(s_t, 5)
            c.done(v.tensor_copy(stepf[:, 0, :], turn[:, 0, 0:STEPS]))
            c.inc(v.tensor_copy(m.step_group[:], stepf[:, 0, :]))
            c.done(v.tensor_tensor(stepf[:, 1, :], giota[:], stepf[:, 0, :], ALU.subtract))
            c.inc(v.tensor_copy(m.step_tile[:], stepf[:, 1, :]))
            c.inc(v.tensor_tensor(last[:, 0:STEPS - 1], stepf[:, 1, 1:STEPS], stepf[:, 1, 0:STEPS - 1],
                                  ALU.subtract))
            c.inc(v.memset(last[:, STEPS - 1:STEPS], 1))
            c.inc(v.tensor_scalar(m.step_base[:], stepf[:, 1, :], float(P), None, ALU.mult))
            v.wait_ge(s_edge, c.n)
            c.inc(v.tensor_scalar(odd[:], m.step_tile[:], 1, 1, ALU.bitwise_and, ALU.logical_shift_left))
            c.done(v.tensor_scalar(m.step_code[:], m.step_group[:], 2, None, ALU.logical_shift_left))
            c.done(v.tensor_tensor(m.step_code[:], m.step_code[:], odd[:], ALU.bitwise_or))
            c.done(v.tensor_tensor(m.step_code[:], m.step_code[:], last[:], ALU.bitwise_or))
            v.sem_inc(s_ev, 1)

            with v.Fori(1, CHUNKS // XB) as i:
                for k in range(XB):
                    statistics(i * XB + k, k)
                    scale(i * XB + (k - 1), (k - 1) % XB)
            for n in range(CHUNKS // XB * XB, CHUNKS):
                if n == CHUNKS - 1:
                    v.wait_ge(s_norm, n - XB + 1)
                    v.memset(xin[:, n % XB, CH - 1, :], 0.0).then_inc(s_clear, 1)
                statistics(n, n % XB)
                scale(n - 1, (n - 1) % XB)
            scale(CHUNKS - 1, (CHUNKS - 1) % XB)
            v.wait_ge(s_norm, CHUNKS)
        @block.tensor
        def _(pe):
            pe.wait_ge(s_edge, 2)
            pe.wait_ge(s_const, 5)
            for n in range(3):
                if n == 2:
                    pe.wait_ge(s_ev, 1)
                for q in range(EBLOCKS):
                    t = pe.transpose(turn[:, n % 2, q * P:(q + 1) * P], raw_f[:, n, q, :], m.ident[:])
                t.then_inc(s_t, 1)
            pe.wait_ge(s_ev, 2)
            pe.matmul(turn[:, 1, 0:GROUPS], last_sel[:], m.dst_t[:, GT - 1:GROUPS * GT:GT],
                      start=True, stop=True).then_inc(s_t, 1)
            pe.wait_ge(s_ev, 4)
            for q in range(4):
                w = min(P, GROUPS - q * P)
                t = pe.matmul(turn[:, 0, 0:STEPS], m.ones[0:w, :], passed[0:w, q, :], start=(q == 0), stop=(q == 3))
            t.then_inc(s_t, 1)


def weighted_sums(nc, sem, feats, edge_index, x, W, b, W_gat, m):
    XS = 4
    with ExitStack() as ctx:
        def sb(name, shape, dt=F32):
            return ctx.enter_context(nc.sbuf_tensor(name, shape, dt))

        def pb(name, cols=512):
            return ctx.enter_context(nc.psum_tensor(name, [P, cols], F32))

        rows = sb("rows", [P, RING, GT, FEAT])
        idx = sb("idx", [P, 2, RING, GT], I32)
        rel = sb("rel", [P, XS, GT])
        hot = sb("hot", [P, XS, GT, P])
        key = [m.seg_keep[:], m.src_sorted[:].bitcast(F32), sb("key", [P, GCOLS])[:]]
        key_i = [m.seg_keep[:].bitcast(I32), m.src_sorted[:], key[2].bitcast(I32)]
        sign = sb("sign", [P, 2])
        shift_dn = sb("shift_dn", [P, P])
        lastd = sb("lastd", [P, 2])
        w_raw = sb("w_raw", [P, HALVES, FEAT])
        w_t = sb("w_t", [P, HALVES, FEAT])
        wg = sb("wg", [P, HALVES, HE])
        brow = sb("brow", [1, FEAT])
        zero_b = sb("b_zeros", [1, FEAT], BF16)
        sums = sb("sums", [P, FEAT])
        sums_t = sb("sums_t", [P, FEAT])
        xs = sb("x_ring", [P, XS, FEAT])
        x1 = sb("x1", [P, 2, FEAT])
        xc = sb("xc", [P, FEAT])
        xc_t = sb("xc_t", [P, FEAT])
        squares = sb("squares", [P, FEAT])
        psA = pb("node_sums", 1024)
        psT = pb("turned", GCOLS)
        psS, psX, psY, psH = pb("sums_turned"), pb("x1_product"), pb("xc_turned"), pb("h_product")

        s_ei = sem("b_edge_index")
        s_idx, s_ready = sem("b_idx_ready"), sem("b_rows_ready")
        s_got = [sem(f"b_gathered{k}") for k in range(RING)]
        s_past = sem("b_past")
        s_rel, s_hot, s_mm = sem("b_rel"), sem("b_hot_ready"), sem("b_step_multiplied")
        s_s = sem("b_sort")
        s_turn, s_turned = sem("b_turn_ask"), sem("b_turned")
        s_pc = sem("b_pool_const")
        s_w, s_wt, s_wte = sem("b_weights"), sem("b_w_turned"), sem("b_w_ready")
        s_tile = sem("b_tile_summed")
        s_evac = sem("b_tile_out_of_psum")
        s_a = sem("b_scalar")
        s_xin, s_x1o = sem("b_x_loaded"), [sem("b_x1_stored0"), sem("b_x1_stored1")]

        block = ctx.enter_context(nc.Block())
        full_rounds = GROUPS // RING
        left = GROUPS - full_rounds * RING
        QUADS = STEPS // XS
        PIECES = 24
        CUT = [1 + (QUADS - 1) * n // (PIECES + 9) for n in range(PIECES + 1)] + [QUADS]
        assert STEPS % XS == 0 and TILES % 2 == 0 and full_rounds % 2 == 0 and RING == 8

        turned_keys, cur = [], 2
        for k in range(1, 18):
            if k >= 11:
                turned_keys.append(cur)
                cur = 1 if cur != 1 else 0
                for _ in range(k - 10):
                    cur = 1 - cur
                turned_keys.append(cur)
                cur = 1 - cur
                for _ in range(10):
                    cur = 1 - cur
            else:
                for _ in range(k):
                    cur = 1 if cur == 2 else 1 - cur

        @block.sync
        def _(sp):
            sp.dma_start(key_i[0], edge_index[1, :].rearrange("(p j) -> p j", p=P)).then_inc(s_ei, 16)
            sp.dma_start(key_i[1], edge_index[0, :].rearrange("(p j) -> p j", p=P)).then_inc(s_ei, 16)
            sp.dma_start(w_raw[:], W.rearrange("(o p) i -> p o i", p=P)).then_inc(s_w, 16)
            sp.dma_start(wg[:], W_gat.rearrange("(k p) c -> p k c", p=P)).then_inc(s_w, 16)
            sp.dma_start(brow[:], b.rearrange("(a n) -> a n", a=1)).then_inc(s_w, 16)
            with sp.Fori(1, full_rounds + 1) as i:
                for k in range(RING):
                    sp.wait_ge(s_got[k], i * (16 * GT))
                    sp.sem_inc(s_ready, 1)
            for k in range(left):
                sp.wait_ge(s_got[k], (full_rounds + 1) * 16 * GT)
                sp.sem_inc(s_ready, 1)

        @block.gpsimd
        def _(pool):
            def indices(i, half):
                pool.tensor_copy(idx[:, half, :, :].rearrange("p r t -> p (r t)"),
                                 m.src_t[:, ds(i * (RING * GT), RING * GT)]).then_inc(s_idx, 1)
                pool.wait_ge(s_idx, i + 1)
                pool.sem_inc(s_past, 1)

            def gather(k, half):
                for j in range(GT):
                    pool.indirect_dma_start(rows[:, k, j, :], None, feats,
                                            bass.IndirectOffsetOnAxis(ap=idx[:, half, k, j:j + 1], axis=0)
                                            ).then_inc(s_got[k], 16)

            def refill(i, k, half):
                end = pool.value_load(m.group_end[0:1, ds(i * RING + (k - RING), 1)], min_val=1, max_val=STEPS)
                pool.wait_ge(s_mm, end)
                pool.sem_inc(s_past, 1)
                gather(k, half)

            indices(0, 0)
            for k in range(RING):
                gather(k, 0)
            c = Count(pool, s_pc)
            c.inc(pool.memset(zero_b[:], 0.0))
            c.inc(pool.memset(shift_dn[:], 0.0))
            c.inc(pool.iota(sign[:, 1:2], pattern=[[0, 1]], base=0, channel_multiplier=1,
                            allow_small_or_imprecise_dtypes=True))
            pool.wait_ge(s_pc, c.n)
            for t in (sums, sums_t, xc, xc_t, xs[:, 2:XS, :]):
                c.inc(pool.memset(t[:], 0.0))
            c.inc(pool.affine_select(out=shift_dn[:], in_=shift_dn[:], compare_op=ALU.not_equal, fill=1.0,
                                     base=1, pattern=[[-1, P]], channel_multiplier=1))
            with pool.Fori(0, full_rounds // 2 - 1) as u:
                for half in (1, 0):
                    i = u * 2 + (2 - half)
                    indices(i, half)
                    for k in range(RING):
                        refill(i, k, half)
            i = full_rounds - 1
            indices(i, 1)
            for k in range(RING):
                refill(i, k, 1)
            indices(full_rounds, 0)
            for k in range(left):
                refill(full_rounds, k, 0)

        @block.scalar
        def _(act):
            def load(d, slot):
                if isinstance(d, int) and d == TILES - 1:
                    act.dma_start(xs[0:LAST_ROWS, slot, :], x[FULL_TILES * P:NODES, :]).then_inc(s_xin, 16)
                else:
                    act.dma_start(xs[:, slot, :], x[0:FULL_TILES * P, :].rearrange("(t p) f -> t p f", p=P)[
                        ds(d, 1), :, :].rearrange("t p f -> p (t f)")).then_inc(s_xin, 16)

            def tile(j, r):
                real = isinstance(j, int)
                par = r % 2
                act.wait_ge(s_tile, j + 1)
                if not real or j < TILES:
                    t = act.copy(sums[:], psA[:, par * 512:par * 512 + FEAT])
                if not real or 1 <= j < TILES + 1:
                    t = act.copy(sums_t[:], psS[:, 0:FEAT])
                if not real or 2 <= j < TILES + 2:
                    n = j - 2
                    if not real or n >= 2:
                        act.wait_ge(s_x1o[par], j * 8 - (16 + 8 * par))
                        act.sem_inc(s_past, 1)
                    act.activation(x1[:, par, :], psX[:, 0:FEAT], ACT.Copy, accum_out=m.mean[:, ds(n, 1)]
                                   ).then_inc(s_a, 1)
                    act.wait_ge(s_a, j * 2 - 3)
                    act.sem_inc(s_past, 1)
                    act.mul(m.mean[:, ds(n, 1)], m.mean[:, ds(n, 1)], -1.0 / FEAT).then_inc(s_a, 1)
                    act.dma_start(m.x1_dram.rearrange("(t p) f -> t p f", p=P)[ds(n, 1), :, :].rearrange(
                        "t p f -> p (t f)"), x1[:, par, :]).then_inc(s_x1o[par], 16)
                    act.wait_ge(s_a, j * 2 - 2)
                    act.sem_inc(s_past, 1)
                    act.activation(xc[:], psX[:, 0:FEAT], ACT.Identity, bias=m.mean[:, ds(n, 1)])
                    t = act.activation(squares[:], psX[:, 0:FEAT], ACT.Square, bias=m.mean[:, ds(n, 1)],
                                       accum_out=m.rstd[:, ds(n, 1)])
                if not real or 3 <= j < TILES + 3:
                    t = act.copy(xc_t[:], psY[:, 0:FEAT])
                if not real or 4 <= j < TILES + 4:
                    t = act.copy(m.node_row[:, ds(j - 4, 1), 0:HE], psH[:, 0:HE])
                t.then_inc(s_evac, 1)
                if not real or j + 2 <= TILES:
                    act.wait_ge(s_xin, j * 16 + 32)
                if not real or j + 2 < TILES:
                    load(j + 2, (r + 2) % XS)

            act.sem_inc(s_evac, 1)
            act.wait_ge(s_w, 16 * 3)
            load(0, 0)
            act.wait_ge(s_xin, 16)
            load(1, 1)
            act.wait_ge(s_wt, 1)
            act.copy(w_t[:], psX[:, :].rearrange("p (k o) -> p k o", k=HALVES)).then_inc(s_wte, 1)
            for j in range(XS):
                tile(j, j)
            LOOPED = (TILES - 3) // XS
            with act.Fori(1, LOOPED) as u:
                for r in range(XS):
                    tile(u * XS + r, r)
            for j in range(LOOPED * XS, TILES + 4):
                tile(j, j % XS)
            for par in range(2):
                act.wait_ge(s_x1o[par], 16 * (TILES // 2))

        @block.tensor
        def _(pe):
            pe.wait_ge(s_w, 16 * 3)
            for k in range(HALVES):
                for o in range(HALVES):
                    t = pe.transpose(psX[:, k * FEAT + o * P:k * FEAT + (o + 1) * P],
                                     w_raw[:, o, k * P:(k + 1) * P], m.ident[:])
            t.then_inc(s_wt, 1)
            pe.wait_ge(s_wte, 1)
            pe.wait_ge(s_pc, 9)

            def open_or_close(bank, start):
                pe.matmul(psA[:, ds(bank * 512, FEAT)], zero_b[:, 0:P], zero_b[:], start=start, stop=not start)

            def stages(d):
                pe.wait_ge(s_evac, d + 1)
                for k in range(HALVES):
                    t = pe.matmul(psH[:, 0:HE], xc_t[:, k * P:(k + 1) * P], wg[:, k, :],
                                  start=(k == 0), stop=(k == HALVES - 1))
                real = isinstance(d, int)
                if not real or d < TILES + 3:
                    for k in range(HALVES):
                        t = pe.transpose(psY[:, k * P:(k + 1) * P], xc[:, k * P:(k + 1) * P], m.ident[:])
                if not real or d < TILES + 2:
                    pe.matmul(psX[:, 0:FEAT], m.ones[0:1, :], brow[:], start=True, stop=False)
                    pe.matmul(psX[:, 0:FEAT], m.ident[:], xs[:, ds((d + 2) % XS, 1), :], start=False, stop=False)
                    for k in range(HALVES):
                        t = pe.matmul(psX[:, 0:FEAT], sums_t[:, k * P:(k + 1) * P], w_t[:, k, :],
                                      start=False, stop=(k == HALVES - 1))
                if not real or d < TILES + 1:
                    for k in range(HALVES):
                        t = pe.transpose(psS[:, k * P:(k + 1) * P], sums[:, k * P:(k + 1) * P], m.ident[:])
                t.then_inc(s_tile, 1)

            def step(s, r):
                code = pe.value_load(m.step_code[0:1, ds(s, 1)], min_val=0, max_val=GROUPS * 4 - 1)
                pe.wait_ge(s_hot, s + 1)
                pe.wait_ge(s_ready, (code >> 2) + 1)
                for j in range(GT):
                    t = pe.matmul(psA[:, ds(((code >> 1) & 1) * 512, FEAT)], hot[:, r, j, :],
                                  rows[:, ds((code >> 2) & (RING - 1), 1), j, :], start=False, stop=False)
                t.then_inc(s_mm, 1)
                with pe.If((code & 1) == 1):
                    d = pe.value_load(m.step_tile[0:1, ds(s, 1)], min_val=0, max_val=TILES - 1)
                    open_or_close(d & 1, False)
                    stages(d)
                    open_or_close((d + 1) & 1, True)

            open_or_close(0, True)
            for r in range(XS):
                step(r, r)
            for n in range(PIECES):
                with pe.Fori(CUT[n], CUT[n + 1]) as u:
                    for r in range(XS):
                        step(u * XS + r, r)
                if n >= 9 and n < PIECES - 1:
                    pe.wait_ge(s_turn, n - 8)
                    for q in range(GCOLS // P):
                        t = pe.transpose(psT[:, q * P:(q + 1) * P], key[turned_keys[n - 9]][:, q * P:(q + 1) * P],
                                         m.ident[:])
                    t.then_inc(s_turned, 1)
            pe.wait_ge(s_turn, PIECES - 9)
            pe.matmul(psT[:, 0:2], shift_dn[:], lastd[:], start=True, stop=True).then_inc(s_turned, 1)
            with pe.Fori(CUT[PIECES], CUT[PIECES + 1]) as u:
                for r in range(XS):
                    step(u * XS + r, r)
            open_or_close(TILES & 1, False)
            for d in range(TILES, TILES + 4):
                stages(d)

        @block.vector
        def _(v):
            c = Count(v, s_s)

            def one_hots(s, r, first=False):
                g = v.value_load(m.step_group[0:1, ds(s, 1)], min_val=0, max_val=GROUPS - 1)
                if not first:
                    v.wait_ge(s_mm, s - (XS - 1))
                v.tensor_scalar(rel[:, r, :], m.dst_t[:, ds(g * GT, GT)], m.step_base[:, ds(s, 1)], None,
                                ALU.subtract).then_inc(s_rel, 1)
                v.wait_ge(s_rel, s + 1)
                for j in range(GT):
                    t = v.tensor_scalar(hot[:, r, j, :], m.iota[:], rel[:, r, j:j + 1],
                                        m.ew_t[:, ds(g * GT + j, 1)], ALU.is_equal, ALU.mult)
                t.then_inc(s_hot, 1)

            def sort_init():
                v.wait_ge(s_ei, 32)
                c.done(v.tensor_scalar(key_i[0], key_i[0], KEY_SHIFT, KEY_TOP, ALU.logical_shift_left,
                                       ALU.bitwise_or))
                c.done(v.tensor_tensor(key_i[2], key_i[0], key_i[1], ALU.bitwise_or))
                v.wait_ge(s_pc, 9)
                c.done(v.tensor_copy(m.dst_first[:], sign[:, 1:2]))
                c.done(v.tensor_scalar(m.dst_first[:], m.dst_first[:], 1, None, ALU.bitwise_and))
                c.done(v.tensor_copy(sign[:, 0:1], m.dst_first[:]))
                c.done(v.tensor_scalar(sign[:, 0:1], sign[:, 0:1], -2.0, 1.0, ALU.mult, ALU.add))

            def flip(buf, k, col_bits):
                t = key[buf]
                hb, lb = k - col_bits, k - 1 - col_bits
                if k == 1:
                    w = t.rearrange("p (a h w) -> p a h w", h=2, w=1 << hb)
                    c.done(v.tensor_scalar(w[:, :, 1, :], w[:, :, 1, :], -1.0, None, ALU.mult))
                elif k == 17:
                    w = t.rearrange("p (a h w) -> p a h w", h=2, w=1 << lb)
                    c.done(v.tensor_scalar(w[:, :, 1, :], w[:, :, 1, :], -1.0, None, ALU.mult))
                elif k == 10:
                    w = t.rearrange("p (a h w) -> p a h w", h=2, w=1 << lb)
                    c.done(v.tensor_scalar(w[:, :, 1, :], w[:, :, 1, :], -1.0, None, ALU.mult))
                    c.done(v.tensor_scalar(t, t, sign[:, 0:1], None, ALU.mult))
                else:
                    w = t.rearrange("p (a h l w) -> p a h l w", h=2, l=2, w=1 << lb)
                    c.inc(v.tensor_scalar(w[:, :, 0, 1, :], w[:, :, 0, 1, :], -1.0, None, ALU.mult))
                    c.done(v.tensor_scalar(w[:, :, 1, 0, :], w[:, :, 1, 0, :], -1.0, None, ALU.mult))

            def exchange(buf, bit):
                to = 1 if buf == 2 else 1 - buf
                a = key[buf].rearrange("p (a h w) -> p a h w", h=2, w=1 << bit)
                o = key[to].rearrange("p (a h w) -> p a h w", h=2, w=1 << bit)
                c.inc(v.tensor_tensor(o[:, :, 0, :], a[:, :, 0, :], a[:, :, 1, :], ALU.min))
                c.done(v.tensor_tensor(o[:, :, 1, :], a[:, :, 0, :], a[:, :, 1, :], ALU.max))
                return to

            def columns(buf, bits):
                for bit in range(bits - 1, -1, -1):
                    buf = exchange(buf, bit)
                return buf

            def take(buf, n):
                v.wait_ge(s_turned, n)
                c.done(v.tensor_copy(key[buf], psT[:]))
                return buf

            def sort_piece(n, buf):
                if n < 10:
                    flip(buf, n + 1, 0)
                    buf = columns(buf, n + 1)
                else:
                    k, back = 11 + (n - 10) // 2, (n - 10) % 2
                    if back:
                        buf = columns(take(1 - buf, n - 9), 10)
                    else:
                        buf = take(1 if buf != 1 else 0, n - 9)
                        flip(buf, k, 10)
                        buf = columns(buf, k - 10)
                if 9 <= n < PIECES - 1:
                    v.sem_inc(s_turn, 1)
                return buf

            def sort_end(buf):
                k, d = key_i[buf], key_i[2]
                c.done(v.tensor_scalar(d, k, KEY_SHIFT, (1 << KEY_SHIFT) - 1, ALU.logical_shift_right,
                                       ALU.bitwise_and))
                c.inc(v.tensor_scalar(m.src_sorted[:], k, (1 << KEY_SHIFT) - 1, None, ALU.bitwise_and))
                c.done(v.tensor_copy(m.dst_first[:], d[:, 0:1]))
                c.done(v.tensor_copy(key[2], d))
                c.inc(v.tensor_copy(lastd[:, 0:1], key[2][:, GCOLS - 1:GCOLS]))
                c.done(v.tensor_copy(lastd[:, 1:2], key[2][:, 0:1]))
                v.sem_inc(s_turn, 1)
                c.inc(v.tensor_tensor(m.seg_keep[:, 1:GCOLS], key[2][:, 1:GCOLS], key[2][:, 0:GCOLS - 1],
                                      ALU.is_equal))
                c.done(v.memset(m.seg_keep[:, 0:1], 1.0))
                c.done(v.tensor_reduce(m.link[:, 1:2], m.seg_keep[:], AX_X, ALU.min))
                v.wait_ge(s_turned, PIECES - 9)
                c.done(v.tensor_tensor(m.link[:, 0:1], psT[:, 0:1], key[2][:, 0:1], ALU.is_equal))
                c.done(v.memset(m.link[0:1, 0:1], 0.0))

            for r in range(XS):
                one_hots(r, r, first=True)
            sort_init()
            buf = 2
            for n in range(PIECES):
                with v.Fori(CUT[n], CUT[n + 1]) as u:
                    for r in range(XS):
                        one_hots(u * XS + r, r)
                buf = sort_piece(n, buf)
            sort_end(buf)
            with v.Fori(CUT[PIECES], CUT[PIECES + 1]) as u:
                for r in range(XS):
                    one_hots(u * XS + r, r)

def attention_terms(nc, sem, att_src, att_dst, m):
    with ExitStack() as ctx:
        def sb(name, shape, dt=F32):
            return ctx.enter_context(nc.sbuf_tensor(name, shape, dt))

        att = sb("att", [P, 2, HE])
        prod = sb("prod", [P, 2, TILES, HE])
        zeros = sb("zeros", [P, 512])
        std = sb("std_all", [P, TILES])
        s_std = sem("c_std")
        s_att, s_v, s_row = sem("c_att"), sem("c_vector"), sem("c_rows_ready")
        s_z, s_zo, s_fin = sem("c_zero"), sem("c_zero_stored"), sem("c_rows_stored")
        block = ctx.enter_context(nc.Block())

        @block.sync
        def _(sp):
            for n, a in enumerate((att_src, att_dst)):
                sp.dma_start(att[:, n, :], a.rearrange("(o h) e -> o (h e)", o=1).to_broadcast([P, HE])
                             ).then_inc(s_att, 16)
            for n, (d, t) in enumerate(((m.row_dram, m.node_row), (m.adst_dram, m.node_dst))):
                sp.wait_ge(s_row, n + 1)
                sp.dma_start(d.rearrange("(t p) c -> p t c", p=P), t[:]).then_inc(s_fin, 16)
            sp.wait_ge(s_fin, 32)

        @block.gpsimd
        def _(pool):
            pool.memset(zeros[:], 0.0).then_inc(s_z, 1)

        @block.scalar
        def _(act):
            act.activation(std[:], m.rstd[:], ACT.Sqrt, bias=m.eps[:, 0:1], scale=1.0 / FEAT).then_inc(s_std, 1)
            act.wait_ge(s_z, 1)
            flat = m.adst_first.rearrange("(q p n) c -> q p (n c)", q=8, p=P)
            for q in range(8):
                act.dma_start(flat[q], zeros[:]).then_inc(s_zo, 16)
            act.wait_ge(s_zo, 16 * 8)

        @block.vector
        def _(v):
            c = Count(v, s_v)
            c.inc(v.tensor_scalar(m.mean[:], m.mean[:], -1.0, None, ALU.mult))
            v.wait_ge(s_std, 1)
            c.done(v.reciprocal(m.rstd[:], std[:]))
            c.inc(v.scalar_tensor_tensor(m.shift[:], m.mean[:], -1.0, m.rstd[:], ALU.mult, ALU.mult))
            c.done(v.tensor_tensor(m.node_row[:, :, 0:HE], m.node_row[:, :, 0:HE],
                                   m.rstd[:, :, None].to_broadcast([P, TILES, HE]), ALU.mult))
            v.wait_ge(s_att, 32)
            for q, o in enumerate((m.node_row[:, :, HE:ROWF], m.node_dst[:])):
                c.done(v.tensor_tensor(prod[:, q, :, :], m.node_row[:, :, 0:HE],
                                       att[:, q:q + 1, :].to_broadcast([P, TILES, HE]), ALU.mult))
                c.done(v.tensor_reduce(o, prod[:, q, :, :].rearrange("p t (h e) -> p t h e", e=EXPERTS), AX_X,
                                       ALU.add))
                v.sem_inc(s_row, 1)


def late_experts(nc, sem, ctx, m, name, first, pairs):
    def sb(what, shape):
        return ctx.enter_context(nc.sbuf_tensor(f"{name}_{what}", shape, F32))

    def pb(what, shape):
        return ctx.enter_context(nc.psum_tensor(f"{name}_{what}", shape, F32))

    lane = Shared()
    nothing = lambda: None
    xl = sb("x1", [P, 2, FEAT])
    yn = sb("y", [P, 2, FEAT])
    yt = sb("y_turned", [P, 2, HALVES, N2])
    hid = sb("hidden", [P, 2, FB, N2])
    yo = sb("expert_out", [P, 2, 2, FEAT])
    psL = [pb(f"ps_hidden{n}", [P, 2, N2]) for n in range(4)]
    psO = [pb(f"ps_expert{n}", [P, 2, FEAT]) for n in range(2)]
    psY = pb("ps_y_turned", [P, HALVES, N2])
    s_x, s_yn, s_ty, s_yt = (sem(f"{name}_{w}") for w in ("x_loaded", "normed", "y_turned", "yt_ready"))
    s_l1 = sem(f"{name}_layer1")
    s_hid = sem(f"{name}_hidden_ready")
    s_l2 = sem(f"{name}_layer2")
    s_yo = sem(f"{name}_out_ready")
    s_st = [sem(f"{name}_stored{k}") for k in range(2)]
    s_past = sem(f"{name}_past")

    def scalar_pair(act, u, more, between={}):
        def load(n):
            act.dma_start(xl[:], m.x1_dram.rearrange("(t p) f -> p t f", p=P)[:, ds((first + n) * 2, 2), :]
                          ).then_inc(s_x, 16)

        def normalise(n):
            act.wait_ge(s_x, n * 16 + 16)
            act.sem_inc(s_past, 1)
            for t in range(2):
                q = act.activation(yn[:, t, :], xl[:, t, :], ACT.Identity,
                                   scale=m.rstd[:, ds((first + n) * 2 + t, 1)],
                                   bias=m.shift[:, ds((first + n) * 2 + t, 1)])
            q.then_inc(s_yn, 1)
            if not isinstance(n, int) or n + 1 < pairs:
                act.wait_ge(s_yn, n + 1)
                load(n + 1)

        def out_of_psum(n):
            act.wait_ge(s_ty, n + 1)
            act.copy(yt[:, ds(n % 2, 1), :, :], psY[:]).then_inc(s_yt, 1)

        def hidden(e):
            n = u * EXPERTS + e
            for q in range(2):
                act.wait_ge(s_l1, n * 2 + (q + 1))
                if q == 0:
                    act.wait_ge(s_l2, n + 1)
                for f in range(2):
                    t = act.activation(hid[:, e % 2, 2 * q + f, :], psL[(e % 2) * 2 + q][:, f, :], ACT.Gelu,
                                       bias=m.b1c[:, e, 2 * q + f:2 * q + f + 1])
                t.then_inc(s_hid, 1)

        def store(e):
            n = u * EXPERTS + e
            act.wait_ge(s_l2, n + 3)
            act.wait_ge(s_st[e % 2], u * 32 + (16 + e // 2 * 16))
            act.copy(yo[:, e % 2, :, :], psO[e % 2][:]).then_inc(s_yo, 1)
            act.wait_ge(s_yo, n + 3)
            act.dma_start(m.y_dram.rearrange("(t p) e f -> p t e f", p=P)[:, ds((first + u) * 2, 2), e, :],
                          yo[:, e % 2, :, :]).then_inc(s_st[e % 2], 16)

        if u is None:
            for s, start in ((s_hid, 4), (s_l2, 2), (s_yo, 2)):
                act.sem_inc(s, start)
            for s in s_st:
                act.sem_inc(s, 16)
            load(0)
            normalise(0)
            out_of_psum(0)
            return
        hidden(0)
        between.get(0, nothing)()
        hidden(1)
        if more:
            normalise(u + 1)
        store(0)
        between.get(1, nothing)()
        hidden(2)
        store(1)
        if more:
            out_of_psum(u + 1)
        between.get(2, nothing)()
        hidden(3)
        store(2)
        store(3)
        between.get(3, nothing)()

    def tensor_pair(pe, u, more, between=None):
        def turn(n):
            pe.wait_ge(s_yn, n + 1)
            for t in range(2):
                for h in range(HALVES):
                    q = pe.transpose(psY[:, h, t * P:(t + 1) * P], yn[:, t, h * P:(h + 1) * P], m.ident[:])
            q.then_inc(s_ty, 1)

        def layer1(e):
            n = u * EXPERTS + e
            if e == 0:
                pe.wait_ge(s_yt, u + 1)
            for q in range(2):
                pe.wait_ge(s_hid, n * 2 + (q + 1))
                for f in range(2):
                    for h in range(HALVES):
                        t = pe.matmul(psL[(e % 2) * 2 + q][:, f, :],
                                      m.w1[:, h, e, (2 * q + f) * P:(2 * q + f + 1) * P],
                                      yt[:, ds(u % 2, 1), h, :], start=(h == 0), stop=(h == HALVES - 1))
                t.then_inc(s_l1, 1)

        def layer2(e):
            n = u * EXPERTS + e
            pe.wait_ge(s_hid, n * 2 + 6)
            pe.wait_ge(s_yo, n + 1)
            for t in range(2):
                pe.matmul(psO[e % 2][:, t, :], m.ones[0:1, :], m.b2r[0:1, e, :], start=True, stop=False)
                for f in range(FB):
                    q = pe.matmul(psO[e % 2][:, t, :], hid[:, e % 2, f, t * P:(t + 1) * P], m.w2[:, f, e, :],
                                  start=False, stop=(f == FB - 1))
            q.then_inc(s_l2, 1)

        if u is None:
            turn(0)
            return
        layer1(0)
        layer1(1)
        layer2(0)
        if more:
            turn(u + 1)
        layer1(2)
        if between:
            between()
        layer2(1)
        layer1(3)
        layer2(2)
        layer2(3)

    def scalar(act, start, stop):
        if start == 0:
            scalar_pair(act, None, True)
        if start < min(stop, pairs - 2):
            with act.Fori(start, min(stop, pairs - 2)) as u:
                scalar_pair(act, u, True)
        for u in range(max(start, pairs - 2), stop):
            scalar_pair(act, u, u < pairs - 1)

    def tensor(pe, start, stop):
        if start == 0:
            tensor_pair(pe, None, True)
        if start < min(stop, pairs - 1):
            with pe.Fori(start, min(stop, pairs - 1)) as u:
                tensor_pair(pe, u, True)
        if stop == pairs:
            tensor_pair(pe, pairs - 1, False)

    def wait_begun(eng):
        eng.wait_ge(s_x, 32)

    def wait_stored(eng, n):
        for s in s_st:
            eng.wait_ge(s, 32 * n + 16)

    lane.scalar, lane.scalar_pair, lane.wait_stored = scalar, scalar_pair, wait_stored
    lane.tensor, lane.tensor_pair, lane.wait_begun = tensor, tensor_pair, wait_begun
    return lane


def gather_and_experts(nc, sem, W1, b1, W2, b2, edge_index, m):
    with ExitStack() as ctx:
        def sb(name, shape, dt):
            return ctx.enter_context(nc.sbuf_tensor(name, shape, dt))

        GB, SLOTS = 16, 4
        BATCHES = GCOLS // GB
        WEIGHT_LOADS = HALVES + FB + 2 * EXPERTS

        w1, w2, b1c, b2r = m.w1, m.w2, m.b1c, m.b2r
        xd = sb("d_x", [P, 2, 2, FEAT], F32)
        yn = sb("d_y", [P, 2, FEAT], F32)
        yt = sb("d_yt", [P, 2, HALVES, N2], F32)
        hid = sb("hid", [P, 2, FB, N2], F32)
        yo = sb("yo", [P, EXPERTS, 2, FEAT], F32)
        got = sb("got", [P, SLOTS, GB, STATE], F32)
        idx = sb("d_idx", [P, SLOTS, GB], I32)
        lo = sb("lo", [P, GCOLS], BF16)
        hi = sb("hi", [P, GCOLS], BF16)
        hot_lo = sb("hot_lo", [P, HCOLS, P], BF16)
        hot_hi = sb("hot_hi", [P, HCOLS, TILES], BF16)
        di = hot_lo[:].rearrange("p a b -> p (a b)").bitcast(I32)[:, 0:2 * GCOLS].rearrange("p (n j) -> p n j", n=2)
        iota_b = sb("iota_b", [P, P], BF16)
        zero_b = sb("zero_b", [P, P], BF16)
        before = sb("before", [P, P], F32)
        cnt = sb("cnt", [P, TILES], F32)
        tot = sb("tot", [P, TILES], F32)
        pos = sb("pos", [P, 2, TILES], F32)
        sidx = sb("sidx", [P, 2, CH], I32)
        sdat = sb("sdat", [P, 2, CH, HEADS], F32)
        psL = [ctx.enter_context(nc.psum_tensor(f"d_hidden{n}", [P, 2, N2], F32)) for n in range(4)]
        psO = [ctx.enter_context(nc.psum_tensor(f"d_expert{n}", [P, 2, FEAT], F32)) for n in range(2)]
        psC = ctx.enter_context(nc.psum_tensor("counts", [P, 512], F32))
        psY = ctx.enter_context(nc.psum_tensor("d_y_turned", [P, HALVES, N2], F32))

        s_w, s_ei = sem("d_weights"), sem("d_edges")
        s_x = [sem("d_x0"), sem("d_x1")]
        s_yn, s_ty, s_yt = sem("d_normed"), sem("d_y_turned"), sem("d_yt_ready")
        s_l1, s_hid, s_l2, s_yo = sem("d_l1"), sem("d_hidden_ready"), sem("d_l2"), sem("d_out_ready")
        s_st = [sem(f"d_stored{e}") for e in range(EXPERTS)]
        s_pc, s_pi = sem("d_pool_const"), sem("d_idx_ready")
        s_got = [sem(f"d_gathered{k}") for k in range(SLOTS)]
        s_past = sem("d_past")
        s_mv = [sem(f"d_moved{k}") for k in range(SLOTS)]
        s_v, s_hh, s_hm = sem("d_count_vector"), sem("d_hot"), sem("d_hist")
        s_cnt, s_pos = sem("d_counts_read"), sem("d_positions")
        s_sc, s_sd = [sem("d_scattered0"), sem("d_scattered1")], sem("d_scatter_staged")

        block = ctx.enter_context(nc.Block())

        @block.sync
        def _(sp):
            sp.dma_start(di[:, 0, :], edge_index[1, :].rearrange("(p j) -> p j", p=P)).then_inc(s_ei, 16)
            for k in range(HALVES):
                sp.dma_start(w1[:, k, :, :], W1[:, k * P:(k + 1) * P, :].rearrange("e p n -> p e n")).then_inc(s_w, 16)
            for k in range(FB):
                sp.dma_start(w2[:, k, :, :], W2[:, k * P:(k + 1) * P, :].rearrange("e p n -> p e n")).then_inc(s_w, 16)
            for e in range(EXPERTS):
                sp.dma_start(b2r[:, e, :], b2[e:e + 1, :].to_broadcast([P, FEAT])).then_inc(s_w, 16)
            with nc.allow_non_contiguous_dma(reason="a bias of 8 KB, once"):
                for e in range(EXPERTS):
                    sp.dma_start(b1c[:, e, :], b1[e, :].rearrange("(k p) -> p k", p=P)).then_inc(s_w, 16)

            def move(i, k):
                sp.wait_ge(s_got[k], i * (16 * GB) + 16 * GB)
                sp.dma_start(m.states[:, ds(i * (SLOTS * GB) + k * GB, GB), :], got[:, k, :, :]
                             ).then_inc(s_mv[k], 16)

            with sp.Fori(0, BATCHES // SLOTS) as i:
                for k in range(SLOTS):
                    move(i, k)
            for k in range(SLOTS):
                sp.wait_ge(s_mv[k], 16 * (BATCHES // SLOTS))

        @block.gpsimd
        def _(pool):
            c = Count(pool, s_pc)
            c.inc(pool.iota(iota_b[:], pattern=[[1, P]], base=0, channel_multiplier=0,
                            allow_small_or_imprecise_dtypes=True))
            c.inc(pool.memset(zero_b[:], 0.0))
            c.inc(pool.memset(before[:], 1.0))
            c.inc(pool.memset(got[:], 0.0))
            pool.wait_ge(s_pc, c.n)
            c.inc(pool.affine_select(out=before[:], in_=before[:], compare_op=ALU.is_gt, fill=0.0, base=0,
                                     pattern=[[1, P]], channel_multiplier=-1))

            def batch(i, k, first=False):
                if not first:
                    pool.wait_ge(s_mv[k], i * 16)
                pool.tensor_copy(idx[:, k, :], m.src_sorted[:, ds(i * (SLOTS * GB) + k * GB, GB)]
                                 ).then_inc(s_pi, 1)
                pool.wait_ge(s_pi, i * SLOTS + (k + 1))
                pool.sem_inc(s_past, 1)
                for j in range(GB):
                    pool.indirect_dma_start(got[:, k, j, 0:ROWF], None, m.row_dram,
                                            bass.IndirectOffsetOnAxis(ap=idx[:, k, j:j + 1], axis=0)
                                            ).then_inc(s_got[k], 16)

            for k in range(SLOTS):
                batch(0, k, first=True)
            with pool.Fori(1, BATCHES // SLOTS) as i:
                for k in range(SLOTS):
                    batch(i, k)

            pool.wait_ge(s_pos, 1)

            def spread(i, k, first=False):
                if not first:
                    pool.wait_ge(s_sc[k], i * (16 * CH))
                pool.tensor_copy(sidx[:, k, :], m.first_pos[:, ds((i * 2 + k) * CH, CH)])
                pool.tensor_copy(sdat[:, k, :, :], m.node_dst[:, ds((i * 2 + k) * CH, CH), :]).then_inc(s_sd, 1)
                pool.wait_ge(s_sd, i * 2 + (k + 1))
                pool.sem_inc(s_past, 1)
                for j in range(CH):
                    pool.indirect_dma_start(m.adst_first, bass.IndirectOffsetOnAxis(ap=sidx[:, k, j:j + 1], axis=0),
                                            sdat[:, k, j, :], None, bounds_check=GEDGES - 1, oob_is_err=False
                                            ).then_inc(s_sc[k], 16)

            for k in range(2):
                spread(0, k, first=True)
            with pool.Fori(1, CHUNKS // 2) as i:
                for k in range(2):
                    spread(i, k)
            for k in range(2):
                pool.wait_ge(s_sc[k], 16 * CH * (CHUNKS // 2))

        @block.scalar
        def _(act):
            act.wait_ge(s_w, 16 * WEIGHT_LOADS)

            def load(i, k):
                act.dma_start(xd[:, k, :, :], m.x1_dram.rearrange("(t p) f -> p t f", p=P)[:, ds(i * 2, 2), :]
                              ).then_inc(s_x[k], 16)

            def hidden(n, e, first=False):
                for q in range(2):
                    act.wait_ge(s_l1, n * 2 + (q + 1))
                    if q == 0 and not first:
                        act.wait_ge(s_l2, n - 1)
                    for f in range(2):
                        t = act.activation(hid[:, e % 2, 2 * q + f, :], psL[(e % 2) * 2 + q][:, f, :], ACT.Gelu,
                                           bias=b1c[:, e, 2 * q + f:2 * q + f + 1])
                    t.then_inc(s_hid, 1)

            def store(n, e, i):
                act.wait_ge(s_yo, n + 1)
                act.dma_start(m.y_dram.rearrange("(t p) e f -> p t e f", p=P)[:, ds(i * 2, 2), e, :], yo[:, e, :, :]
                              ).then_inc(s_st[e], 16)

            def pair(i, k, first=False, last=False):
                for e in range(EXPERTS):
                    hidden(i * EXPERTS + e, e, first=first and e < 2)
                    if e == 0 and not last:
                        load(i + 2, k)
                    if e >= 1:
                        store(i * EXPERTS + (e - 1), e - 1, i)
                    elif not first:
                        store(i * EXPERTS - 1, EXPERTS - 1, i - 1)

            load(0, 0)
            load(1, 1)
            pair(0, 0, first=True)
            with act.Fori(0, EARLY_PAIRS // 2 - 1) as u:
                for k in range(2):
                    pair(u * 2 + (k + 1), (k + 1) % 2)
            pair(EARLY_PAIRS - 2, 1, last=True)
            pair(EARLY_PAIRS - 1, 0, last=True)
            store(EARLY_PAIRS * EXPERTS - 1, EXPERTS - 1, EARLY_PAIRS - 1)
            for e in range(EXPERTS):
                act.wait_ge(s_st[e], 16 * EARLY_PAIRS)

        HLOOP = HPIECES // 2

        @block.tensor
        def _(pe):
            pe.wait_ge(s_pc, 5)
            pe.wait_ge(s_w, 16 * WEIGHT_LOADS)
            pe.matmul(psC[:, 0:TILES], zero_b[:], zero_b[:, 0:TILES], start=True, stop=False)

            def layer1(i, k, n, e, first=False):
                if e == 0:
                    pe.wait_ge(s_yt, i + 1)
                for q in range(2):
                    if not first:
                        pe.wait_ge(s_hid, n * 2 + (q - 3))
                    for f in range(2):
                        for h in range(HALVES):
                            t = pe.matmul(psL[(e % 2) * 2 + q][:, f, :],
                                          w1[:, h, e, (2 * q + f) * P:(2 * q + f + 1) * P], yt[:, k, h, :],
                                          start=(h == 0), stop=(h == HALVES - 1))
                    t.then_inc(s_l1, 1)

            def layer2(n, e, first=False):
                pe.wait_ge(s_hid, n * 2 + 2)
                if not first:
                    pe.wait_ge(s_yo, n - 1)
                for t in range(2):
                    for f in range(FB):
                        q = pe.matmul(psO[e % 2][:, t, :], hid[:, e % 2, f, t * P:(t + 1) * P], w2[:, f, e, :],
                                      start=(f == 0), stop=(f == FB - 1))
                q.then_inc(s_l2, 1)

            def turn(i):
                pe.wait_ge(s_yn, i + 1)
                if not isinstance(i, int) or i >= 1:
                    pe.wait_ge(s_yt, i)
                for t in range(2):
                    for h in range(HALVES):
                        q = pe.transpose(psY[:, h, t * P:(t + 1) * P], yn[:, t, h * P:(h + 1) * P], m.ident[:])
                q.then_inc(s_ty, 1)

            def pair(i, k, first=False):
                for e in range(EXPERTS):
                    if e == 2 and not (isinstance(i, int) and i == EARLY_PAIRS - 1):
                        turn(i + 1)
                    layer1(i, k, i * EXPERTS + e, e, first=first and e < 2)
                    if e >= 1:
                        layer2(i * EXPERTS + (e - 1), e - 1, first=first and e < 3)
                    elif not first:
                        layer2(i * EXPERTS - 1, EXPERTS - 1)

            def count(q):
                pe.wait_ge(s_hh, q + 1)
                for j in range(HCOLS):
                    t = pe.matmul(psC[:, 0:TILES], hot_lo[:, j, :], hot_hi[:, j, :], start=False, stop=False)
                t.then_inc(s_hm, 1)

            turn(0)
            pair(0, 0, first=True)
            with pe.Fori(0, HLOOP) as u:
                for k in range(2):
                    count(u * 2 + k)
                    pair(u * 2 + (k + 1), (k + 1) % 2)
            pe.matmul(psC[:, 0:TILES], zero_b[:], zero_b[:, 0:TILES], start=False, stop=True).then_inc(s_hm, 1)
            pe.wait_ge(s_cnt, 1)
            pe.matmul(psC[:, P:P + TILES], m.ones[:], cnt[:], start=True, stop=True)
            pe.matmul(psC[:, 2 * P:2 * P + TILES], before[:], cnt[:], start=True, stop=True).then_inc(s_hm, 1)
            with pe.Fori(HLOOP, (EARLY_PAIRS - 1) // 2 - 1) as u:
                for k in range(2):
                    pair(u * 2 + (k + 1), (k + 1) % 2)
            pair(EARLY_PAIRS - 2, 1)
            pair(EARLY_PAIRS - 1, 0)
            layer2(EARLY_PAIRS * EXPERTS - 1, EXPERTS - 1)

        @block.vector
        def _(v):
            c = Count(v, s_v)
            v.wait_ge(s_ei, 16)
            c.done(v.tensor_scalar(di[:, 1, :], di[:, 0, :], P - 1, None, ALU.bitwise_and))
            c.done(v.tensor_copy(lo[:], di[:, 1, :]))
            c.done(v.tensor_scalar(di[:, 1, :], di[:, 0, :], 7, None, ALU.arith_shift_right))
            c.done(v.tensor_copy(hi[:], di[:, 1, :]))
            v.wait_ge(s_pc, 5)
            v.wait_ge(s_w, 16 * WEIGHT_LOADS)

            def hots(q, n):
                part, wide, t = ((lo, P, hot_lo), (hi, TILES, hot_hi))[n]
                if n == 0 and not (isinstance(q, int) and q == 0):
                    v.wait_ge(s_hm, q)
                o = v.tensor_tensor(t[:], iota_b[:, None, 0:wide].to_broadcast([P, HCOLS, wide]),
                                    part[:, ds(q * HCOLS, HCOLS)][:, :, None].to_broadcast([P, HCOLS, wide]),
                                    ALU.is_equal)
                if n == 1:
                    o.then_inc(s_hh, 1)

            def outs(n, e, i, first=False):
                v.wait_ge(s_l2, n + 1)
                if not first:
                    v.wait_ge(s_st[e], i * 16)
                v.tensor_tensor(yo[:, e, :, :], psO[e % 2][:], b2r[:, e:e + 1, :].to_broadcast([P, 2, FEAT]),
                                ALU.add).then_inc(s_yo, 1)

            def normalise(i, k):
                v.wait_ge(s_x[k], (i // 2) * 16 + 16 if isinstance(i, int) else i * 8 + (16 - 8 * k))
                if not isinstance(i, int) or i >= 1:
                    v.wait_ge(s_ty, i)
                for t in range(2):
                    o = v.tensor_scalar(yn[:, t, :], xd[:, k, t, :], m.mean[:, ds(i * 2 + t, 1)],
                                        m.rstd[:, ds(i * 2 + t, 1)], ALU.subtract, ALU.mult)
                o.then_inc(s_yn, 1)

            def out_of_psum(i, k):
                v.wait_ge(s_ty, i + 1)
                v.tensor_copy(yt[:, k, :, :], psY[:]).then_inc(s_yt, 1)

            def pair(i, k, first=False, between=None, count=False):
                more = not (isinstance(i, int) and i == EARLY_PAIRS - 1)
                if more:
                    normalise(i + 1, 1 - k)
                for e in range(EXPERTS):
                    if e == 3 and between:
                        between()
                    outs(i * EXPERTS + e, e, i, first=first)
                    if e == 1 and more:
                        out_of_psum(i + 1, 1 - k)
                    if count and e < 2:
                        hots(i, e)

            def positions():
                v.wait_ge(s_hm, HPIECES + 1)
                c.done(v.tensor_copy(cnt[:], psC[:, 0:TILES]))
                v.sem_inc(s_cnt, 1)
                v.wait_ge(s_hm, HPIECES + 2)
                c.done(v.tensor_copy(tot[:], psC[:, P:P + TILES]))
                c.done(v.tensor_tensor_scan(pos[:, 0, :], m.ones[:, 0:TILES], tot[:], 0.0, ALU.mult, ALU.add))
                c.done(v.tensor_tensor(pos[:, 0, :], pos[:, 0, :], tot[:], ALU.subtract))
                c.done(v.tensor_tensor(pos[:, 0, :], pos[:, 0, :], psC[:, 2 * P:2 * P + TILES], ALU.add))
                c.inc(v.tensor_scalar(m.has_edges[:], cnt[:], 0.5, None, ALU.is_gt))
                c.done(v.tensor_tensor(pos[:, 1, :], pos[:, 0, :], cnt[:], ALU.add))
                c.done(v.tensor_scalar(cnt[:], m.has_edges[:], -4.0 * GEDGES, 4.0 * GEDGES, ALU.mult, ALU.add))
                c.inc(v.tensor_tensor(m.first_pos[:], pos[:, 0, :], cnt[:], ALU.add))
                c.done(v.scalar_tensor_tensor(m.last_pos[:], pos[:, 1, :], -1.0, cnt[:], ALU.add, ALU.add))
                v.sem_inc(s_pos, 1)

            normalise(0, 0)
            out_of_psum(0, 0)
            pair(0, 0, first=True, count=True)
            with v.Fori(0, HLOOP - 1) as u:
                for k in range(2):
                    pair(u * 2 + (k + 1), 1 - k, count=True)
            pair(HPIECES - 1, 1, count=True)
            pair(HPIECES, 0, between=positions)
            with v.Fori(HLOOP, (EARLY_PAIRS - 1) // 2 - 1) as u:
                for k in range(2):
                    pair(u * 2 + (k + 1), 1 - k)
            pair(EARLY_PAIRS - 2, 1)
            pair(EARLY_PAIRS - 1, 0)


def segment_softmax(nc, sem, m):
    with ExitStack() as ctx:
        def sb(name, shape, dt=F32):
            return ctx.enter_context(nc.sbuf_tensor(name, shape, dt))

        adfirst = sb("adfirst", [P, HEADS])
        e = sb("e", [P, HEADS, GCOLS])
        decay = sb("decay", [P, HEADS, GCOLS])
        adst = decay[:].rearrange("p h j -> p (h j)").rearrange("p (j h) -> p j h", h=HEADS)
        limit = m.src_sorted[:].bitcast(F32)
        tail = sb("tail", [P, 2, ROWF])
        tail_t = sb("tail_t", [ROWF, 2, P])
        carried = sb("carried", [ROWF, P + 1])
        cin = sb("cin", [P, 2, ROWF])
        whole = sb("whole", [P, 1])
        SPANS = 4
        SPAN = GCOLS // SPANS
        psE = ctx.enter_context(nc.psum_tensor("e_turn", [P, 512], F32))
        psT, psB = psE[:, 0:2 * P], psE[:, 2 * P:3 * P]
        lane = late_experts(nc, sem, ctx, m, "scan", EARLY_PAIRS, SCAN_PAIRS)

        s_ad, s_af = sem("e_adst"), sem("e_adst_first")
        s_v, s_t, s_a, s_ask, s_go = sem("e_vector"), sem("e_turned"), sem("e_scalar"), sem("e_ask_pe"), sem("e_ask_act")
        s_st = sem("e_stored")
        s_fin = sem("e_states_ready")
        states = m.states
        mx = states[:, :, ROWF:STATE]
        by_head = lambda a: a.rearrange("p j h -> p h j")

        block = ctx.enter_context(nc.Block())

        @block.sync
        def _(sp):
            sp.dma_start(adst, m.adst_first.rearrange("(p j) h -> p j h", p=P)).then_inc(s_ad, 16)
            for q in range(SPANS):
                sp.wait_ge(s_fin, q + 1)
                sp.dma_start(m.state_dram.rearrange("(p j) c -> p j c", p=P)[:, q * SPAN:(q + 1) * SPAN, :],
                             states[:, q * SPAN:(q + 1) * SPAN, :]).then_inc(s_st, 16)
            sp.wait_ge(s_st, 16 * SPANS)

        @block.gpsimd
        def _(pool):
            pool.indirect_dma_start(adfirst[:], None, m.adst_dram,
                                    bass.IndirectOffsetOnAxis(ap=m.dst_first[:], axis=0)).then_inc(s_af, 16)

        @block.scalar
        def _(act):
            lane.scalar(act, 0, 1)
            act.wait_ge(s_go, 1)
            act.activation(decay[:], decay[:], ACT.Exp).then_inc(s_a, 1)
            act.activation(by_head(states[:, :, HE:ROWF]), e[:], ACT.Exp).then_inc(s_a, 1)
            act.wait_ge(s_go, 2)
            act.activation(tail[:, 1, 0:HEADS], tail[:, 1, 0:HEADS], ACT.Exp).then_inc(s_a, 1)
            lane.scalar(act, 1, SCAN_PAIRS)
            lane.wait_stored(act, SCAN_PAIRS)

        @block.tensor
        def _(pe):
            def turn(n, w):
                pe.wait_ge(s_ask, 2 * n + 1)
                for k in range(2):
                    t = pe.transpose(psT[0:w, k * P:(k + 1) * P], tail[:, k, 0:w], m.ident[:])
                t.then_inc(s_t, 1)
                pe.wait_ge(s_ask, 2 * n + 2)
                pe.transpose(psB[:, 0:w], carried[0:w, 0:P], m.ident[0:w, 0:w]).then_inc(s_t, 1)

            lane.tensor_pair(pe, None, True)
            lane.tensor_pair(pe, 0, True, lambda: turn(0, HEADS))
            lane.tensor_pair(pe, 1, True)
            lane.tensor_pair(pe, 2, True, lambda: turn(1, ROWF))
            lane.tensor(pe, 3, SCAN_PAIRS)

        @block.vector
        def _(v):
            c = Count(v, s_v)

            def carry(n, w, start, op0, op1):
                v.sem_inc(s_ask, 1)
                v.wait_ge(s_t, 2 * n + 1)
                c.done(v.tensor_copy(tail_t[0:w, :, :], psT[0:w, 0:2 * P].rearrange("p (k n) -> p k n", k=2)))
                c.inc(v.memset(carried[0:w, 0:1], start))
                c.done(v.tensor_tensor_scan(carried[0:w, 1:P + 1], tail_t[0:w, 1, :], tail_t[0:w, 0, :], start,
                                            op0, op1))
                v.sem_inc(s_ask, 1)
                v.wait_ge(s_t, 2 * n + 2)
                c.done(v.tensor_copy(cin[:, n, 0:w], psB[:, 0:w]))

            v.wait_ge(s_ad, 16)
            v.wait_ge(s_af, 16)
            c.inc(v.memset(m.seg_keep[:, 0:1], 0.0))
            c.inc(v.tensor_copy(adst[:, 0, :], adfirst[:]))
            c.done(v.tensor_tensor(whole[:], m.link[:, 0:1], m.link[:, 1:2], ALU.mult))
            for h in range(HEADS):
                c.inc(v.tensor_tensor_scan(adst[:, :, h], m.seg_keep[:], adst[:, :, h], 0.0, ALU.mult, ALU.add))
            c.inc(v.tensor_scalar(limit, m.seg_keep[:], 2 * BIG, -BIG, ALU.mult, ALU.add))
            v.wait_ge(s_v, c.n)
            c.done(v.tensor_tensor(e[:], by_head(states[:, :, HE:ROWF]), by_head(adst), ALU.add))
            c.done(v.scalar_tensor_tensor(e[:], e[:], SLOPE, e[:], ALU.mult, ALU.max))
            for h in range(HEADS):
                c.inc(v.tensor_tensor_scan(mx[:, :, h], limit, e[:, h, :], -BIG, ALU.min, ALU.max))
            v.wait_ge(s_v, c.n)
            c.inc(v.tensor_copy(tail[:, 0, 0:HEADS], mx[:, GCOLS - 1, :]))
            c.inc(v.tensor_scalar(tail[:, 1, 0:HEADS], whole[:].to_broadcast([P, HEADS]), 2 * BIG, -BIG,
                                  ALU.mult, ALU.add))
            c.inc(v.tensor_scalar(limit[:, 0:1], m.link[:, 0:1], 2 * BIG, -BIG, ALU.mult, ALU.add))
            c.done(v.tensor_copy(m.seg_keep[:, 0:1], m.link[:, 0:1]))
            carry(0, HEADS, -BIG, ALU.min, ALU.max)
            for h in range(HEADS):
                c.inc(v.tensor_tensor_scan(mx[:, :, h], limit, e[:, h, :], cin[:, 0, h:h + 1], ALU.min, ALU.max))
            v.wait_ge(s_v, c.n)
            c.inc(v.tensor_tensor(decay[:, :, 1:GCOLS], by_head(mx[:, 0:GCOLS - 1, :]), by_head(mx[:, 1:GCOLS, :]),
                                  ALU.subtract))
            c.inc(v.tensor_tensor(decay[:, :, 0], cin[:, 0, 0:HEADS], mx[:, 0, :], ALU.subtract))
            c.inc(v.tensor_tensor(e[:], e[:], by_head(mx), ALU.subtract))
            c.inc(v.tensor_tensor(tail[:, 1, 0:HEADS], cin[:, 0, 0:HEADS], mx[:, GCOLS - 1, :], ALU.subtract))
            v.wait_ge(s_v, c.n)
            c.inc(v.tensor_scalar(tail[:, 1, 0:HEADS], tail[:, 1, 0:HEADS], 0.0, None, ALU.min))
            c.done(v.tensor_scalar(decay[:], decay[:], 0.0, None, ALU.min))
            v.sem_inc(s_go, 1)
            v.sem_inc(s_go, 1)
            v.wait_ge(s_a, 1)
            c.inc(v.tensor_tensor(decay[:], decay[:], m.seg_keep[:, None, :].to_broadcast([P, HEADS, GCOLS]),
                                  ALU.mult))
            v.wait_ge(s_a, 2)
            msg = states[:, :, 0:HE].rearrange("p j (h x) -> p j h x", x=EXPERTS)
            c.done(v.tensor_tensor(msg, msg, states[:, :, HE:ROWF][:, :, :, None].to_broadcast(
                [P, GCOLS, HEADS, EXPERTS]), ALU.mult))
            head = [ch // EXPERTS if ch < HE else ch - HE for ch in range(ROWF)]
            for q in range(ROWF // HEADS):
                for k in range(HEADS):
                    ch = q * HEADS + k
                    c.inc(v.tensor_tensor_scan(e[:, k, :], decay[:, head[ch], :], states[:, :, ch], 0.0,
                                               ALU.mult, ALU.add))
                v.wait_ge(s_v, c.n)
                c.done(v.tensor_copy(tail[:, 0, q * HEADS:(q + 1) * HEADS], e[:, :, GCOLS - 1]))
            v.wait_ge(s_a, 3)
            c.done(v.tensor_scalar(cin[:, 1, 0:HEADS], tail[:, 1, 0:HEADS], whole[:, 0:1], None, ALU.mult))
            c.inc(v.tensor_copy(tail[:, 1, 0:HE].rearrange("p (h x) -> p h x", x=EXPERTS),
                                cin[:, 1, 0:HEADS][:, :, None].to_broadcast([P, HEADS, EXPERTS])))
            c.done(v.tensor_copy(tail[:, 1, HE:ROWF], cin[:, 1, 0:HEADS]))
            carry(1, ROWF, 0.0, ALU.mult, ALU.add)
            for q in range(SPANS):
                a, b = q * SPAN, (q + 1) * SPAN
                for ch in range(ROWF):
                    start = cin[:, 1, ch:ch + 1] if q == 0 else states[:, a - 1, ch:ch + 1]
                    c.inc(v.tensor_tensor_scan(states[:, a:b, ch], decay[:, head[ch], a:b], states[:, a:b, ch],
                                               start, ALU.mult, ALU.add))
                v.wait_ge(s_v, c.n)
                v.sem_inc(s_fin, 1)


def combine(nc, sem, b_gat, gamma, beta, out, m):
    with ExitStack() as ctx:
        def sb(name, shape, dt=F32):
            return ctx.enter_context(nc.sbuf_tensor(name, shape, dt))

        T = TILES
        SLOTS = 10
        ROUNDS = PAIRS // SLOTS
        REST = PAIRS - ROUNDS * SLOTS
        PART = [0, 2 * SLOTS, 4 * SLOTS, T]
        PARTS = len(PART) - 1
        ns = sb("ns", [P, T, STATE])
        spare = [a[:, n * T * HEADS:(n + 1) * T * HEADS].rearrange("p (t h) -> p t h", h=HEADS)
                 for a in (m.seg_keep, m.src_sorted[:].bitcast(F32)) for n in range(2)]
        mxm, top_, den, rank = spare
        e0 = sb("e0", [P, T, HEADS])
        w1 = sb("f_w1", [P, T, HEADS])
        w0 = e0
        num = sb("num", [P, T, HE])
        tmp = sb("f_tmp", [P, T, HE])
        vec = sb("vec", [P, 3, HE])
        one = sb("one", [P, 4, T])
        sc = sb("sc", [P, T, EXPERTS])
        ge = sb("f_ge", [P, T, EXPERTS])
        ys = sb("ys", [P, SLOTS, 2, EXPERTS, FEAT])
        xs = sb("xs", [P, SLOTS, 2, FEAT])
        LATE = EARLY_PAIRS + SCAN_PAIRS
        lane = late_experts(nc, sem, ctx, m, "last", LATE, PAIRS - LATE)
        assert LATE >= PAIRS - REST

        s_c, s_clear = sem("f_const"), sem("f_states_cleared")
        s_got = [sem(f"f_gathered{n}") for n in range(PARTS)]
        s_v, s_go, s_a = sem("f_vector"), sem("f_ask_act"), sem("f_act")
        s_in = [sem(f"f_loaded{k}") for k in range(SLOTS)]
        s_out = [sem(f"f_stored{k}") for k in range(SLOTS)]
        s_g, s_sum, s_done = sem("f_gates"), sem("f_summing"), sem("f_pair_done")

        y_t = m.y_dram.rearrange("(t p) e f -> p t e f", p=P)
        x1_t = m.x1_dram.rearrange("(t p) f -> p t f", p=P)
        out_t = out[0:FULL_TILES * P, :].rearrange("(t p) f -> p t f", p=P)
        block = ctx.enter_context(nc.Block())

        @block.sync
        def _(sp):
            for n, a in enumerate((b_gat, gamma, beta)):
                sp.dma_start(vec[:, n, :], a.rearrange("(o c) -> o c", o=1).to_broadcast([P, HE])).then_inc(s_c, 16)

            def load(i, k):
                sp.dma_start(ys[:, k, :, :, :], y_t[:, ds(i * (2 * SLOTS) + 2 * k, 2), :, :]).then_inc(s_in[k], 16)
                sp.dma_start(xs[:, k, :, :], x1_t[:, ds(i * (2 * SLOTS) + 2 * k, 2), :]).then_inc(s_in[k], 16)

            def store(i, k):
                sp.wait_ge(s_done, i * SLOTS + (k + 1))
                if isinstance(i, int) and i * SLOTS + k == PAIRS - 1:
                    sp.dma_start(out_t[:, T - 2, :], xs[:, k, 0, :]).then_inc(s_out[k], 16)
                    sp.dma_start(out[FULL_TILES * P:NODES, :], xs[0:LAST_ROWS, k, 1, :]).then_inc(s_out[k], 16)
                else:
                    sp.dma_start(out_t[:, ds(i * (2 * SLOTS) + 2 * k, 2), :], xs[:, k, :, :]).then_inc(s_out[k], 16)

            def refill(i, k):
                sp.wait_ge(s_out[k], i * 16)
                if isinstance(i, int) and i * SLOTS + k >= LATE:
                    lane.wait_stored(sp, i * SLOTS + k - LATE + 1)
                load(i, k)

            def round_(i):
                fixed = isinstance(i, int)
                for k in range(SLOTS):
                    if fixed and i * SLOTS + k >= PAIRS:
                        return
                    store(i, k)
                    if k >= 2 and not (fixed and (i + 1) * SLOTS + k - 2 >= PAIRS):
                        refill(i + 1, k - 2)
                    if k < 2 and not (fixed and (i == 0 or (i + 1) * SLOTS + k - 2 >= PAIRS)):
                        refill(i, SLOTS + k - 2)

            lane.wait_begun(sp)
            for k in range(SLOTS):
                if k == SLOTS // 2:
                    sp.wait_ge(s_got[0], 16 * PART[1])
                load(0, k)
            round_(0)
            with sp.Fori(1, ROUNDS - 1) as i:
                round_(i)
            round_(ROUNDS - 1)
            round_(ROUNDS)
            for k in range(SLOTS):
                sp.wait_ge(s_out[k], 16 * (ROUNDS + (k < REST) + (k == REST - 1)))

        @block.gpsimd
        def _(pool):
            pool.memset(ns[:], 0.0).then_inc(s_clear, 1)
            pool.wait_ge(s_clear, 1)
            for part in range(PARTS):
                for t in range(PART[part], PART[part + 1]):
                    pool.indirect_dma_start(ns[:, t, :], None, m.state_dram,
                                            bass.IndirectOffsetOnAxis(ap=m.last_pos[:, t:t + 1], axis=0),
                                            bounds_check=GEDGES - 1, oob_is_err=False).then_inc(s_got[part], 16)

        @block.scalar
        def _(act):
            def weights(n):
                a, b = PART[n], PART[n + 1]
                act.wait_ge(s_go, 3 * n + 1)
                act.activation(w1[:, a:b, :], w1[:, a:b, :], ACT.Exp).then_inc(s_a, 1)
                act.activation(w0[:, a:b, :], w0[:, a:b, :], ACT.Exp).then_inc(s_a, 1)

            def deviation(n):
                a, b = PART[n], PART[n + 1]
                act.wait_ge(s_go, 3 * n + 2)
                act.activation(one[:, 1, a:b], one[:, 1, a:b], ACT.Sqrt, bias=m.eps[:, 0:1]).then_inc(s_a, 1)

            def gate(n):
                a, b = PART[n], PART[n + 1]
                act.wait_ge(s_go, 3 * n + 3)
                act.activation(ge[:, a:b, :], ge[:, a:b, :], ACT.Exp).then_inc(s_a, 1)

            places = [[(0, 1), (0, 2), (0, 3)], [(1, 3), (2, 0), (2, 1)], [(3, 1), (3, 2), (3, 3)]]
            pairs = PAIRS - LATE
            between = [{} for _ in range(pairs)]
            for n in range(PARTS):
                for f, (u, place) in zip((weights, deviation, gate), places[n]):
                    between[u][place] = lambda f=f, n=n: f(n)
            lane.scalar_pair(act, None, True)
            for u in range(pairs):
                lane.scalar_pair(act, u, u < pairs - 1, between[u])
            lane.wait_stored(act, pairs)

        @block.tensor
        def _(pe):
            lane.tensor(pe, 0, PAIRS - LATE)

        @block.vector
        def _(v):
            c = Count(v, s_v)
            wide = lambda a: a.rearrange("p t (h x) -> p t h x", x=EXPERTS)

            c.done(v.tensor_tensor(e0[:], m.node_row[:, :, HE:ROWF], m.node_dst[:], ALU.add))
            c.done(v.scalar_tensor_tensor(e0[:], e0[:], SLOPE, e0[:], ALU.mult, ALU.max))
            c.done(v.tensor_scalar(one[:, 0, :], m.has_edges[:], BIG, -BIG, ALU.mult, ALU.add))

            def gates(part):
                a, b = PART[part], PART[part + 1]
                n4 = [P, b - a, HEADS]
                heads4 = lambda q: q[:, :, :, None].to_broadcast(n4 + [EXPERTS])
                per16 = lambda q: q[:, :, None].to_broadcast([P, b - a, HE])
                row = lambda n: vec[:, n:n + 1, :].to_broadcast([P, b - a, HE])
                has4 = m.has_edges[:, a:b, None].to_broadcast(n4)
                v.wait_ge(s_got[part], 16 * (b - a))
                c.done(v.tensor_tensor(mxm[:, a:b, :], ns[:, a:b, ROWF:STATE], has4, ALU.mult))
                c.done(v.tensor_tensor(mxm[:, a:b, :], mxm[:, a:b, :], one[:, 0, a:b][:, :, None].to_broadcast([P, b - a, HEADS]), ALU.add))
                c.done(v.tensor_tensor(top_[:, a:b, :], mxm[:, a:b, :], e0[:, a:b, :], ALU.max))
                c.inc(v.tensor_tensor(w1[:, a:b, :], mxm[:, a:b, :], top_[:, a:b, :], ALU.subtract))
                c.done(v.tensor_tensor(w0[:, a:b, :], e0[:, a:b, :], top_[:, a:b, :], ALU.subtract))
                v.sem_inc(s_go, 1)
                v.wait_ge(s_a, 4 * part + 2)
                c.done(v.tensor_tensor(w1[:, a:b, :], w1[:, a:b, :], has4, ALU.mult))
                c.inc(v.tensor_tensor(wide(num[:, a:b, :]), wide(ns[:, a:b, 0:HE]), heads4(w1[:, a:b, :]), ALU.mult))
                c.inc(v.tensor_tensor(wide(tmp[:, a:b, :]), wide(m.node_row[:, a:b, 0:HE]), heads4(w0[:, a:b, :]), ALU.mult))
                c.done(v.tensor_tensor(den[:, a:b, :], ns[:, a:b, HE:ROWF], w1[:, a:b, :], ALU.mult))
                c.inc(v.tensor_tensor(num[:, a:b, :], num[:, a:b, :], tmp[:, a:b, :], ALU.add))
                c.done(v.tensor_tensor(den[:, a:b, :], den[:, a:b, :], w0[:, a:b, :], ALU.add))
                c.done(v.tensor_scalar(den[:, a:b, :], den[:, a:b, :], 1e-16, None, ALU.add))
                c.done(v.reciprocal(den[:, a:b, :], den[:, a:b, :]))
                c.done(v.tensor_tensor(wide(num[:, a:b, :]), wide(num[:, a:b, :]), heads4(den[:, a:b, :]), ALU.mult))
                v.wait_ge(s_c, 48)
                c.done(v.tensor_tensor(num[:, a:b, :], num[:, a:b, :], row(0), ALU.add))
                c.done(v.tensor_reduce(one[:, 0, a:b], num[:, a:b, :], AX_X, ALU.add))
                c.done(v.tensor_scalar(one[:, 0, a:b], one[:, 0, a:b], 1.0 / HE, None, ALU.mult))
                c.done(v.tensor_tensor(num[:, a:b, :], num[:, a:b, :], per16(one[:, 0, a:b]), ALU.subtract))
                c.done(v.tensor_tensor(tmp[:, a:b, :], num[:, a:b, :], num[:, a:b, :], ALU.mult))
                c.done(v.tensor_reduce(one[:, 1, a:b], tmp[:, a:b, :], AX_X, ALU.add))
                c.done(v.tensor_scalar(one[:, 1, a:b], one[:, 1, a:b], 1.0 / HE, None, ALU.mult))
                v.sem_inc(s_go, 1)
                v.wait_ge(s_a, 4 * part + 3)
                c.done(v.reciprocal(one[:, 1, a:b], one[:, 1, a:b]))
                c.done(v.tensor_tensor(num[:, a:b, :], num[:, a:b, :], per16(one[:, 1, a:b]), ALU.mult))
                c.done(v.tensor_tensor(num[:, a:b, :], num[:, a:b, :], row(1), ALU.mult))
                c.done(v.tensor_tensor(num[:, a:b, :], num[:, a:b, :], row(2), ALU.add))
                c.done(v.tensor_reduce(sc[:, a:b, :], num[:, a:b, :].rearrange("p t (h x) -> p t x h", x=EXPERTS), AX_X, ALU.add))
                c.done(v.tensor_scalar(sc[:, a:b, :], sc[:, a:b, :], 1.0 / HEADS, None, ALU.mult))
                c.done(v.memset(rank[:, a:b, :], 0.0))
                for x in range(EXPERTS - 1):
                    n = EXPERTS - 1 - x
                    c.done(v.tensor_tensor(ge[:, a:b, 0:n], sc[:, a:b, x:x + 1].to_broadcast([P, b - a, n]), sc[:, a:b, x + 1:EXPERTS],
                                           ALU.is_ge))
                    c.inc(v.tensor_reduce(one[:, 2, a:b], ge[:, a:b, 0:n], AX_X, ALU.add))
                    c.done(v.tensor_tensor(rank[:, a:b, x + 1:EXPERTS], rank[:, a:b, x + 1:EXPERTS], ge[:, a:b, 0:n], ALU.add))
                    c.done(v.tensor_scalar(one[:, 2, a:b], one[:, 2, a:b], -1.0, float(n), ALU.mult, ALU.add))
                    c.done(v.tensor_tensor(rank[:, a:b, x], rank[:, a:b, x], one[:, 2, a:b], ALU.add))
                c.done(v.tensor_scalar(rank[:, a:b, :], rank[:, a:b, :], 1.5, None, ALU.is_lt))
                c.done(v.tensor_reduce(one[:, 3, a:b], sc[:, a:b, :], AX_X, ALU.max))
                c.done(v.tensor_tensor(ge[:, a:b, :], sc[:, a:b, :], one[:, 3, a:b][:, :, None].to_broadcast([P, b - a, EXPERTS]), ALU.subtract))
                v.sem_inc(s_go, 1)
                v.wait_ge(s_a, 4 * part + 4)
                c.done(v.tensor_tensor(ge[:, a:b, :], ge[:, a:b, :], rank[:, a:b, :], ALU.mult))
                c.done(v.tensor_reduce(one[:, 3, a:b], ge[:, a:b, :], AX_X, ALU.add))
                c.done(v.reciprocal(one[:, 3, a:b], one[:, 3, a:b]))
                c.done(v.tensor_tensor(sc[:, a:b, :], ge[:, a:b, :], one[:, 3, a:b][:, :, None].to_broadcast([P, b - a, EXPERTS]), ALU.mult))

            def pair(i, k, base):
                v.wait_ge(s_in[k], i * 32 + 32)
                for n in range(2 * EXPERTS):
                    e, t = n // 2, n % 2
                    if n >= 2:
                        v.wait_ge(s_v, (i * SLOTS + k) * LINKS + (base + n - 1))
                    q = v.scalar_tensor_tensor(xs[:, k, t, :], ys[:, k, t, e, :],
                                               sc[:, ds(i * (2 * SLOTS) + (2 * k + t), 1), e],
                                               xs[:, k, t, :], ALU.mult, ALU.add)
                    if n < LINKS:
                        q.then_inc(s_v, 1)
                q.then_inc(s_done, 1)

            LINKS = 2 * EXPERTS - 1
            for part in range(PARTS):
                gates(part)
                first = PART[part] // (2 * SLOTS)
                stop = PART[part + 1] // (2 * SLOTS)
                base = c.n
                c.n += (stop - first) * SLOTS * LINKS
                with v.Fori(first, stop) as i:
                    for k in range(SLOTS):
                        pair(i, k, base - first * SLOTS * LINKS)
            for k in range(REST):
                pair(ROUNDS, k, base - first * SLOTS * LINKS)


_INS = ["x", "src", "dst", "edge_weight", "L0_gnn_W", "L0_gnn_b", "L0_ffn_W_gat", "L0_ffn_att_src",
        "L0_ffn_att_dst", "L0_ffn_b_gat", "L0_ffn_ln_gamma", "L0_ffn_ln_beta", "L0_ffn_W1", "L0_ffn_b1",
        "L0_ffn_W2", "L0_ffn_b2", "L0_ffn_edge_index"]


def kernel(**inputs):
    import numpy as _np
    import concourse.bacc as _bacc
    from concourse import mybir as _mybir
    from concourse.bass_utils import run_bass_kernel_spmd as _run

    nc = _bacc.Bacc("TRN2", target_bir_lowering=False, num_devices=1)
    arrays, args = {}, []
    for name in _INS:
        a = _np.ascontiguousarray(inputs[name])
        arrays[f"in_{name}"] = a
        args.append(nc.dram_tensor(f"in_{name}", a.shape, _mybir.dt.from_np(a.dtype), kind="ExternalInput").ap())
    out = nc.dram_tensor("out_0", (NODES, FEAT), F32, kind="ExternalOutput").ap()
    build(nc, *args, out)
    r = _run(nc, [arrays], core_ids=[0])
    return r.results[0]["out_0"]
```
